# Optimizing a Trainium2 kernel written in Bass

```python
import numpy as np
import jax
import jax.numpy as jnp

def _softmax(x, axis=-1):
    return jax.nn.softmax(x, axis=axis)

def _gelu(x):
    return jax.nn.gelu(x, approximate=True)

def _silu(x):
    return jax.nn.silu(x)

def _sigmoid(x):
    return jax.nn.sigmoid(x)

def _layernorm(x, axis=-1, eps=1e-05):
    m = jnp.mean(x, axis=axis, keepdims=True)
    v = jnp.var(x, axis=axis, keepdims=True)
    return (x - m) / jnp.sqrt(v + eps)

def _scatter_add(tgt, idx, src, axis=0):
    return tgt.at[idx].add(src)

def _segment_sum(src, seg, n):
    return jax.ops.segment_sum(src, seg, n)
kernel_name = 'mk_vit_tower_postln_d1_tok_img512_r4_294afb'

def setup_inputs(seed: int=0):
    np.random.seed(seed)
    _w = jnp.asarray

    def _rec_inputs():
        import jax
        import jax.numpy as jnp
        _rk = jax.random.key(seed)
        x = 7.57192e-06 + 1.00007 * jax.random.normal(jax.random.fold_in(_rk, 1), (64, 3, 224, 224), jnp.float32)
        return x
    x = _rec_inputs()

    def _L0_tok_setup():
        import jax, jax.numpy as jnp
        import numpy as np
        D_MODEL = 128
        N_HEADS = 8
        D_HEAD = D_MODEL // N_HEADS
        D_FF = 344
        PATCH = 16
        IMG = 224
        N_PATCHES = (IMG // PATCH) ** 2
        T = N_PATCHES + 1
        B = 64
        EPS = 1e-06

        def rmsnorm(x, w):
            xf = x.astype(jnp.float32)
            norm = jax.lax.rsqrt(jnp.mean(xf * xf, axis=-1, keepdims=True) + EPS)
            return (xf * norm).astype(x.dtype) * w

        def _patch_embed(images, conv_w, conv_b, cls_token, pos_emb):
            y = jax.lax.conv_general_dilated(images, conv_w, window_strides=(PATCH, PATCH), padding='VALID', dimension_numbers=('NCHW', 'OIHW', 'NCHW'))
            y = y + conv_b[None, :, None, None]
            patches = y.reshape(y.shape[0], D_MODEL, -1).transpose(0, 2, 1)
            cls = jnp.broadcast_to(cls_token, (images.shape[0], 1, D_MODEL))
            return jnp.concatenate([cls, patches], axis=1) + pos_emb

        def _block(x, ln1w, wqkv, wo, ln2w, wg, wu, wd):
            Bx, Tx, C = x.shape
            h = rmsnorm(x, ln1w)
            qkv = (h @ wqkv.T).reshape(Bx, Tx, 3, N_HEADS, D_HEAD)
            q, k, v = jnp.moveaxis(qkv, 2, 0)
            scale = 1.0 / float(np.sqrt(D_HEAD))
            attn = jnp.einsum('bthd,bshd->bhts', q, k) * scale
            attn = jax.nn.softmax(attn, axis=-1)
            out = jnp.einsum('bhts,bshd->bthd', attn, v).reshape(Bx, Tx, C)
            x = x + out @ wo.T
            h2 = rmsnorm(x, ln2w)
            ff = jax.nn.silu(h2 @ wg.T) * (h2 @ wu.T) @ wd.T
            return x + ff
        key = jax.random.key(seed)
        ks = jax.random.split(key, 16)
        std = 0.02
        d = {'images': jax.random.normal(ks[0], (B, 3, IMG, IMG), dtype=jnp.float32), 'conv_w': jax.random.normal(ks[1], (D_MODEL, 3, PATCH, PATCH), dtype=jnp.float32) * std, 'conv_b': jnp.zeros((D_MODEL,), dtype=jnp.float32), 'cls_token': jax.random.normal(ks[2], (1, 1, D_MODEL), dtype=jnp.float32) * std, 'pos_emb': jax.random.normal(ks[3], (1, T, D_MODEL), dtype=jnp.float32) * std, 'ln_f': jnp.ones((D_MODEL,), dtype=jnp.float32)}
        ki = 4
        for i in range(2):
            d[f'ln1_{i}'] = jnp.ones((D_MODEL,), dtype=jnp.float32)
            d[f'qkv_{i}'] = jax.random.normal(ks[ki + 0], (3 * D_MODEL, D_MODEL), dtype=jnp.float32) * std
            d[f'wo_{i}'] = jax.random.normal(ks[ki + 1], (D_MODEL, D_MODEL), dtype=jnp.float32) * std
            d[f'ln2_{i}'] = jnp.ones((D_MODEL,), dtype=jnp.float32)
            d[f'gate_{i}'] = jax.random.normal(ks[ki + 2], (D_FF, D_MODEL), dtype=jnp.float32) * std
            d[f'up_{i}'] = jax.random.normal(ks[ki + 3], (D_FF, D_MODEL), dtype=jnp.float32) * std
            d[f'down_{i}'] = jax.random.normal(ks[ki + 4], (D_MODEL, D_FF), dtype=jnp.float32) * std
            ki += 5
        return d
    _L0_tok_all = _L0_tok_setup()
    _L0_tok_in = {k: v for k, v in _L0_tok_all.items() if k in ('conv_w', 'conv_b', 'cls_token', 'pos_emb', 'ln_f', 'ln1_0', 'qkv_0', 'wo_0', 'ln2_0', 'gate_0', 'up_0', 'down_0', 'ln1_1', 'qkv_1', 'wo_1', 'ln2_1', 'gate_1', 'up_1', 'down_1')}
    del _L0_tok_all

    def _L0_attn_setup():
        import jax, jax.numpy as jnp
        import numpy as np
        EPS = 1e-05

        def _layernorm(x):
            mu = x.mean(axis=-1, keepdims=True)
            var = x.var(axis=-1, keepdims=True)
            return (x - mu) / jnp.sqrt(var + EPS)
        key = jax.random.key(seed)
        k1, k2, k3, k4, k5 = jax.random.split(key, 5)
        B, T, E, H = (8, 512, 128, 8)
        d = E // H
        return {'input1': jax.random.normal(k1, (B, T, E), dtype=jnp.float32), 'Wq': jax.random.normal(k2, (H, d), dtype=jnp.float32) * 0.1, 'Wk': jax.random.normal(k3, (H, d), dtype=jnp.float32) * 0.1, 'Wv': jax.random.normal(k4, (H, d, d), dtype=jnp.float32) * 0.1, 'Wm': jax.random.normal(k5, (E, E), dtype=jnp.float32) * 0.05}
    _L0_attn_all = _L0_attn_setup()
    _L0_attn_in = {k: v for k, v in _L0_attn_all.items() if k in ('Wq', 'Wk', 'Wv', 'Wm')}
    del _L0_attn_all

    def _L0_ffn_setup():
        import jax, jax.numpy as jnp
        import numpy as np
        D = 128
        E = 8
        K = 2
        EXP = 4
        LN_EPS = 1e-05
        key = jax.random.key(seed)
        ks = jax.random.split(key, 8)
        B, T = (8, 512)
        Dh = D * EXP
        x = jax.random.normal(ks[0], (B, T, D), dtype=jnp.float32)
        ln_g = jnp.ones((D,), dtype=jnp.float32)
        ln_b = jnp.zeros((D,), dtype=jnp.float32)
        lim_r = np.sqrt(6.0 / (D + E)).astype(np.float32)
        w_r = jax.random.uniform(ks[1], (E, D), dtype=jnp.float32, minval=-lim_r, maxval=lim_r)
        b_r = jnp.zeros((E,), dtype=jnp.float32)
        lim1 = np.sqrt(6.0 / (D + Dh)).astype(np.float32)
        W1 = jax.random.uniform(ks[2], (E, D, Dh), dtype=jnp.float32, minval=-lim1, maxval=lim1)
        b1 = jnp.zeros((E, Dh), dtype=jnp.float32)
        W2 = jax.random.uniform(ks[3], (E, Dh, D), dtype=jnp.float32, minval=-lim1, maxval=lim1)
        b2 = jnp.zeros((E, D), dtype=jnp.float32)
        return {'x': x, 'ln_g': ln_g, 'ln_b': ln_b, 'w_r': w_r, 'b_r': b_r, 'W1': W1, 'b1': b1, 'W2': W2, 'b2': b2}
    _L0_ffn_all = _L0_ffn_setup()
    _L0_ffn_in = {k: v for k, v in _L0_ffn_all.items() if k in ('ln_g', 'ln_b', 'w_r', 'b_r', 'W1', 'b1', 'W2', 'b2')}
    del _L0_ffn_all
    return {'x': x, 'L0_tok_conv_w': _L0_tok_in['conv_w'], 'L0_tok_conv_b': _L0_tok_in['conv_b'], 'L0_tok_cls_token': _L0_tok_in['cls_token'], 'L0_tok_pos_emb': _L0_tok_in['pos_emb'], 'L0_tok_ln_f': _L0_tok_in['ln_f'], 'L0_tok_ln1_0': _L0_tok_in['ln1_0'], 'L0_tok_qkv_0': _L0_tok_in['qkv_0'], 'L0_tok_wo_0': _L0_tok_in['wo_0'], 'L0_tok_ln2_0': _L0_tok_in['ln2_0'], 'L0_tok_gate_0': _L0_tok_in['gate_0'], 'L0_tok_up_0': _L0_tok_in['up_0'], 'L0_tok_down_0': _L0_tok_in['down_0'], 'L0_tok_ln1_1': _L0_tok_in['ln1_1'], 'L0_tok_qkv_1': _L0_tok_in['qkv_1'], 'L0_tok_wo_1': _L0_tok_in['wo_1'], 'L0_tok_ln2_1': _L0_tok_in['ln2_1'], 'L0_tok_gate_1': _L0_tok_in['gate_1'], 'L0_tok_up_1': _L0_tok_in['up_1'], 'L0_tok_down_1': _L0_tok_in['down_1'], 'L0_attn_Wq': _L0_attn_in['Wq'], 'L0_attn_Wk': _L0_attn_in['Wk'], 'L0_attn_Wv': _L0_attn_in['Wv'], 'L0_attn_Wm': _L0_attn_in['Wm'], 'L0_ffn_ln_g': _L0_ffn_in['ln_g'], 'L0_ffn_ln_b': _L0_ffn_in['ln_b'], 'L0_ffn_w_r': _L0_ffn_in['w_r'], 'L0_ffn_b_r': _L0_ffn_in['b_r'], 'L0_ffn_W1': _L0_ffn_in['W1'], 'L0_ffn_b1': _L0_ffn_in['b1'], 'L0_ffn_W2': _L0_ffn_in['W2'], 'L0_ffn_b2': _L0_ffn_in['b2']}

def reference(x, L0_tok_conv_w, L0_tok_conv_b, L0_tok_cls_token, L0_tok_pos_emb, L0_tok_ln_f, L0_tok_ln1_0, L0_tok_qkv_0, L0_tok_wo_0, L0_tok_ln2_0, L0_tok_gate_0, L0_tok_up_0, L0_tok_down_0, L0_tok_ln1_1, L0_tok_qkv_1, L0_tok_wo_1, L0_tok_ln2_1, L0_tok_gate_1, L0_tok_up_1, L0_tok_down_1, L0_attn_Wq, L0_attn_Wk, L0_attn_Wv, L0_attn_Wm, L0_ffn_ln_g, L0_ffn_ln_b, L0_ffn_w_r, L0_ffn_b_r, L0_ffn_W1, L0_ffn_b1, L0_ffn_W2, L0_ffn_b2):
    import jax
    import jax.numpy as jnp

    def _L0_tok_ref(images, conv_w, conv_b, cls_token, pos_emb, ln_f, ln1_0, qkv_0, wo_0, ln2_0, gate_0, up_0, down_0, ln1_1, qkv_1, wo_1, ln2_1, gate_1, up_1, down_1):
        import jax, jax.numpy as jnp
        import numpy as np
        D_MODEL = 128
        N_HEADS = 8
        D_HEAD = D_MODEL // N_HEADS
        D_FF = 344
        PATCH = 16
        IMG = 224
        N_PATCHES = (IMG // PATCH) ** 2
        T = N_PATCHES + 1
        B = 64
        EPS = 1e-06

        def rmsnorm(x, w):
            xf = x.astype(jnp.float32)
            norm = jax.lax.rsqrt(jnp.mean(xf * xf, axis=-1, keepdims=True) + EPS)
            return (xf * norm).astype(x.dtype) * w

        def _patch_embed(images, conv_w, conv_b, cls_token, pos_emb):
            y = jax.lax.conv_general_dilated(images, conv_w, window_strides=(PATCH, PATCH), padding='VALID', dimension_numbers=('NCHW', 'OIHW', 'NCHW'))
            y = y + conv_b[None, :, None, None]
            patches = y.reshape(y.shape[0], D_MODEL, -1).transpose(0, 2, 1)
            cls = jnp.broadcast_to(cls_token, (images.shape[0], 1, D_MODEL))
            return jnp.concatenate([cls, patches], axis=1) + pos_emb

        def _block(x, ln1w, wqkv, wo, ln2w, wg, wu, wd):
            Bx, Tx, C = x.shape
            h = rmsnorm(x, ln1w)
            qkv = (h @ wqkv.T).reshape(Bx, Tx, 3, N_HEADS, D_HEAD)
            q, k, v = jnp.moveaxis(qkv, 2, 0)
            scale = 1.0 / float(np.sqrt(D_HEAD))
            attn = jnp.einsum('bthd,bshd->bhts', q, k) * scale
            attn = jax.nn.softmax(attn, axis=-1)
            out = jnp.einsum('bhts,bshd->bthd', attn, v).reshape(Bx, Tx, C)
            x = x + out @ wo.T
            h2 = rmsnorm(x, ln2w)
            ff = jax.nn.silu(h2 @ wg.T) * (h2 @ wu.T) @ wd.T
            return x + ff
        x = _patch_embed(images, conv_w, conv_b, cls_token, pos_emb)
        x = _block(x, ln1_0, qkv_0, wo_0, ln2_0, gate_0, up_0, down_0)
        x = _block(x, ln1_1, qkv_1, wo_1, ln2_1, gate_1, up_1, down_1)
        return rmsnorm(x, ln_f)

    def _L0_attn_ref(input1, Wq, Wk, Wv, Wm):
        import jax, jax.numpy as jnp
        import numpy as np
        EPS = 1e-05

        def _layernorm(x):
            mu = x.mean(axis=-1, keepdims=True)
            var = x.var(axis=-1, keepdims=True)
            return (x - mu) / jnp.sqrt(var + EPS)
        B, T, E = input1.shape
        H, d = Wq.shape
        xn = _layernorm(input1)
        xh = xn.reshape(B, T, H, d)
        Q = jnp.einsum('bthd,hd->bht', xh, Wq)
        K = jnp.einsum('bthd,hd->bht', xh, Wk)
        V = jnp.einsum('bthd,hde->bhte', xh, Wv)
        A = -(Q[:, :, :, None] - K[:, :, None, :]) ** 2
        P = jax.nn.softmax(A / d ** 0.5, axis=-1)
        O = jnp.einsum('bhts,bhse->bhte', P, V)
        head_result = O.transpose(0, 2, 1, 3).reshape(B, T, E)
        return head_result @ Wm + input1

    def _L0_ffn_ref(x, ln_g, ln_b, w_r, b_r, W1, b1, W2, b2):
        import jax, jax.numpy as jnp
        import numpy as np
        D = 128
        E = 8
        K = 2
        EXP = 4
        LN_EPS = 1e-05
        B, T, d = x.shape
        mu = jnp.mean(x, axis=-1, keepdims=True)
        var = jnp.mean(jnp.square(x - mu), axis=-1, keepdims=True)
        h = (x - mu) * jax.lax.rsqrt(var + LN_EPS) * ln_g + ln_b
        logits = jnp.einsum('btd,ed->bte', h, w_r) + b_r
        topk_vals, topk_idx = jax.lax.top_k(logits, K)
        gates = jax.nn.softmax(topk_vals, axis=-1)
        hf = h.reshape(B * T, d)
        hid = jax.nn.gelu(jnp.einsum('nd,edf->nef', hf, W1) + b1, approximate=False)
        expert_stack = jnp.einsum('nef,efd->ned', hid, W2) + b2
        idx_flat = topk_idx.reshape(B * T, K)
        gates_flat = gates.reshape(B * T, K)
        gathered = jnp.take_along_axis(expert_stack, idx_flat[:, :, None], axis=1)
        mixed = jnp.sum(gathered * gates_flat[:, :, None], axis=1).reshape(B, T, d)
        return x + mixed
    h = _L0_tok_ref(x, L0_tok_conv_w, L0_tok_conv_b, L0_tok_cls_token, L0_tok_pos_emb, L0_tok_ln_f, L0_tok_ln1_0, L0_tok_qkv_0, L0_tok_wo_0, L0_tok_ln2_0, L0_tok_gate_0, L0_tok_up_0, L0_tok_down_0, L0_tok_ln1_1, L0_tok_qkv_1, L0_tok_wo_1, L0_tok_ln2_1, L0_tok_gate_1, L0_tok_up_1, L0_tok_down_1)
    h = _layernorm(h + _L0_attn_ref(h, L0_attn_Wq, L0_attn_Wk, L0_attn_Wv, L0_attn_Wm), axis=-1)
    h = _layernorm(h + _L0_ffn_ref(h, L0_ffn_ln_g, L0_ffn_ln_b, L0_ffn_w_r, L0_ffn_b_r, L0_ffn_W1, L0_ffn_b1, L0_ffn_W2, L0_ffn_b2), axis=-1)
    return h

_drawn_inputs = setup_inputs


def setup_inputs(seed=0):
    import zlib

    import numpy as np

    out = dict(_drawn_inputs(seed))
    spreads = {'L0_tok_conv_b': (0.0, 0.1),
     'L0_tok_ln_f': (1.0, 0.2),
     'L0_tok_ln1_0': (1.0, 0.6),
     'L0_tok_ln2_0': (1.0, 0.6),
     'L0_tok_ln1_1': (1.0, 0.6),
     'L0_tok_ln2_1': (1.0, 0.6),
     'L0_ffn_ln_g': (1.0, 0.2),
     'L0_ffn_ln_b': (0.0, 0.1),
     'L0_ffn_b_r': (0.0, 0.1),
     'L0_ffn_b1': (0.0, 0.269),
     'L0_ffn_b2': (0.0, 0.1)}
    factors = {'L0_attn_Wq': 8.0, 'L0_attn_Wk': 8.0}
    for name, (base, spread) in spreads.items():
        noise = np.random.default_rng([zlib.crc32(name.encode()), seed]).standard_normal(out[name].shape)
        drawn = base * np.exp(spread * noise) if base else spread * noise
        out[name] = jnp.asarray(drawn.astype(out[name].dtype))
    for name, factor in factors.items():
        out[name] = (out[name] * factor).astype(out[name].dtype)
    return out
```

```python
from contextlib import ExitStack

import concourse.bass as bass
from concourse import mybir

F32 = mybir.dt.float32
F32R = mybir.dt.float32r
BF16 = mybir.dt.bfloat16
U32 = mybir.dt.uint32
ALU = mybir.AluOpType
ACT = mybir.ActivationFunctionType
AX = mybir.AxisListType

D = 128
HEADS = 8
HD = D // HEADS
T = 197
TP = 198
HT = TP // 2
RT = 100
PK = 6
FF = 345
FC = 3
FP = FF // FC
NORMS = 8
EXPERTS = 8
EH = 512
EC = EH // 128
BLK = 512
BC = BLK // 128
EPS_RMS = 1e-6
EPS_LN = 1e-5


def sizes(images):
    tokens = images * T
    blocks = (2 * tokens + EXPERTS * (BLK - 1)) // BLK
    blocks += blocks % 2
    region_blocks = (tokens + BLK - 1) // BLK
    region = region_blocks * BLK
    return blocks, region_blocks, region, EXPERTS * region + blocks * BLK


def pack_layout(images):
    blocks, region_blocks, _, _ = sizes(images)
    cols = [("conv", PK * D), ("pos", TP), ("cls", 1), ("conv_b", 1)]
    for l in range(2):
        cols += [(f"ln1_{l}", 1), (f"ln2_{l}", 1), (f"qk_{l}", 2 * D), (f"v_{l}", D), (f"wo_{l}", D),
                 (f"gate_{l}", FF), (f"up_{l}", FF), (f"down_{l}", FC * D)]
    cols += [("ln_f", 1), ("qk_2", 2 * HEADS), ("v_2", D), ("wo_2", D), ("ln_g", 1), ("ln_b", 1),
             ("wr", EXPERTS), ("br", EXPERTS), ("center", D), ("ident", D), ("mask", HEADS),
             ("lower", HT), ("iota", EXPERTS), ("first", EXPERTS), ("token", 4), ("inv", 1),
             ("fill", region_blocks), ("block", blocks)]
    at, out = 0, {}
    for name, n in cols:
        out[name] = (at, n)
        at += n
    return out, at


SEL_COLS = 4 * D + HEADS * D
EXPERT_COLS = EH + EC * D + EC + D

CHAINS = [
    ["patch", "sum0", "scale0", "qkv0", "sel0a", "sel0b", "sel0c"],
    ["turn0", "back0", "proj0", "sum1", "scale1", "glu0", "down0", "sum2", "scale2", "qkv1",
     "sel1a", "sel1b", "sel1c"],
    ["turn1", "back1", "proj1", "sum3", "scale3", "glu1", "down1", "sum4", "scale4", "center0",
     "sum5", "scale5", "qkv2", "stack", "masks"],
    ["turn2", "back2", "proj2", "center1", "sum6", "scale6", "center2", "sum7", "scale7", "route",
     "slots"],
]
LAG = 2
HEAD_STEPS = [f"head{i}" for i in range(HEADS + LAG)]


def merge(a, b):
    out = [((i + 0.5) / len(a), 0, x) for i, x in enumerate(a)]
    out += [((i + 0.5) / len(b), 1, x) for i, x in enumerate(b)]
    return [x for _, _, x in sorted(out, key=lambda y: y[:2])]


def plan_body():
    def of(s, steps, a=None):
        return [(s, x, a) for x in steps]

    order = of(0, CHAINS[0])
    for a in range(3):
        order += merge(of(0, HEAD_STEPS, a), of(1, CHAINS[a]))
        order += merge(of(1, HEAD_STEPS, a), of(0, CHAINS[a + 1]))
    return order + of(1, CHAINS[3])


def uses_of(step):
    kind = step.rstrip("0123456789abc")
    return {"qkv": ["qk", "v"], "sel": ["p0", "p1"], "glu": ["f0", "f1", "f2"],
            "route": ["rows", "logits"], "head": [], "masks": []}.get(kind, ["x"])


def plan_banks(order, banks):
    where, count, n = {}, [0] * banks, 0
    for s, step, _ in order:
        for use in uses_of(step):
            where[(s, step, use)] = (n % banks, count[n % banks])
            count[n % banks] += 1
            n += 1
    return where, count


NORM_SOURCE = ["patch", "proj0", "down0", "proj1", "down1", "center0", "center1", "center2"]
NORM_WEIGHT = {0: "ln1_0", 1: "ln2_0", 2: "ln1_1", 3: "ln2_1", 4: "ln_f", 7: "ln_g"}
CENTER_SOURCE = ["scale4", "proj2", "scale6"]
SCALE = float(HD) ** -0.5


def vit_moe_kernel(nc, img, pack, sel, experts, out):
    images = img.shape[0]
    turns = images // 2
    blocks, region_blocks, region, all_slots = sizes(images)
    tiles = 2 * images
    cols, pack_cols = pack_layout(images)
    order = plan_body()
    MB = 3
    where, uses = plan_banks(order, MB)

    token_rows = nc.dram_tensor("token_rows", [images * T, D], F32, kind="Internal").ap()
    slot_token = nc.dram_tensor("slot_token", [all_slots, 1], U32, kind="Internal").ap()
    slot_rows = nc.dram_tensor("slot_rows", [blocks * BLK, D], F32, kind="Internal").ap()

    with ExitStack() as ctx:
        def sb(name, shape, dt=F32):
            return ctx.enter_context(nc.sbuf_tensor(name, shape, dt))

        def pair(name, shape, dt=F32):
            return [sb(f"{name}{s}", shape, dt) for s in range(2)]

        def bank(name):
            return ctx.enter_context(nc.psum_tensor(name, [128, 512], F32))

        def sem(name):
            return ctx.enter_context(nc.semaphore(name))

        def sems(name, n=2):
            return [sem(f"{name}{s}") for s in range(n)]

        wp = sb("wp", [128, pack_cols])

        def w(name, rows=128):
            at, n = cols[name]
            return wp[0:rows, at:at + n]

        selr = sb("selr", [128, 2, SEL_COLS], F32R)
        identr = sb("identr", [RT, RT], F32R)
        lowb = sb("lowb", [HT, HT], BF16)
        onesb = sb("onesb", [HT, HT], BF16)
        minus_half = sb("minus_half", [HT, 2])
        ones1 = sb("ones1", [1, 128])

        imgs = pair("imgs", [128, PK, TP])
        xT = pair("xT", [128, TP])
        hT = pair("hT", [128, TP])
        sq = pair("sq", [128, TP])
        ms = pair("ms", [HT, 2])
        rn = pair("rn", [HT, 2])
        qk_hi = pair("qk_hi", [128, 2, TP], F32R)
        qk_lo = pair("qk_lo", [128, 2, TP], F32R)
        qs = pair("qs", [128, 4, TP], F32R)
        km = pair("km", [128, HEADS, TP], F32R)
        va = pair("va", [HT, 2, HEADS, 32])
        nm = pair("nm", [RT, 2, HEADS], F32R)
        ptw = pair("ptw", [128, HEADS * 2 * TP])
        pt = [x[0:HT, :].rearrange("p (h k t) -> p h k t", h=HEADS, k=2) for x in ptw]
        ot = pair("ot", [128, 2, TP])
        rc = pair("rc", [HT, 2 * HEADS])
        ao = pair("ao", [HT, 2 * HEADS, HD])
        aT = pair("aT", [128, TP])
        th = pair("th", [FP, FC, TP])
        gl = pair("gl", [FP, FC, TP])
        stq = pair("stq", [HT, 2, HEADS, HD], F32R)
        stk = pair("stk", [HT, 2, HEADS, HD], F32R)
        kf = pair("kf", [HT, 2, 2, HEADS])
        k3 = pair("k3", [128, TP])
        hmr = pair("hmr", [HT, 2, D])
        lg = pair("lg", [HT, 2, EXPERTS])
        top = pair("top", [HT, 2, 8])
        topi = pair("topi", [HT, 2, 8], U32)
        chosen = pair("chosen", [HT, 4])
        gd = pair("gd", [HT, 2])
        ge = pair("ge", [HT, 2])
        gs = pair("gs", [HT, 2])
        gr = pair("gr", [HT, 2])
        oneh = pair("oneh", [HT, 4, EXPERTS])
        onehb = pair("onehb", [HT, 4, EXPERTS], BF16)
        cnt3 = pair("cnt3", [HT, 3, EXPERTS])
        rank = pair("rank", [HT, 2, EXPERTS])
        cand = pair("cand", [HT, 4, EXPERTS])
        slotf = pair("slotf", [HT, 4])
        slotu = pair("slotu", [HT, 4], U32)
        tokf = pair("tokf", [HT, 2])
        toku = pair("toku", [HT, 2], U32)

        h1r = sb("h1r", [HT, tiles, D])
        gates = sb("gates", [HT, tiles, 2])
        slots = sb("slots", [HT, tiles, 2])
        nxt = sb("nxt", [HT, EXPERTS])
        zeros = sb("zeros", [128, all_slots // 128], U32)

        hid = [x[:, 0:EC * BLK].rearrange("p (f n) -> p f n", f=EC) for x in ptw]
        ex = [x[:, EC * BLK:(EC + 1) * BLK] for x in ptw]
        ey = [x[:, (EC + 1) * BLK:(EC + 2) * BLK].rearrange("p (c n) -> p c n", c=BC) for x in ptw]
        exr = [x[:, :, :].rearrange("p a b -> p (a b)")[:, 0:BC * D].rearrange("p (c n) -> p c n", c=BC)
               for x in imgs]
        ew = [wp[:, k * EXPERT_COLS:(k + 1) * EXPERT_COLS] for k in range(2)]
        assert 2 * EXPERT_COLS <= cols["ln_f"][0]
        ew1 = [x[:, 0:EH].rearrange("p (f n) -> p f n", f=EC) for x in ew]
        ew2 = [x[:, EH:EH + EC * D].rearrange("p (f n) -> p f n", f=EC) for x in ew]
        eb1 = [x[:, EH + EC * D:EH + EC * D + EC] for x in ew]
        eb2 = [x[0:1, EH + EC * D + EC:EXPERT_COLS] for x in ew]
        eidx = pair("eidx", [128, BC], U32)
        held = sb("held", [HT, EXPERTS])
        fills = sb("fills", [HT, EXPERTS, region_blocks])
        nblk = sb("nblk", [HT, EXPERTS])
        cum = sb("cum", [1, EXPERTS + 1])
        jump = sb("jump", [HT, EXPERTS])
        less = sb("less", [HT, 2 * tiles])
        moved = sb("moved", [HT, 2 * tiles])
        past = sb("past", [1, blocks, EXPERTS])
        jumped = sb("jumped", [1, blocks, EXPERTS])
        of_expert = sb("of_expert", [1, blocks])
        of_row = sb("of_row", [1, blocks])
        work = sb("work", [1, 2, blocks], U32)
        gidx = pair("gidx", [HT, 2], U32)
        gg = pair("gg", [HT, 2])
        gy = [x[0:HT, :, :].rearrange("p a b -> p (a b)")[:, 0:2 * D].rearrange("p (a n) -> p a n", a=2) for x in th]
        fin = [x[0:HT, :, :].rearrange("p a b -> p (a b)")[:, 2 * D:3 * D] for x in th]
        mix = [x[0:HT, :, :].rearrange("p a b -> p (a b)")[:, 0:3 * D].rearrange("p (a n) -> p a n", a=3) for x in gl]
        bn6 = pair("bn6", [HT, 6])
        bn2 = pair("bn2", [HT, 2])
        sd = pair("sd", [HT, 1])
        rs = pair("rs", [HT, 1])

        scores = [bank(f"scores{k}") for k in range(2)]
        scoresT = [bank(f"scoresT{k}") for k in range(2)]
        heads = bank("heads")
        misc = [bank(f"misc{k}") for k in range(MB)]

        def two(ps, rows=128, n=TP):
            return ps[0:rows, 0:2 * n].rearrange("p (a n) -> p a n", a=2)

        pack_loaded = sem("pack_loaded")
        sel_loaded = sem("sel_loaded")
        consts_ready = sem("consts_ready")
        credits = sem("credits")
        zeros_ready = sem("zeros_ready")
        table_cleared = sem("table_cleared")
        img_loaded = sems("img_loaded")
        full = sems("bank_full", MB)
        free = sems("bank_drained", MB)
        scores_full = sem("scores_full")
        max_done = sem("max_done")
        scoresT_full = sem("scoresT_full")
        exp_done = sem("exp_done")
        heads_full = sem("heads_full")
        heads_copied = sem("heads_copied")
        sq_ready = sems("sq_ready")
        rn_ready = sems("rn_ready")
        hi_ready = sems("hi_ready")
        th_ready = sems("th_ready")
        glu_half = sems("glu_half")
        recip_ready = sems("recip_ready")
        stack_step = sems("stack_step")
        masks_dve = sems("masks_dve")
        masks_act = sems("masks_act")
        hm_ready = sems("hm_ready")
        top_step = sems("top_step")
        gd_ready = sems("gd_ready")
        ge_ready = sems("ge_ready")
        gate_step = sems("gate_step")
        chosen_ready = sems("chosen_ready")
        slot_step = sems("slot_step")
        nxt_ready = sem("nxt_ready")
        tok_ready = sems("tok_ready")
        rows_stored = sems("rows_stored")
        slots_sent = sems("slots_sent")
        sends_done = sems("sends_done")
        stage1_done = sem("stage1_done")
        map_step = sem("map_step")
        idx_loaded = sems("idx_loaded")
        gathered = sems("gathered")
        w_loaded = sems("w_loaded")
        turned = sem("turned")
        tokens_ready = sem("tokens_ready")
        hid_full = sem("hid_full")
        act_done = sem("act_done")
        y_full = sem("y_full")
        y_ready = sem("y_ready")
        y_stored = sems("y_stored")
        idx_ready = sems("idx_ready")
        rows_got = sems("rows_got")
        mix_step = sems("mix_step")
        var_ready = sems("var_ready")
        sd_ready = sems("sd_ready")
        fin_ready = sems("fin_ready")
        out_stored = sems("out_stored")
        gather_free = sems("gather_free")

        passed = {eng.engine: sem(f"passed_{name}")
                  for name, eng in (("sp", nc.sync), ("pool", nc.gpsimd), ("dve", nc.vector))}

        def take(pe, it, key):
            b, n = where[key]
            pe.wait_ge(free[b], it * uses[b] + (n + 1))
            return misc[b]

        def filled(eng, it, key):
            b, n = where[key]
            eng.wait_ge(full[b], it * uses[b] + (n + 1))
            return misc[b]

        def drained(eng, it, key):
            b, n = where[key]
            eng.wait_ge(free[b], it * uses[b] + (n + 2))

        def wait_apart(eng, semaphore, value):
            eng.wait_ge(semaphore, value)
            eng.sem_inc(passed[eng.engine], 1)

        def full_of(key):
            return full[where[key][0]]

        def free_of(key):
            return free[where[key][0]]

        def norm_src(s, n):
            return hT[s] if n in (5, 7) else xT[s]

        def norm_dst(s, n):
            return xT[s] if n in (4, 6) else hT[s]

        def sel_tiles(part):
            if part == "a":
                return [("p0", qs, 0, 0), ("p1", qs, 2, 2)]
            first = 0 if part == "b" else 4
            return [("p0", km, first, 4 + first), ("p1", km, first + 2, 6 + first)]

        block = ctx.enter_context(nc.Block())

        @block.sync
        def _(sp):
            sp.dma_start(wp[:, :], pack).then_inc(pack_loaded, 16)
            sp.dma_start(ptw[0][:, 0:2 * SEL_COLS], sel).then_inc(sel_loaded, 16)
            for s in range(2):
                sp.dma_start(imgs[s][:, :, :], img[s]).then_inc(img_loaded[s], 16)
            sp.wait_ge(zeros_ready, 1)
            sp.dma_start(slot_token.rearrange("(p n) o -> p (n o)", p=128), zeros[:, :]).then_inc(table_cleared, 16)
            if turns > 1:
                with sp.Fori(0, turns - 1) as it:
                    for s in range(2):
                        b, n = where[(s, "patch", "x")]
                        nth = sp.snap(it * uses[b] + (n + 1))
                        nxt_img = sp.snap(it * 2 + (s + 2))
                        wait_apart(sp, full[b], nth)
                        sp.dma_start(imgs[s][:, :, :], img[bass.ds(nxt_img, 1)].rearrange("a p k t -> (a p) k t")
                                     ).then_inc(img_loaded[s], 16)

            sp.wait_ge(map_step, MAP_STEPS)
            sp.wait_ge(stage1_done, 4)
            with sp.Fori(0, blocks // 2) as it:
                for k in range(2):
                    e = sp.value_load(work[0:1, 0, bass.ds(it * 2 + k, 1)], min_val=0, max_val=EXPERTS - 1)
                    row = sp.value_load(work[0:1, 1, bass.ds(it * 2 + k, 1)], min_val=0,
                                        max_val=all_slots - BLK)
                    nth = sp.snap(it * 2 + (k + 1))
                    wait_apart(sp, turned, nth)
                    sp.dma_start(eidx[k][:, :], slot_token[bass.ds(row, BLK), :].rearrange("(p c) o -> p (c o)", p=128)
                                 ).then_inc(idx_loaded[k], 16)
                    wait_apart(sp, y_full, nth)
                    sp.dma_start(ew[k], experts[bass.ds(e, 1)].rearrange("a p n -> (a p) n")).then_inc(w_loaded[k], 16)

            with sp.Fori(0, images) as it:
                for k in range(2):
                    rows = T - HT if k else HT
                    nth = sp.snap(it + 1)
                    first = sp.snap(it * T + k * HT)
                    wait_apart(sp, fin_ready[k], nth)
                    sp.dma_start(out[bass.ds(first, rows), :], fin[k][0:rows, :]).then_inc(out_stored[k], 16)
            for k in range(2):
                sp.wait_ge(out_stored[k], 16 * images + 16)

        @block.gpsimd
        def _(pool):
            pool.memset(zeros[:, :], 0).then_inc(zeros_ready, 1)
            pool.wait_ge(table_cleared, 16)
            pool.wait_ge(credits, 1)

            def inverse_root(s, n, it):
                drained(pool, it, (s, f"sum{n}", "x"))
                pool.tensor_tensor(rn[s][:, :], ms[s][:, :], minus_half[:, :], ALU.pow).then_inc(rn_ready[s], 1)

            def send(s, it):
                wait_apart(pool, slot_step[s], it * SLOT_STEPS + SLOT_STEPS)
                for k in range(2):
                    rows = T - HT if k else HT
                    for c in range(2):
                        pool.indirect_dma_start(
                            out=slot_token, out_offset=bass.IndirectOffsetOnAxis(ap=slotu[s][0:rows, 2 * k + c:2 * k + c + 1], axis=0),
                            in_=toku[s][0:rows, k:k + 1], in_offset=None).then_inc(slots_sent[s], 16)
                drained(pool, it, (s, "route", "rows"))
                for k in range(2):
                    rows = T - HT if k else HT
                    pool.dma_start(token_rows[bass.ds((it * 2 + s) * T + k * HT, rows), :], hmr[s][0:rows, k, :]
                                   ).then_inc(rows_stored[s], 16)

            def sent(s, it):
                pool.wait_ge(slots_sent[s], it * 64 + 64)
                pool.wait_ge(rows_stored[s], it * 32 + 32)
                pool.sem_inc(sends_done[s], 1)

            with pool.Fori(0, turns) as it:
                for s, step, a in order:
                    if step.startswith("sum"):
                        inverse_root(s, int(step[3:]), it)
                    if step == "slots":
                        send(s, it)
                    if (s, step) == (1, "scale7"):
                        sent(0, it)
                sent(1, it)
            pool.drain().then_inc(stage1_done, 1)

            with pool.Fori(0, blocks // 2) as it:
                for k in range(2):
                    pool.wait_ge(idx_loaded[k], it * 16 + 16)
                    wait_apart(pool, turned, it * 2 + (k + 1))
                    for c in range(BC):
                        pool.indirect_dma_start(
                            out=exr[k][:, c, :], out_offset=None, in_=token_rows,
                            in_offset=bass.IndirectOffsetOnAxis(ap=eidx[k][:, c:c + 1], axis=0)).then_inc(gathered[k], 16)

            for k in range(2):
                pool.wait_ge(y_stored[k], 16 * (blocks // 2) + 16)
            with pool.Fori(0, images) as it:
                for k in range(2):
                    rows = T - HT if k else HT
                    pool.wait_ge(idx_ready[k], it * 2 + 2)
                    wait_apart(pool, gather_free[k], it + 1)
                    for c in range(2):
                        pool.indirect_dma_start(
                            out=gy[k][0:rows, c, :], out_offset=None, in_=slot_rows,
                            in_offset=bass.IndirectOffsetOnAxis(ap=gidx[k][0:rows, c:c + 1], axis=0)).then_inc(rows_got[k], 16)

        @block.scalar
        def _(act):
            act.sem_inc(exp_done, 2)
            act.sem_inc(heads_copied, 1)
            act.wait_ge(pack_loaded, 16)
            act.wait_ge(credits, 1)

            def square(s, n, it):
                drained(act, it, (s, NORM_SOURCE[n], "x"))
                act.activation(sq[s][:, :], norm_src(s, n)[:, :], ACT.Square).then_inc(sq_ready[s], 1)

            def qk_high(s, l, it):
                ps = filled(act, it, (s, f"qkv{l}", "qk"))
                act.activation(qk_hi[s][:, :, :], two(ps), ACT.Copy).then_inc(hi_ready[s], 1)

            def values(s, l, it):
                ps = filled(act, it, (s, f"qkv{l}", "v"))
                act.activation(va[s][:, :, :, 0:HD].rearrange("p k h d -> p (k h) d"),
                               ps[0:HT, 0:2 * D].rearrange("p (k d) -> p k d", d=HD), ACT.Copy
                               ).then_inc(free_of((s, f"qkv{l}", "v")), 1)

            def stacks(s, step, it):
                use, dst, tile, _ = sel_tiles(step[-1])[1]
                ps = filled(act, it, (s, step, use))
                act.activation(dst[s][:, tile:tile + 2, :], two(ps), ACT.Copy).then_inc(free_of((s, step, use)), 1)

            def exp(s, a, h, it):
                g = 8 * (2 * a + s) + h
                act.wait_ge(scoresT_full, it * 48 + (g + 1))
                act.activation(pt[s][:, h, :, :], two(scoresT[g % 2], HT), ACT.Exp, scale=SCALE).then_inc(exp_done, 1)

            def heads_copy(s, a, it):
                act.wait_ge(heads_full, it * 6 + (2 * a + s + 1))
                act.activation(ot[s][:, :, :], two(heads), ACT.Copy).then_inc(heads_copied, 1)

            def back(s, a, it):
                key = (s, f"back{a}", "x")
                ps = filled(act, it, key)
                act.activation(aT[s][:, :], ps[:, 0:TP], ACT.Copy).then_inc(free_of(key), 1)

            def tanh(s, l, it):
                for f in range(FC):
                    ps = filled(act, it, (s, f"glu{l}", f"f{f}"))
                    act.activation(th[s][:, f, :], ps[0:FP, 0:TP], ACT.Tanh, scale=0.5).then_inc(th_ready[s], 1)

            def stack_copy(s, it):
                key = (s, "stack", "x")
                ps = filled(act, it, key)
                act.activation(qs[s][:, 0, :], ps[:, 0:TP], ACT.Copy)
                act.activation(k3[s][:, :], ps[:, TP:2 * TP], ACT.Copy).then_inc(free_of(key), 1)

            def masks(s, it):
                drained(act, it, (s, "stack", "x"))
                for h in range(4, HEADS):
                    i = act.activation(km[s][:, h, :], k3[s][:, :], ACT.Copy, scale=w("mask")[:, h:h + 1])
                i.then_inc(masks_act[s], 1)

            def rows(s, it):
                key = (s, "route", "rows")
                ps = filled(act, it, key)
                r = ps[0:HT, 0:4 * D].rearrange("p (a k d) -> p a k d", a=2, k=2)
                act.activation(h1r[:, bass.ds((it * 2 + s) * 2, 2), :], r[:, 0, :, :], ACT.Copy)
                act.wait_ge(sends_done[s], it + 1)
                act.activation(hmr[s][:, :, :], r[:, 1, :, :], ACT.Copy).then_inc(free_of(key), 1)

            with act.Fori(0, turns) as it:
                for s, step, a in order:
                    n = int("0" + "".join(c for c in step if c.isdigit()))
                    if step.startswith("sum"):
                        square(s, n, it)
                    elif step.startswith("qkv"):
                        if n < 2:
                            qk_high(s, n, it)
                        values(s, n, it)
                    elif step.startswith("sel"):
                        stacks(s, step, it)
                    elif step.startswith("head"):
                        if n >= LAG:
                            exp(s, a, n - LAG, it)
                    elif step.startswith("turn"):
                        heads_copy(s, n, it)
                    elif step.startswith("back"):
                        back(s, n, it)
                    elif step.startswith("glu"):
                        tanh(s, n, it)
                    elif step == "stack":
                        stack_copy(s, it)
                    elif step == "masks":
                        masks(s, it)
                    elif step == "route":
                        rows(s, it)
                        act.wait_ge(gd_ready[s], it + 1)
                        act.activation(ge[s][:, :], gd[s][:, :], ACT.Exp).then_inc(ge_ready[s], 1)

            act.drain().then_inc(stage1_done, 1)
            act.sem_inc(act_done, 2)
            act.sem_inc(y_stored[0], 16)
            act.sem_inc(y_stored[1], 16)
            act.wait_ge(map_step, MAP_STEPS)
            with act.Fori(0, blocks // 2) as it:
                for k in range(2):
                    for f in range(EC):
                        n = k * EC + f
                        act.wait_ge(hid_full, it * 2 * EC + (n + 1))
                        act.activation(hid[k][:, f, :], scoresT[n % 2][:, :], ACT.Gelu, bias=eb1[k][:, f:f + 1]
                                       ).then_inc(act_done, 1)
                for k in range(2):
                    act.wait_ge(y_ready, it * 2 + (k + 3))
                    act.dma_start(slot_rows[bass.ds((it * 2 + k) * BLK, BLK), :].rearrange("(p c) n -> p c n", p=128), ey[k]
                                  ).then_inc(y_stored[k], 16)

            with act.Fori(0, images) as it:
                for k in range(2):
                    act.wait_ge(gather_free[k], it + 1)
                    act.activation(gidx[k][:, :], moved[:, bass.ds((it * 2 + k) * 2, 2)], ACT.Copy).then_inc(idx_ready[k], 1)
                    act.activation(gg[k][:, :], gates[:, bass.ds(it * 2 + k, 1), :].rearrange("p a c -> p (a c)"), ACT.Copy).then_inc(idx_ready[k], 1)
                for k in range(2):
                    act.wait_ge(var_ready[k], it + 1)
                    rows = T - HT if k else HT
                    act.activation(sd[k][0:rows, :], bn2[k][0:rows, 1:2], ACT.Sqrt).then_inc(sd_ready[k], 1)

        @block.tensor
        def _(pe):
            pe.sem_inc(turned, 2)
            pe.sem_inc(y_full, 2)
            pe.wait_ge(pack_loaded, 16)
            pe.wait_ge(consts_ready, 1)
            ident = w("ident")

            def patch(s, it):
                key = (s, "patch", "x")
                pe.wait_ge(img_loaded[s], it * 16 + 16)
                ps = take(pe, it, key)
                conv = w("conv").rearrange("p (k o) -> p k o", k=PK)
                for k in range(PK):
                    mm = pe.matmul(ps[:, 0:TP], conv[:, k, :], imgs[s][:, k, :], start=(k == 0), stop=(k == PK - 1))
                mm.then_inc(full_of(key), 1)

            def sums(s, n, it):
                key = (s, f"sum{n}", "x")
                pe.wait_ge(sq_ready[s], it * NORMS + (n + 1))
                ps = take(pe, it, key)
                for k in range(2):
                    mm = pe.matmul(ps[0:HT, k:k + 1], sq[s][:, k * HT:(k + 1) * HT], w("inv"), start=True, stop=True)
                mm.then_inc(full_of(key), 1)

            def scales(s, n, it):
                key = (s, f"scale{n}", "x")
                pe.wait_ge(rn_ready[s], it * NORMS + (n + 1))
                ps = take(pe, it, key)
                for k in range(2):
                    mm = pe.matmul(ps[:, k * HT:(k + 1) * HT], rn[s][:, k:k + 1].to_broadcast([HT, 128]),
                                   ident[0:HT, 0:HT], start=True, stop=True)
                mm.then_inc(full_of(key), 1)

            def center(s, n, it):
                key = (s, f"center{n}", "x")
                drained(pe, it, (s, CENTER_SOURCE[n], "x"))
                ps = take(pe, it, key)
                pe.matmul(ps[:, 0:TP], w("center"), xT[s][:, :], start=True, stop=True).then_inc(full_of(key), 1)

            def qkv(s, l, it):
                drained(pe, it, (s, ["scale0", "scale2", "scale5"][l], "x"))
                ps = take(pe, it, (s, f"qkv{l}", "qk"))
                for k in range(2):
                    if l < 2:
                        mm = pe.matmul(ps[:, k * TP:(k + 1) * TP], w(f"qk_{l}")[:, k * D:(k + 1) * D], hT[s][:, :],
                                       start=True, stop=True)
                    else:
                        mm = pe.matmul(ps[0:HT, k * 2 * HEADS:(k + 1) * 2 * HEADS], hT[s][:, k * HT:(k + 1) * HT],
                                       w("qk_2"), start=True, stop=True)
                mm.then_inc(full_of((s, f"qkv{l}", "qk")), 1)
                ps = take(pe, it, (s, f"qkv{l}", "v"))
                for k in range(2):
                    mm = pe.matmul(ps[0:HT, k * D:(k + 1) * D], hT[s][:, k * HT:(k + 1) * HT], w(f"v_{l}"),
                                   start=True, stop=True)
                mm.then_inc(full_of((s, f"qkv{l}", "v")), 1)

            def select(s, step, it):
                l, which = int(step[3]), 0 if step[-1] == "a" else 1
                drained(pe, it, (s, f"qkv{l}", "qk"))
                for use, _, _, at in sel_tiles(step[-1]):
                    ps = take(pe, it, (s, step, use))
                    for j in range(2):
                        for part, src in enumerate((qk_hi, qk_lo)):
                            mm = pe.matmul(ps[:, j * TP:(j + 1) * TP], selr[:, part, (at + j) * D:(at + j + 1) * D],
                                           src[s][:, which, :], start=(part == 0), stop=(part == 1))
                    mm.then_inc(full_of((s, step, use)), 1)

            def head_scores(s, a, h, it):
                g = 8 * (2 * a + s) + h
                if a < 2:
                    if h == 0:
                        drained(pe, it, (s, f"sel{a}a", "p0"))
                        drained(pe, it, (s, f"sel{a}a", "p1"))
                    if h in (0, 4):
                        drained(pe, it, (s, f"sel{a}" + "bc"[h // 4], "p0"))
                        drained(pe, it, (s, f"sel{a}" + "bc"[h // 4], "p1"))
                elif h == 0:
                    pe.wait_ge(masks_dve[s], it + 1)
                    pe.wait_ge(masks_act[s], it + 1)
                pe.wait_ge(max_done, it * 48 + (g + 1))
                q = qs[s][:, h // 2 if a < 2 else 0, :]
                for k in range(2):
                    mm = pe.matmul(scores[g % 2][0:RT, k * TP:(k + 1) * TP], q[:, k * (TP - RT):k * (TP - RT) + RT],
                                   km[s][:, h, :], start=True, stop=True)
                mm.then_inc(scores_full, 1)

            def head_scoresT(s, a, h, it):
                g = 8 * (2 * a + s) + h
                pe.wait_ge(max_done, it * 48 + (g + 3))
                pe.wait_ge(exp_done, it * 48 + (g + 1))
                q = qs[s][:, h // 2 if a < 2 else 0, :]
                ps = scoresT[g % 2]
                for k in range(2):
                    for j in range(2):
                        skip = j * (2 * RT - TP)
                        first = k * TP + j * RT
                        pe.matmul(ps[0:HT, first:first + RT - skip], nm[s][:, j, h:h + 1].to_broadcast([RT, HT]),
                                  identr[:, skip:RT], start=(j == 0), stop=False, skip_group_check=True)
                    mm = pe.matmul(ps[0:HT, k * TP:(k + 1) * TP], km[s][:, h, k * HT:(k + 1) * HT], q,
                                   start=False, stop=True, skip_group_check=True)
                mm.then_inc(scoresT_full, 1)

            def head_values(s, a, g, it):
                n = 2 * a + s
                if g == 0:
                    drained(pe, it, (s, f"qkv{a}", "v"))
                    pe.wait_ge(heads_copied, it * 6 + (n + 1))
                pe.wait_ge(exp_done, it * 48 + (8 * n + 4 * g + 3 + 3))
                for k in range(2):
                    rows = T - HT if k else HT
                    for j in range(4):
                        mm = pe.matmul(heads[32 * j:32 * j + 32, g * TP:(g + 1) * TP], va[s][0:rows, k, 4 * g + j, :],
                                       pt[s][0:rows, 4 * g + j, k, :], start=(k == 0), stop=(k == 1),
                                       skip_group_check=True)
                if g == 1:
                    mm.then_inc(heads_full, 1)

            def turn(s, a, it):
                key = (s, f"turn{a}", "x")
                pe.wait_ge(heads_copied, it * 6 + (2 * a + s + 2))
                ps = take(pe, it, key)
                for k in range(2):
                    for g in range(2):
                        mm = pe.transpose(ps[0:HT, (2 * k + g) * D:(2 * k + g + 1) * D],
                                          ot[s][:, g, k * HT:(k + 1) * HT], ident)
                mm.then_inc(full_of(key), 1)

            def back(s, a, it):
                key = (s, f"back{a}", "x")
                drained(pe, it, (s, f"turn{a}", "x"))
                ps = take(pe, it, key)
                for k in range(2):
                    mm = pe.transpose(ps[:, k * HT:(k + 1) * HT],
                                      ao[s][:, 8 * k:8 * k + 8, :].rearrange("p h d -> p (h d)"), ident[0:HT, 0:HT])
                mm.then_inc(full_of(key), 1)

            def proj(s, a, it):
                key = (s, f"proj{a}", "x")
                drained(pe, it, (s, f"back{a}", "x"))
                ps = take(pe, it, key)
                pe.matmul(ps[:, 0:TP], w(f"wo_{a}"), aT[s][:, :], start=True, stop=True).then_inc(full_of(key), 1)

            def glu(s, l, it):
                drained(pe, it, (s, f"scale{2 * l + 1}", "x"))
                for f in range(FC):
                    key = (s, f"glu{l}", f"f{f}")
                    ps = take(pe, it, key)
                    for k, name in enumerate(("gate", "up")):
                        mm = pe.matmul(ps[0:FP, k * TP:(k + 1) * TP], w(f"{name}_{l}")[:, f * FP:(f + 1) * FP],
                                       hT[s][:, :], start=True, stop=True)
                    mm.then_inc(full_of(key), 1)

            def down(s, l, it):
                key = (s, f"down{l}", "x")
                ps = take(pe, it, key)
                wd = w(f"down_{l}").rearrange("p (f o) -> p f o", f=FC)
                for f in range(FC):
                    drained(pe, it, (s, f"glu{l}", f"f{f}"))
                    mm = pe.matmul(ps[:, 0:TP], wd[0:FP, f, :], gl[s][:, f, :], start=(f == 0), stop=(f == FC - 1))
                mm.then_inc(full_of(key), 1)

            def stack(s, it):
                key = (s, "stack", "x")
                pe.wait_ge(stack_step[s], it * 8 + 8)
                ps = take(pe, it, key)
                for j, src in enumerate((stq, stk)):
                    for k in range(2):
                        mm = pe.transpose(ps[:, j * TP + k * HT:j * TP + (k + 1) * HT],
                                          src[s][:, k, :, :].rearrange("p h d -> p (h d)").bitcast(F32),
                                          ident[0:HT, 0:HT])
                mm.then_inc(full_of(key), 1)

            def route(s, it):
                drained(pe, it, (s, "scale6", "x"))
                pe.wait_ge(hm_ready[s], it + 1)
                key = (s, "route", "rows")
                ps = take(pe, it, key)
                for j, src in enumerate((xT, hT)):
                    for k in range(2):
                        mm = pe.transpose(ps[0:HT, (2 * j + k) * D:(2 * j + k + 1) * D], src[s][:, k * HT:(k + 1) * HT], ident)
                mm.then_inc(full_of(key), 1)
                key = (s, "route", "logits")
                ps = take(pe, it, key)
                for k in range(2):
                    mm = pe.matmul(ps[0:HT, k * EXPERTS:(k + 1) * EXPERTS], hT[s][:, k * HT:(k + 1) * HT], w("wr"),
                                   start=True, stop=True)
                mm.then_inc(full_of(key), 1)

            def ranks(s, it):
                key = (s, "slots", "x")
                pe.wait_ge(chosen_ready[s], it + 1)
                ps = take(pe, it, key)
                last = T - HT
                groups = [[(lowb, HT, 0)], [(lowb, last, 1), (onesb, HT, 0)], [(onesb, HT, 0), (onesb, last, 1)]]
                for j, group in enumerate(groups):
                    terms = [(m, rows, k, c) for m, rows, k in group for c in range(2)]
                    for i, (m, rows, k, c) in enumerate(terms):
                        mm = pe.matmul(ps[0:HT, j * EXPERTS:(j + 1) * EXPERTS], m[0:rows, :], onehb[s][0:rows, 2 * k + c, :],
                                       start=(i == 0), stop=(i == len(terms) - 1))
                mm.then_inc(full_of(key), 1)

            with pe.Fori(0, turns) as it:
                for s, step, a in order:
                    n = int("0" + "".join(c for c in step if c.isdigit()))
                    if step == "patch":
                        patch(s, it)
                    elif step.startswith("sum"):
                        sums(s, n, it)
                    elif step.startswith("scale"):
                        scales(s, n, it)
                    elif step.startswith("center"):
                        center(s, n, it)
                    elif step.startswith("qkv"):
                        qkv(s, n, it)
                    elif step.startswith("sel"):
                        select(s, step, it)
                    elif step.startswith("head"):
                        if n >= LAG:
                            head_scoresT(s, a, n - LAG, it)
                        if n < HEADS:
                            head_scores(s, a, n, it)
                        if n in (6, 9):
                            head_values(s, a, n // 7, it)
                    elif step.startswith("turn"):
                        turn(s, n, it)
                    elif step.startswith("back"):
                        back(s, n, it)
                    elif step.startswith("proj"):
                        proj(s, n, it)
                    elif step.startswith("glu"):
                        glu(s, n, it)
                    elif step.startswith("down"):
                        down(s, n, it)
                    elif step == "stack":
                        stack(s, it)
                    elif step == "route":
                        route(s, it)
                    elif step == "slots":
                        ranks(s, it)

            pe.drain().then_inc(stage1_done, 1)
            pe.wait_ge(stage1_done, 4)
            turn_bank, hid_bank, y_bank = scores, scoresT, [heads, misc[0]]
            with pe.Fori(0, blocks // 2) as it:
                for k in range(2):
                    pe.wait_ge(gathered[k], it * 16 * BC + 16 * BC)
                    for c in range(BC):
                        mm = pe.transpose(turn_bank[k][:, c * D:(c + 1) * D], exr[k][:, c, :], ident)
                    mm.then_inc(turned, 1)
                for k in range(2):
                    pe.wait_ge(w_loaded[k], it * 16 + 16)
                    pe.wait_ge(tokens_ready, it * 2 + (k + 1))
                    for f in range(EC):
                        n = k * EC + f
                        pe.wait_ge(act_done, it * 2 * EC + (n + 1))
                        pe.matmul(hid_bank[n % 2][:, :], ew1[k][:, f, :], ex[k], start=True, stop=True
                                  ).then_inc(hid_full, 1)
                for k in range(2):
                    pe.wait_ge(y_ready, it * 2 + (k + 1))
                    for c in range(BC):
                        for f in range(EC):
                            if c == 0:
                                pe.wait_ge(act_done, it * 2 * EC + (k * EC + f + 3))
                            pe.matmul(y_bank[k][:, c * D:(c + 1) * D], hid[k][:, f, c * D:(c + 1) * D], ew2[k][:, f, :],
                                      start=(f == 0), stop=False)
                        mm = pe.matmul(y_bank[k][:, c * D:(c + 1) * D], ones1[:, :], eb2[k], start=False, stop=True)
                    mm.then_inc(y_full, 1)

        @block.vector
        def _(dve):
            dve.memset(minus_half[:, :], -0.5)
            dve.memset(ones1[:, :], 1.0)
            dve.memset(onesb[:, :], 1.0)
            for s in range(2):
                dve.memset(va[s][:, :, :, :], 0.0)
                dve.memset(stq[s][:, :, :, :].bitcast(F32), 0.0)
                dve.memset(stk[s][:, :, :, :].bitcast(F32), 0.0)
            dve.drain()
            for s in range(2):
                dve.memset(va[s][:, :, :, HD:HD + 1], 1.0)
                dve.memset(stq[s][:, :, :, 4:6].bitcast(F32), 1.0)
            dve.wait_ge(pack_loaded, 16)
            dve.tensor_copy(lowb[:, :], w("lower", HT))
            dve.tensor_copy(nxt[:, :], w("first", HT))
            dve.tensor_copy(identr[:, :], w("ident", RT)[:, 0:RT])
            for s in range(2):
                dve.tensor_copy(tokf[s][:, :], w("token", HT)[:, 2 * s:2 * s + 2])
            pos = w("pos")
            dve.tensor_scalar(pos[:, 1:TP], pos[:, 1:TP], w("conv_b"), None, ALU.add)
            dve.tensor_tensor(pos[:, 0:1], pos[:, 0:1], w("cls"), ALU.add)
            for l in range(2):
                dve.tensor_scalar(w(f"down_{l}"), w(f"down_{l}"), 0.5, None, ALU.mult)
            dve.wait_ge(sel_loaded, 16)
            dve.tensor_copy(selr[:, :, :].rearrange("p a n -> p (a n)"), ptw[0][:, 0:2 * SEL_COLS])
            dve.drain().then_inc(consts_ready, 1)
            for b in range(MB):
                dve.sem_inc(free[b], 1)
            dve.sem_inc(max_done, 2)
            dve.sem_inc(nxt_ready, 1)
            for s in range(2):
                dve.sem_inc(tok_ready[s], 1)
                dve.sem_inc(sends_done[s], 1)
                dve.sem_inc(gather_free[s], 1)
                dve.sem_inc(out_stored[s], 16)
            dve.sem_inc(y_ready, 2)
            dve.sem_inc(credits, 1)

            def embed(s, it):
                key = (s, "patch", "x")
                ps = filled(dve, it, key)
                dve.tensor_tensor(xT[s][:, :], ps[:, 0:TP], w("pos"), ALU.add).then_inc(free_of(key), 1)

            def mean_square(s, n, it):
                key = (s, f"sum{n}", "x")
                ps = filled(dve, it, key)
                dve.tensor_scalar(ms[s][:, :], ps[0:HT, 0:2], EPS_LN if n >= 5 else EPS_RMS, None, ALU.add
                                  ).then_inc(free_of(key), 1)

            def normed(s, n, it):
                key = (s, f"scale{n}", "x")
                ps = filled(dve, it, key)
                src, dst = norm_src(s, n)[:, :], norm_dst(s, n)[:, :]
                if n in NORM_WEIGHT:
                    i = dve.scalar_tensor_tensor(out=dst, in0=src, scalar=w(NORM_WEIGHT[n]), in1=ps[:, 0:TP],
                                                 op0=ALU.mult, op1=ALU.mult)
                else:
                    i = dve.tensor_tensor(dst, src, ps[:, 0:TP], ALU.mult)
                i.then_inc(free_of(key), 1)
                if n == 7:
                    drained(dve, it, key)
                    dve.tensor_scalar(dst, dst, w("ln_b"), None, ALU.add).then_inc(hm_ready[s], 1)

            def centered(s, n, it):
                key = (s, f"center{n}", "x")
                ps = filled(dve, it, key)
                dve.tensor_copy((xT if n == 1 else hT)[s][:, :], ps[:, 0:TP]).then_inc(free_of(key), 1)

            def qk_low(s, l, it):
                key = (s, f"qkv{l}", "qk")
                ps = filled(dve, it, key)
                dve.wait_ge(hi_ready[s], it * 2 + (l + 1))
                dve.tensor_tensor(qk_lo[s][:, :, :], two(ps), qk_hi[s][:, :, :], ALU.subtract).then_inc(free_of(key), 1)

            def stacks(s, step, it):
                use, dst, tile, _ = sel_tiles(step[-1])[0]
                ps = filled(dve, it, (s, step, use))
                dve.tensor_copy(dst[s][:, tile:tile + 2, :], two(ps)).then_inc(free_of((s, step, use)), 1)

            def maxima(s, a, h, it):
                g = 8 * (2 * a + s) + h
                dve.wait_ge(scores_full, it * 48 + (g + 1))
                dve.tensor_reduce(nm[s][:, :, h], two(scores[g % 2], RT)[:, :, 0:T], AX.X, ALU.max, negate=True
                                  ).then_inc(max_done, 1)

            def divide(s, a, it):
                key = (s, f"turn{a}", "x")
                ps = filled(dve, it, key)
                r = ps[0:HT, :].rearrange("p (n c) -> p n c", c=32)
                dve.reciprocal(rc[s][:, :], r[:, :, HD]).then_inc(recip_ready[s], 1)
                dve.wait_ge(recip_ready[s], it * 3 + (a + 1))
                dve.tensor_tensor(ao[s][:, :, :], r[:, :, 0:HD], rc[s][:, :, None].to_broadcast([HT, 2 * HEADS, HD]),
                                  ALU.mult).then_inc(free_of(key), 1)

            def add(s, key, it, twice=False):
                ps = filled(dve, it, key)
                if twice:
                    i = dve.scalar_tensor_tensor(out=xT[s][:, :], in0=xT[s][:, :], scalar=2.0, in1=ps[:, 0:TP],
                                                 op0=ALU.mult, op1=ALU.add)
                else:
                    i = dve.tensor_tensor(xT[s][:, :], xT[s][:, :], ps[:, 0:TP], ALU.add)
                i.then_inc(free_of(key), 1)

            def gated(s, l, it):
                for f in range(FC):
                    key = (s, f"glu{l}", f"f{f}")
                    n = FC * l + f + 1
                    dve.wait_ge(th_ready[s], it * 2 * FC + n)
                    ps = misc[where[key][0]]
                    dve.scalar_tensor_tensor(out=gl[s][:, f, :], in0=th[s][:, f, :], scalar=1.0, in1=ps[0:FP, 0:TP],
                                             op0=ALU.add, op1=ALU.mult).then_inc(glu_half[s], 1)
                    dve.wait_ge(glu_half[s], it * 2 * FC + n)
                    dve.tensor_tensor(gl[s][:, f, :], gl[s][:, f, :], ps[0:FP, TP:2 * TP], ALU.mult
                                      ).then_inc(free_of(key), 1)

            def stack(s, it):
                key = (s, "qkv2", "qk")
                ps = filled(dve, it, key)
                qk = ps[0:HT, 0:4 * HEADS].rearrange("p (k n) -> p k n", k=2)
                q, k_ = qk[:, :, 0:HEADS], qk[:, :, HEADS:2 * HEADS]

                def twice(ap):
                    return ap[:, :, :, None].to_broadcast([HT, 2, HEADS, 2])

                q_hi = stq[s][:, :, :, 0]
                dve.tensor_copy(stq[s][:, :, :, 0:2], twice(q)).then_inc(stack_step[s], 1)
                dve.tensor_scalar(kf[s][:, 0, :, :], k_, 2.0, None, ALU.mult).then_inc(stack_step[s], 1)
                dve.wait_ge(stack_step[s], it * 8 + 2)
                for j in range(2):
                    i = dve.tensor_tensor(stq[s][:, :, :, 2 + j], q, q_hi, ALU.subtract)
                i.then_inc(free_of(key), 1)
                dve.tensor_copy(stk[s][:, :, :, 0:3:2], twice(kf[s][:, 0, :, :])).then_inc(stack_step[s], 1)
                dve.scalar_tensor_tensor(out=kf[s][:, 1, :, :], in0=kf[s][:, 0, :, :], scalar=-0.25,
                                         in1=kf[s][:, 0, :, :], op0=ALU.mult, op1=ALU.mult).then_inc(stack_step[s], 1)
                dve.wait_ge(stack_step[s], it * 8 + 4)
                for j in range(2):
                    i = dve.tensor_tensor(stk[s][:, :, :, 1 + 2 * j], kf[s][:, 0, :, :], stk[s][:, :, :, 0], ALU.subtract)
                i.then_inc(stack_step[s], 1)
                dve.tensor_copy(stk[s][:, :, :, 4], kf[s][:, 1, :, :]).then_inc(stack_step[s], 1)
                dve.wait_ge(stack_step[s], it * 8 + 6)
                dve.tensor_tensor(stk[s][:, :, :, 5], kf[s][:, 1, :, :], stk[s][:, :, :, 4], ALU.subtract
                                  ).then_inc(stack_step[s], 1)
                dve.drain().then_inc(stack_step[s], 1)

            def masks(s, it):
                drained(dve, it, (s, "stack", "x"))
                for h in range(4):
                    i = dve.tensor_scalar(km[s][:, h, :], k3[s][:, :], w("mask")[:, h:h + 1], None, ALU.mult)
                i.then_inc(masks_dve[s], 1)

            def choose(s, it):
                key = (s, "route", "logits")
                ps = filled(dve, it, key)
                dve.tensor_tensor(lg[s][:, :, :], ps[0:HT, 0:2 * EXPERTS].rearrange("p (k e) -> p k e", k=2),
                                  w("br", HT)[:, None, :].to_broadcast([HT, 2, EXPERTS]), ALU.add).then_inc(free_of(key), 1)
                b, nth = where[key]
                wait_apart(dve, free[b], it * uses[b] + (nth + 2))
                for k in range(2):
                    dve.max(top[s][:, k, :], lg[s][:, k, :]).then_inc(top_step[s], 1)
                dve.wait_ge(top_step[s], it * 5 + 2)
                dve.tensor_tensor(gd[s][:, :], top[s][:, :, 1], top[s][:, :, 0], ALU.subtract).then_inc(gd_ready[s], 1)
                for k in range(2):
                    dve.max_index(topi[s][:, k, :], top[s][:, k, :], lg[s][:, k, :]).then_inc(top_step[s], 1)
                dve.wait_ge(top_step[s], it * 5 + 4)
                dve.tensor_copy(chosen[s][:, :].rearrange("p (k c) -> p k c", k=2), topi[s][:, :, 0:2]).then_inc(top_step[s], 1)
                dve.wait_ge(top_step[s], it * 5 + 5)
                dve.tensor_tensor(oneh[s][:, :, :], w("iota", HT)[:, None, :].to_broadcast([HT, 4, EXPERTS]),
                                  chosen[s][:, :, None].to_broadcast([HT, 4, EXPERTS]), ALU.is_equal)
                dve.tensor_tensor(onehb[s][:, :, :], w("iota", HT)[:, None, :].to_broadcast([HT, 4, EXPERTS]),
                                  chosen[s][:, :, None].to_broadcast([HT, 4, EXPERTS]), ALU.is_equal).then_inc(chosen_ready[s], 1)
                dve.wait_ge(ge_ready[s], it + 1)
                dve.tensor_scalar(gs[s][:, :], ge[s][:, :], 1.0, None, ALU.add).then_inc(gate_step[s], 1)
                dve.wait_ge(gate_step[s], it * 2 + 1)
                dve.reciprocal(gr[s][:, :], gs[s][:, :]).then_inc(gate_step[s], 1)
                dve.wait_ge(gate_step[s], it * 2 + 2)
                dve.tensor_copy(gates[:, bass.ds((it * 2 + s) * 2, 2), 0], gr[s][:, :])
                dve.tensor_tensor(gates[:, bass.ds((it * 2 + s) * 2, 2), 1], ge[s][:, :], gr[s][:, :], ALU.mult)

            def place(s, it):
                key = (s, "slots", "x")
                ps = filled(dve, it, key)
                dve.tensor_copy(cnt3[s][:, :, :], ps[0:HT, 0:3 * EXPERTS].rearrange("p (k e) -> p k e", k=3)
                                ).then_inc(free_of(key), 1)
                drained(dve, it, key)
                dve.wait_ge(nxt_ready, it * 2 + (s + 1))
                dve.tensor_tensor(rank[s][:, :, :], cnt3[s][:, 0:2, :], nxt[:, None, :].to_broadcast([HT, 2, EXPERTS]), ALU.add
                                  ).then_inc(slot_step[s], 1)
                dve.wait_ge(slot_step[s], it * SLOT_STEPS + 1)
                dve.tensor_tensor(nxt[:, :], nxt[:, :], cnt3[s][:, 2, :], ALU.add).then_inc(nxt_ready, 1)
                for k in range(2):
                    i = dve.tensor_tensor(cand[s][:, 2 * k:2 * k + 2, :], oneh[s][:, 2 * k:2 * k + 2, :],
                                          rank[s][:, k:k + 1, :].to_broadcast([HT, 2, EXPERTS]), ALU.mult)
                i.then_inc(slot_step[s], 1)
                dve.wait_ge(slot_step[s], it * SLOT_STEPS + 2)
                dve.tensor_reduce(slotf[s][:, :], cand[s][:, :, :], AX.X, ALU.add).then_inc(slot_step[s], 1)
                dve.wait_ge(slot_step[s], it * SLOT_STEPS + 3)
                dve.tensor_copy(slots[:, bass.ds((it * 2 + s) * 2, 2), :], slotf[s][:, :].rearrange("p (k c) -> p k c", k=2))
                dve.wait_ge(sends_done[s], it + 1)
                dve.tensor_copy(slotu[s][:, :], slotf[s][:, :])
                dve.wait_ge(tok_ready[s], it + 1)
                dve.tensor_copy(toku[s][:, :], tokf[s][:, :]).then_inc(slot_step[s], 1)
                dve.wait_ge(slot_step[s], it * SLOT_STEPS + 4)
                dve.tensor_scalar(tokf[s][:, :], tokf[s][:, :], float(2 * T), None, ALU.add).then_inc(tok_ready[s], 1)

            with dve.Fori(0, turns) as it:
                for s, step, a in order:
                    n = int("0" + "".join(c for c in step if c.isdigit()))
                    if step == "patch":
                        embed(s, it)
                    elif step.startswith("sum"):
                        mean_square(s, n, it)
                    elif step.startswith("scale"):
                        normed(s, n, it)
                    elif step.startswith("center"):
                        centered(s, n, it)
                    elif step.startswith("qkv"):
                        if n < 2:
                            qk_low(s, n, it)
                        else:
                            stack(s, it)
                    elif step.startswith("sel"):
                        stacks(s, step, it)
                    elif step.startswith("head"):
                        if n < HEADS:
                            maxima(s, a, n, it)
                    elif step.startswith("turn"):
                        divide(s, n, it)
                    elif step.startswith("proj"):
                        add(s, (s, step, "x"), it, twice=(n == 2))
                    elif step.startswith("glu"):
                        gated(s, n, it)
                    elif step.startswith("down"):
                        add(s, (s, step, "x"), it)
                    elif step == "masks":
                        masks(s, it)
                    elif step == "route":
                        choose(s, it)
                    elif step == "slots":
                        place(s, it)

            dve.drain().then_inc(stage1_done, 1)
            dve.wait_ge(nxt_ready, 2 * turns + 1)
            at = [0]

            def step(ins):
                ins.then_inc(map_step, 1)
                at[0] += 1
                dve.wait_ge(map_step, at[0])

            first, fill, number = w("first", HT), w("fill", HT), w("block", 1)
            step(dve.tensor_tensor(held[:, :], nxt[:, :], first, ALU.subtract))
            step(dve.tensor_tensor(fills[:, :, :], held[:, :, None].to_broadcast([HT, EXPERTS, region_blocks]),
                                   fill[:, None, :].to_broadcast([HT, EXPERTS, region_blocks]), ALU.is_gt))
            step(dve.tensor_reduce(nblk[:, :], fills[:, :, :], AX.X, ALU.add))
            step(dve.tensor_scalar(jump[:, :], nblk[:, :], -float(BLK), float(region), ALU.mult, ALU.add))
            step(dve.memset(cum[:, 0:1], 0.0))
            for e in range(EXPERTS):
                step(dve.tensor_tensor(cum[:, e + 1:e + 2], cum[:, e:e + 1], nblk[0:1, e:e + 1], ALU.add))
            step(dve.tensor_tensor(past[:, :, :], number[:, :, None].to_broadcast([1, blocks, EXPERTS]),
                                   cum[:, None, 1:EXPERTS + 1].to_broadcast([1, blocks, EXPERTS]), ALU.is_ge))
            step(dve.tensor_reduce(of_expert[:, :], past[:, :, :], AX.X, ALU.add))
            step(dve.tensor_scalar(work[:, 0, :], of_expert[:, :], float(EXPERTS - 1), None, ALU.min))
            step(dve.tensor_tensor(jumped[:, :, :], past[:, :, :], jump[0:1, None, :].to_broadcast([1, blocks, EXPERTS]), ALU.mult))
            step(dve.tensor_reduce(of_row[:, :], jumped[:, :, :], AX.X, ALU.add))
            step(dve.scalar_tensor_tensor(out=work[:, 1, :], in0=number, scalar=float(BLK), in1=of_row[:, :],
                                          op0=ALU.mult, op1=ALU.add))
            assert at[0] == MAP_STEPS
            rows_of = slots[:, :, :].rearrange("p n c -> p (n c)")
            for e in range(1, EXPERTS):
                step(dve.tensor_scalar(less[:, :], rows_of, float(e * region), jump[:, e - 1:e], ALU.is_ge, ALU.mult))
                step(dve.tensor_tensor(moved[:, :], (rows_of if e == 1 else moved[:, :]), less[:, :], ALU.subtract))

            with dve.Fori(0, blocks // 2) as it:
                for k in range(2):
                    dve.wait_ge(turned, it * 2 + (k + 3))
                    dve.tensor_copy(ex[k], scores[k][:, :]).then_inc(tokens_ready, 1)
                for k in range(2):
                    dve.wait_ge(y_full, it * 2 + (k + 3))
                    dve.wait_ge(y_stored[k], it * 16 + 16)
                    dve.tensor_copy(ey[k], [heads, misc[0]][k][:, :].rearrange("p (c n) -> p c n", c=BC)).then_inc(y_ready, 1)

            with dve.Fori(0, images) as it:
                for k in range(2):
                    rows = T - HT if k else HT
                    r = slice(0, rows)
                    m = mix[k]
                    dve.tensor_scalar(m[:, 0:1, :], h1r[:, bass.ds(it * 2 + k, 1), :], 2.0, None, ALU.mult).then_inc(mix_step[k], 1)
                    dve.wait_ge(rows_got[k], it * 32 + 32)
                    dve.wait_ge(mix_step[k], it * 5 + 1)
                    dve.scalar_tensor_tensor(out=m[r, 1, :], in0=gy[k][r, 0, :], scalar=gg[k][r, 0:1], in1=m[r, 0, :],
                                             op0=ALU.mult, op1=ALU.add).then_inc(mix_step[k], 1)
                    dve.wait_ge(mix_step[k], it * 5 + 2)
                    dve.scalar_tensor_tensor(out=m[r, 2, :], in0=gy[k][r, 1, :], scalar=gg[k][r, 1:2], in1=m[r, 1, :],
                                             op0=ALU.mult, op1=ALU.add).then_inc(gather_free[k], 1)
                    dve.wait_ge(gather_free[k], it + 2)
                    dve.bn_stats(bn6[k][r, :], m[r, 2, :]).then_inc(mix_step[k], 1)
                    wait_apart(dve, mix_step[k], it * 5 + 3)
                    dve.bn_aggr(bn2[k][r, :], bn6[k][r, :]).then_inc(mix_step[k], 1)
                    dve.wait_ge(mix_step[k], it * 5 + 4)
                    dve.tensor_scalar(bn2[k][r, 1:2], bn2[k][r, 1:2], EPS_LN, None, ALU.add).then_inc(var_ready[k], 1)
                    dve.wait_ge(sd_ready[k], it + 1)
                    dve.reciprocal(rs[k][r, :], sd[k][r, :]).then_inc(mix_step[k], 1)
                    dve.wait_ge(mix_step[k], it * 5 + 5)
                    dve.wait_ge(out_stored[k], it * 16 + 16)
                    dve.tensor_scalar(fin[k][r, :], m[r, 2, :], bn2[k][r, 0:1], rs[k][r, :], ALU.subtract, ALU.mult
                                      ).then_inc(fin_ready[k], 1)


MAP_STEPS = 4 + EXPERTS + 7
SLOT_STEPS = 4


def layouts(images, x, L0_tok_conv_w, L0_tok_conv_b, L0_tok_cls_token, L0_tok_pos_emb, L0_tok_ln_f,
            L0_attn_Wq, L0_attn_Wk, L0_attn_Wv, L0_attn_Wm, L0_ffn_ln_g, L0_ffn_ln_b, L0_ffn_w_r,
            L0_ffn_b_r, L0_ffn_W1, L0_ffn_b1, L0_ffn_W2, L0_ffn_b2, **rest):
    import numpy as np

    cols, n = pack_layout(images)
    blocks, region_blocks, region, all_slots = sizes(images)
    pack = np.zeros((128, n), np.float32)

    def put(name, a, col=0):
        at = cols[name][0] + col
        pack[0:a.shape[0], at:at + a.shape[1]] = a

    put("conv", np.asarray(L0_tok_conv_w).reshape(D, PK, 128).transpose(2, 1, 0).reshape(128, PK * D))
    pos = np.asarray(L0_tok_pos_emb)[0].T
    put("pos", pos)
    put("pos", pos[:, T - 1:T], T)
    put("cls", np.asarray(L0_tok_cls_token).reshape(D, 1))
    put("conv_b", np.asarray(L0_tok_conv_b).reshape(D, 1))
    for l in range(2):
        r = {k: np.asarray(rest[f"L0_tok_{k}_{l}"]) for k in ("ln1", "qkv", "wo", "ln2", "gate", "up", "down")}
        put(f"ln1_{l}", r["ln1"].reshape(D, 1))
        put(f"ln2_{l}", r["ln2"].reshape(D, 1))
        put(f"qk_{l}", r["qkv"][0:2 * D].T)
        put(f"v_{l}", r["qkv"][2 * D:].T)
        put(f"wo_{l}", r["wo"].T)
        put(f"gate_{l}", r["gate"].T)
        put(f"up_{l}", r["up"].T)
        down = r["down"].T
        for f in range(FC):
            put(f"down_{l}", down[f * FP:(f + 1) * FP], f * D)
    put("ln_f", np.asarray(L0_tok_ln_f).reshape(D, 1))
    for h in range(HEADS):
        at = cols["qk_2"][0]
        pack[h * HD:(h + 1) * HD, at + h] = np.asarray(L0_attn_Wq)[h]
        pack[h * HD:(h + 1) * HD, at + HEADS + h] = np.asarray(L0_attn_Wk)[h]
        at = cols["v_2"][0]
        pack[h * HD:(h + 1) * HD, at + h * HD:at + (h + 1) * HD] = np.asarray(L0_attn_Wv)[h]
        pack[h * HD:(h + 1) * HD, cols["mask"][0] + h] = 1.0
    put("wo_2", np.asarray(L0_attn_Wm))
    put("ln_g", np.asarray(L0_ffn_ln_g).reshape(D, 1))
    put("ln_b", np.asarray(L0_ffn_ln_b).reshape(D, 1))
    put("wr", np.asarray(L0_ffn_w_r).T)
    put("br", np.broadcast_to(np.asarray(L0_ffn_b_r), (128, EXPERTS)))

    put("center", (np.eye(D) - 1.0 / D).astype(np.float32))
    put("ident", np.eye(D, dtype=np.float32))
    put("lower", np.triu(np.ones((HT, HT), np.float32), 1))
    put("iota", np.broadcast_to(np.arange(EXPERTS, dtype=np.float32), (128, EXPERTS)))
    put("first", np.broadcast_to(np.arange(EXPERTS, dtype=np.float32) * region, (128, EXPERTS)))
    t = np.arange(HT, dtype=np.float32)[:, None]
    put("token", np.concatenate([t, t + HT, t + T, t + T + HT], 1))
    put("inv", np.full((128, 1), 1.0 / D, np.float32))
    put("fill", np.broadcast_to(np.arange(region_blocks, dtype=np.float32) * BLK, (128, region_blocks)))
    put("block", np.arange(blocks, dtype=np.float32)[None, :])

    sel = np.zeros((128, 2, 4 + HEADS, 128), np.float32)
    for h in range(HEADS):
        for d in range(HD):
            row = 64 * (h % 2) + d
            for group, (q_part, k_part) in enumerate(((0, 0), (0, 1), (1, 0), (1, 1))):
                sel[h * HD + d, q_part, h // 2, row + 16 * group] = 1.0
                sel[h * HD + d, k_part, 4 + h, row + 16 * group] = 1.0

    pixels = np.asarray(x)[0:images].reshape(images, 3, 14, 16, 14, 16).transpose(0, 1, 3, 5, 2, 4)
    pixels = pixels.reshape(images, PK, 128, T - 1).transpose(0, 2, 1, 3)
    img = np.zeros((images, 128, PK, TP), np.float32)
    img[:, :, :, 1:T] = pixels
    img[:, :, :, T] = pixels[:, :, :, T - 2]

    experts = np.zeros((EXPERTS, 128, EXPERT_COLS), np.float32)
    experts[:, :, 0:EH] = np.asarray(L0_ffn_W1)
    experts[:, :, EH:EH + EC * D] = np.asarray(L0_ffn_W2).reshape(EXPERTS, EC, 128, D).transpose(0, 2, 1, 3).reshape(EXPERTS, 128, EC * D)
    experts[:, :, EH + EC * D:EH + EC * D + EC] = np.asarray(L0_ffn_b1).reshape(EXPERTS, EC, 128).transpose(0, 2, 1)
    experts[:, 0, EH + EC * D + EC:] = np.asarray(L0_ffn_b2)
    return {"img": img, "pack": pack, "sel": sel.reshape(128, 2 * SEL_COLS), "experts": experts}


def kernel(**inputs):
    import numpy as _np
    import concourse.bacc as _bacc
    from concourse import mybir as _mybir
    from concourse.bass_utils import run_bass_kernel_spmd as _run

    images = inputs["x"].shape[0]
    arrays = layouts(images, **inputs)
    nc = _bacc.Bacc("TRN2", target_bir_lowering=False, num_devices=1)
    args = [nc.dram_tensor(f"in_{name}", a.shape, _mybir.dt.float32, kind="ExternalInput").ap()
            for name, a in arrays.items()]
    out = nc.dram_tensor("out_rows", (images * T, D), _mybir.dt.float32, kind="ExternalOutput").ap()
    vit_moe_kernel(nc, *args, out)
    r = _run(nc, [{f"in_{name}": a for name, a in arrays.items()}], core_ids=[0])
    return r.results[0]["out_rows"].reshape(images, T, D)
```

```python
from contextlib import ExitStack

import concourse.bass as bass
from concourse import mybir

F32 = mybir.dt.float32
F32R = mybir.dt.float32r
BF16 = mybir.dt.bfloat16
U32 = mybir.dt.uint32
ALU = mybir.AluOpType
ACT = mybir.ActivationFunctionType
AX = mybir.AxisListType

D = 128
HEADS = 8
HD = D // HEADS
T = 197
TP = 198
HT = TP // 2
RT = 100
PK = 6
FF = 345
FC = 3
FP = FF // FC
SLOTS = 4
SHARED_BANKS = 3
NORMS = 8
EXPERTS = 8
EH = 512
EC = EH // 128
BLK = 512
BC = BLK // 128
EPS_RMS = 1e-6
EPS_LN = 1e-5


def sizes(images):
    tokens = images * T
    blocks = (2 * tokens + EXPERTS * (BLK - 1)) // BLK
    blocks += blocks % 2
    region_blocks = (tokens + BLK - 1) // BLK
    region = region_blocks * BLK
    return blocks, region_blocks, region, EXPERTS * region + blocks * BLK


def pack_layout(images):
    blocks, region_blocks, _, _ = sizes(images)
    cols = [("conv", PK * D), ("pos", TP), ("cls", 1), ("conv_b", 1)]
    for l in range(2):
        cols += [(f"ln1_{l}", 1), (f"ln2_{l}", 1), (f"qk_{l}", 2 * D), (f"v_{l}", D), (f"wo_{l}", D),
                 (f"gate_{l}", FF), (f"up_{l}", FF), (f"down_{l}", FC * D)]
    cols += [("ln_f", 1), ("qk_2", 2 * HEADS), ("v_2", D), ("wo_2", D), ("ln_g", 1), ("ln_b", 1),
             ("wr", EXPERTS), ("br", EXPERTS), ("center", D), ("ident", D), ("mask", HEADS),
             ("lower", HT), ("iota", EXPERTS), ("first", EXPERTS), ("token", 2 * SLOTS), ("inv", 1),
             ("fill", region_blocks), ("block", blocks)]
    at, out = 0, {}
    for name, n in cols:
        out[name] = (at, n)
        at += n
    return out, at


SEL_COLS = 4 * D + HEADS * D
EXPERT_COLS = EH + EC * D + EC + D

CHAINS = [
    ["patch", "sum0", "scale0", "qkv0", "sel0a", "sel0b", "sel0c"],
    ["values0", "turn0", "back0", "proj0", "sum1", "scale1", "glu0a", "glu0b", "glu0c", "down0", "sum2", "scale2", "qkv1",
     "sel1a", "sel1b", "sel1c"],
    ["values1", "turn1", "back1", "proj1", "sum3", "scale3", "glu1a", "glu1b", "glu1c", "down1", "sum4", "scale4", "center0",
     "sum5", "scale5", "qkv2", "stack", "masks"],
    ["values2", "turn2", "back2", "proj2", "center1", "sum6", "scale6", "center2", "sum7", "scale7", "route",
     "slots"],
]
LAG = 2
HEAD_STEPS = [f"head{i}" for i in range(HEADS + LAG)]


STEP_COST = {
    "patch": (1650, 1100, 500), "sum": (250, 1250, 350), "scale": (400, 950, 600),
    "center": (350, 900, 600), "qkv": (1150, 850, 900), "sel": (850, 50, 650), "stack": (350, 2000, 700),
    "masks": (0, 0, 0), "values": (800, 1000, 0), "turn": (450, 900, 800), "back": (170, 600, 500),
    "proj": (350, 1150, 550), "glu": (680, 0, 1000), "gluc": (680, 1000, 1000), "down": (1000, 1150, 550),
    "route": (1100, 2600, 900), "slots": (200, 0, 600), "head": (600, 0, 0), "head0": (170, 0, 0),
    "head1": (170, 0, 0), "head7": (1500, 0, 0),
}
MAXIMA, EXPONENTIALS, COPY = 750, 900, 600


def cost_of(step):
    for kind in (step, step.translate({ord(c): None for c in "0123456789"}), step.rstrip("0123456789abc")):
        if kind in STEP_COST:
            return STEP_COST[kind]


def plan_body():
    streams = []
    heads = []

    def spread(into, steps, first, last, a=None):
        n = len(steps)
        into.extend((first + (i + 0.5) / n * (last - first), x, a) for i, x in enumerate(steps))

    for s in range(SLOTS):
        chain = []
        spread(chain, CHAINS[0], s - 2.5, s)
        for a in range(3):
            w = SLOTS * a + s
            steps = []
            spread(steps, HEAD_STEPS, w, w + 1, a)
            heads += [(due, (s, x, a)) for due, x, a in steps]
            spread(chain, CHAINS[a + 1], w + 1, w + SLOTS)
        streams.append([(due, (s, x, a)) for due, x, a in chain])
    streams.append(sorted(heads))

    order, end = [], {}
    now, ready, drained, used = 0, [0] * len(streams), [0] * SHARED_BANKS, 0

    def earliest(s, step, a):
        needs = []
        if step == "head0":
            needs += [((s, ["sel0c", "sel1c", "masks"][a], None), 800)]
        if step.startswith("head") and int(step[4:]) >= LAG:
            needs += [((s, f"head{int(step[4:]) - 2}", a), MAXIMA)]
        w = SLOTS * (a or 0) + s
        if step == "head7" and w:
            needs += [(((w - 1) % SLOTS, f"values{(w - 1) // SLOTS}", None), COPY)]
        if step.startswith("values"):
            needs += [((s, "head9", int(step[6:])), EXPONENTIALS)]
        if step in ("sel0a", "sel1a", "stack"):
            w = SLOTS * ["sel0a", "sel1a", "stack"].index(step) + s - 2
            needs += [((w % SLOTS, "head9", w // SLOTS), 0)] if w >= 0 else []
        if any(x not in end for x, _ in needs):
            return None
        return max([end[x] + later for x, later in needs], default=0)

    while any(streams):
        best = None
        for n, stream in enumerate(streams):
            if stream:
                due, x = stream[0]
                at = earliest(*x)
                if at is not None:
                    at = max([at, now, ready[n]] + [drained[(used + k) % SHARED_BANKS] for k in range(len(uses_of(x[1])))])
                    key = ((at - now) // 60, due)
                    if best is None or key < best[0]:
                        best = key, n, at
        _, n, at = best
        _, x = streams[n].pop(0)
        time, then, drain = cost_of(x[1])
        now = at + time
        ready[n] = now + then
        for _ in uses_of(x[1]):
            drained[used % SHARED_BANKS] = now + drain
            used += 1
        end[x] = now
        order.append(x)

    on_act, on_dve = [], []
    for s, step, a in order:
        t = end[(s, step, a)]
        if step.startswith("sum"):
            on_act.append((end[(s, NORM_SOURCE[int(step[3:])], None)] + 450, (s, step, a)))
        elif step == "masks":
            on_act.append((t + 600, (s, step, a)))
        else:
            on_act.append((t, (s, step, a)))
        late = {"masks": 600, "qkv": 350, "glu": 350}
        on_dve.append((t + late.get(step.rstrip("0123456789abc"), 0), (s, step, a)))
    by_time = lambda x: [step for _, step in sorted(x, key=lambda y: y[0])]
    return order, by_time(on_act), by_time(on_dve)


def uses_of(step):
    kind = step.rstrip("0123456789abc")
    return {"qkv": ["qk", "v"], "sel": ["p0", "p1"], "values": [],
            "route": ["rows", "logits"], "head": [], "masks": []}.get(kind, ["x"])


def plan_banks(order, banks):
    where, count, n = {}, [0] * banks, 0
    for s, step, _ in order:
        for use in uses_of(step):
            where[(s, step, use)] = (n % banks, count[n % banks])
            count[n % banks] += 1
            n += 1
    return where, count


NORM_SOURCE = ["patch", "proj0", "down0", "proj1", "down1", "center0", "center1", "center2"]
NORM_WEIGHT = {0: "ln1_0", 1: "ln2_0", 2: "ln1_1", 3: "ln2_1", 4: "ln_f", 7: "ln_g"}
CENTER_SOURCE = ["scale4", "proj2", "scale6"]
SCALE = float(HD) ** -0.5
HEADS_A_TURN = SLOTS * 3 * HEADS
ATTENTIONS = SLOTS * 3


def vit_moe_kernel(nc, img, pack, sel, experts, out):
    images = img.shape[0]
    turns = images // SLOTS
    blocks, region_blocks, region, all_slots = sizes(images)
    tiles = 2 * images
    cols, pack_cols = pack_layout(images)
    order, act_order, dve_order = plan_body()
    MB = SHARED_BANKS
    where, uses = plan_banks(order, MB)

    stream_rows = nc.dram_tensor("stream_rows", [images, HT, 2 * D], F32, kind="Internal").ap()
    token_rows = nc.dram_tensor("token_rows", [images * T, D], F32, kind="Internal").ap()
    slot_token = nc.dram_tensor("slot_token", [all_slots, 1], U32, kind="Internal").ap()
    slot_rows = nc.dram_tensor("slot_rows", [blocks * BLK, D], F32, kind="Internal").ap()

    with ExitStack() as ctx:
        def sb(name, shape, dt=F32):
            return ctx.enter_context(nc.sbuf_tensor(name, shape, dt))

        def pair(name, shape, dt=F32):
            return [sb(f"{name}{s}", shape, dt) for s in range(2)]

        def each(name, shape, dt=F32):
            return [sb(f"{name}{s}", shape, dt) for s in range(SLOTS)]

        def shared(name, shape, dt=F32):
            return pair(name, shape, dt) * (SLOTS // 2)

        def bank(name):
            return ctx.enter_context(nc.psum_tensor(name, [128, 512], F32))

        def sem(name):
            return ctx.enter_context(nc.semaphore(name))

        def sems(name, n=2):
            return [sem(f"{name}{s}") for s in range(n)]

        wp = sb("wp", [128, pack_cols])

        def w(name, rows=128):
            at, n = cols[name]
            return wp[0:rows, at:at + n]

        selr = sb("selr", [128, 2, SEL_COLS], F32R)
        identr = sb("identr", [RT, RT], F32R)
        lowb = sb("lowb", [HT, HT], BF16)
        onesb = sb("onesb", [HT, HT], BF16)
        minus_half = sb("minus_half", [HT, 2])
        ones1 = sb("ones1", [1, 128])

        imgs = shared("imgs", [128, PK, TP])
        xT = each("xT", [128, TP])
        hT = each("hT", [128, TP])
        sq = each("sq", [128, TP])
        ms = each("ms", [HT, 2])
        rn = each("rn", [HT, 2])
        qk_hi = each("qk_hi", [128, 2, TP], F32R)
        qk_lo = each("qk_lo", [128, 2, TP], F32R)
        qs = shared("qs", [128, 4, TP], F32R)
        km = shared("km", [128, HEADS, TP], F32R)
        va = each("va", [HT, 2, HEADS, 32])
        nm = each("nm", [RT, 2, HEADS], F32R)
        ptw = shared("ptw", [128, HEADS * 2 * TP])
        pt = [x[0:HT, :].rearrange("p (h k t) -> p h k t", h=HEADS, k=2) for x in ptw]
        ot = each("ot", [128, 2, TP])
        rc = each("rc", [HT, 2 * HEADS])
        ao = each("ao", [HT, 2 * HEADS, HD])
        aT = each("aT", [128, TP])
        th = each("th", [FP, FC, TP])
        gl = each("gl", [FP, FC, TP])
        stq = each("stq", [HT, 2, HEADS, HD], F32R)
        stk = each("stk", [HT, 2, HEADS, HD], F32R)
        kf = each("kf", [HT, 2, 2, HEADS])
        k3 = each("k3", [128, TP])
        srows = each("srows", [HT, 2, D])
        hmr = each("hmr", [HT, 2, D])
        lg = each("lg", [HT, 2, EXPERTS])
        top = each("top", [HT, 2, 8])
        topi = each("topi", [HT, 2, 8], U32)
        chosen = each("chosen", [HT, 4])
        gd = each("gd", [HT, 2])
        ge = each("ge", [HT, 2])
        gs = each("gs", [HT, 2])
        gr = each("gr", [HT, 2])
        oneh = each("oneh", [HT, 4, EXPERTS])
        onehb = each("onehb", [HT, 4, EXPERTS], BF16)
        cnt3 = each("cnt3", [HT, 3, EXPERTS])
        rank = each("rank", [HT, 2, EXPERTS])
        cand = each("cand", [HT, 4, EXPERTS])
        slotf = each("slotf", [HT, 4])
        slotu = each("slotu", [HT, 4], U32)
        tokf = each("tokf", [HT, 2])
        toku = each("toku", [HT, 2], U32)

        gates = sb("gates", [HT, tiles, 2])
        slots = sb("slots", [HT, tiles, 2])
        nxt = sb("nxt", [HT, EXPERTS])
        zeros = sb("zeros", [128, all_slots // 128], U32)

        hid = [x[:, 0:EC * BLK].rearrange("p (f n) -> p f n", f=EC) for x in ptw[0:2]]
        ex = [x[:, EC * BLK:(EC + 1) * BLK] for x in ptw[0:2]]
        ey = [x[:, (EC + 1) * BLK:(EC + 2) * BLK].rearrange("p (c n) -> p c n", c=BC) for x in ptw[0:2]]
        exr = [x[:, :, :].rearrange("p a b -> p (a b)")[:, 0:BC * D].rearrange("p (c n) -> p c n", c=BC)
               for x in imgs[0:2]]
        ew = [wp[:, k * EXPERT_COLS:(k + 1) * EXPERT_COLS] for k in range(2)]
        assert 2 * EXPERT_COLS <= cols["ln_f"][0]
        ew1 = [x[:, 0:EH].rearrange("p (f n) -> p f n", f=EC) for x in ew]
        ew2 = [x[:, EH:EH + EC * D].rearrange("p (f n) -> p f n", f=EC) for x in ew]
        eb1 = [x[:, EH + EC * D:EH + EC * D + EC] for x in ew]
        eb2 = [x[0:1, EH + EC * D + EC:EXPERT_COLS] for x in ew]
        eidx = pair("eidx", [128, BC], U32)
        held = sb("held", [HT, EXPERTS])
        fills = sb("fills", [HT, EXPERTS, region_blocks])
        nblk = sb("nblk", [HT, EXPERTS])
        cum = sb("cum", [1, EXPERTS + 1])
        jump = sb("jump", [HT, EXPERTS])
        less = sb("less", [HT, 2 * tiles])
        moved = sb("moved", [HT, 2 * tiles])
        past = sb("past", [1, blocks, EXPERTS])
        jumped = sb("jumped", [1, blocks, EXPERTS])
        of_expert = sb("of_expert", [1, blocks])
        of_row = sb("of_row", [1, blocks])
        work = sb("work", [1, 2, blocks], U32)
        gidx = pair("gidx", [HT, 2], U32)
        gg = pair("gg", [HT, 2])
        gy = [x[0:HT, :, :].rearrange("p a b -> p (a b)")[:, 0:2 * D].rearrange("p (a n) -> p a n", a=2) for x in th[0:2]]
        fin = [x[0:HT, :, :].rearrange("p a b -> p (a b)")[:, 2 * D:3 * D] for x in th[0:2]]
        mix = [x[0:HT, :, :].rearrange("p a b -> p (a b)")[:, 0:3 * D].rearrange("p (a n) -> p a n", a=3) for x in gl[0:2]]
        hr = [x[0:HT, :, :].rearrange("p a b -> p (a b)")[:, 3 * D:4 * D] for x in gl[0:2]]
        bn6 = pair("bn6", [HT, 6])
        bn2 = pair("bn2", [HT, 2])
        sd = pair("sd", [HT, 1])
        rs = pair("rs", [HT, 1])

        scores = [bank(f"scores{k}") for k in range(2)]
        scoresT = [bank(f"scoresT{k}") for k in range(2)]
        heads = bank("heads")
        misc = [bank(f"misc{k}") for k in range(MB)]

        def two(ps, rows=128, n=TP):
            return ps[0:rows, 0:2 * n].rearrange("p (a n) -> p a n", a=2)

        pack_loaded = sem("pack_loaded")
        sel_loaded = sem("sel_loaded")
        consts_ready = sem("consts_ready")
        credits = sem("credits")
        zeros_ready = sem("zeros_ready")
        table_cleared = sem("table_cleared")
        img_loaded = sems("img_loaded")
        full = sems("bank_full", MB)
        free = sems("bank_drained", MB)
        scores_full = sem("scores_full")
        max_done = sem("max_done")
        scoresT_full = sem("scoresT_full")
        exp_done = sem("exp_done")
        heads_full = sem("heads_full")
        heads_copied = sem("heads_copied")
        sq_ready = sems("sq_ready", SLOTS)
        rn_ready = sems("rn_ready", SLOTS)
        hi_ready = sems("hi_ready", SLOTS)
        th_ready = sems("th_ready", SLOTS)
        glu_half = sems("glu_half", SLOTS)
        recip_ready = sems("recip_ready", SLOTS)
        stack_step = sems("stack_step", SLOTS)
        masks_dve = sems("masks_dve", SLOTS)
        masks_act = sems("masks_act", SLOTS)
        hm_ready = sems("hm_ready", SLOTS)
        top_step = sems("top_step", SLOTS)
        gd_ready = sems("gd_ready", SLOTS)
        ge_ready = sems("ge_ready", SLOTS)
        gate_step = sems("gate_step", SLOTS)
        chosen_ready = sems("chosen_ready", SLOTS)
        slot_step = sems("slot_step", SLOTS)
        nxt_ready = sem("nxt_ready")
        tok_ready = sems("tok_ready", SLOTS)
        rows_stored = sems("rows_stored", SLOTS)
        slots_sent = sems("slots_sent", SLOTS)
        sends_done = sems("sends_done", SLOTS)
        stage1_done = sem("stage1_done")
        map_step = sem("map_step")
        idx_loaded = sems("idx_loaded")
        gathered = sems("gathered")
        w_loaded = sems("w_loaded")
        turned = sem("turned")
        tokens_ready = sem("tokens_ready")
        hid_full = sem("hid_full")
        act_done = sem("act_done")
        y_full = sem("y_full")
        y_ready = sem("y_ready")
        y_stored = sems("y_stored")
        idx_ready = sems("idx_ready")
        hr_loaded = sems("hr_loaded")
        rows_got = sems("rows_got")
        mix_step = sems("mix_step")
        var_ready = sems("var_ready")
        sd_ready = sems("sd_ready")
        fin_ready = sems("fin_ready")
        out_stored = sems("out_stored")
        gather_free = sems("gather_free")

        passed = {eng.engine: sem(f"passed_{name}")
                  for name, eng in (("sp", nc.sync), ("pool", nc.gpsimd), ("dve", nc.vector))}

        def take(pe, it, key):
            b, n = where[key]
            pe.wait_ge(free[b], it * uses[b] + (n + 1))
            return misc[b]

        def filled(eng, it, key):
            b, n = where[key]
            eng.wait_ge(full[b], it * uses[b] + (n + 1))
            return misc[b]

        def drained(eng, it, *keys, taken=()):
            last = {}
            for key in keys:
                b, n = where[key]
                last[b] = max(last.get(b, 0), n)
            for b, n in last.items():
                if b not in [where[key][0] for key in taken]:
                    eng.wait_ge(free[b], it * uses[b] + (n + 2))

        def wait_apart(eng, semaphore, value):
            eng.wait_ge(semaphore, value)
            eng.sem_inc(passed[eng.engine], 1)

        def full_of(key):
            return full[where[key][0]]

        def free_of(key):
            return free[where[key][0]]

        def norm_src(s, n):
            return hT[s] if n in (5, 7) else xT[s]

        def norm_dst(s, n):
            return xT[s] if n in (4, 6) else hT[s]

        def sel_tiles(part):
            if part == "a":
                return [("p0", qs, 0, 0), ("p1", qs, 2, 2)]
            first = 0 if part == "b" else 4
            return [("p0", km, first, 4 + first), ("p1", km, first + 2, 6 + first)]

        block = ctx.enter_context(nc.Block())

        @block.sync
        def _(sp):
            sp.dma_start(wp[:, :], pack).then_inc(pack_loaded, 16)
            sp.dma_start(ptw[0][:, 0:2 * SEL_COLS], sel).then_inc(sel_loaded, 16)
            for s in range(2):
                sp.dma_start(imgs[s][:, :, :], img[s]).then_inc(img_loaded[s], 16)
            sp.wait_ge(zeros_ready, 1)
            sp.dma_start(slot_token.rearrange("(p n) o -> p (n o)", p=128), zeros[:, :]).then_inc(table_cleared, 16)

            def next_image(s, it):
                b, n = where[(s, "patch", "x")]
                nth = sp.snap(it * uses[b] + (n + 1))
                number = sp.snap(it * SLOTS + (s + 2))
                wait_apart(sp, full[b], nth)
                sp.dma_start(imgs[s][:, :, :], img[bass.ds(number, 1)].rearrange("a p k t -> (a p) k t")
                             ).then_inc(img_loaded[s % 2], 16)

            with sp.Fori(0, turns - 1) as it:
                for s in range(SLOTS):
                    next_image(s, it)
            for s in range(SLOTS - 2):
                b, n = where[(s, "patch", "x")]
                sp.wait_ge(full[b], (turns - 1) * uses[b] + (n + 1))
                sp.dma_start(imgs[s][:, :, :], img[(turns - 1) * SLOTS + s + 2]).then_inc(img_loaded[s % 2], 16)

            sp.wait_ge(map_step, MAP_STEPS)
            sp.wait_ge(stage1_done, 4)
            with sp.Fori(0, blocks // 2) as it:
                for k in range(2):
                    e = sp.value_load(work[0:1, 0, bass.ds(it * 2 + k, 1)], min_val=0, max_val=EXPERTS - 1)
                    row = sp.value_load(work[0:1, 1, bass.ds(it * 2 + k, 1)], min_val=0,
                                        max_val=all_slots - BLK)
                    nth = sp.snap(it * 2 + (k + 1))
                    wait_apart(sp, turned, nth)
                    sp.dma_start(eidx[k][:, :], slot_token[bass.ds(row, BLK), :].rearrange("(p c) o -> p (c o)", p=128)
                                 ).then_inc(idx_loaded[k], 16)
                    wait_apart(sp, y_full, nth)
                    sp.dma_start(ew[k], experts[bass.ds(e, 1)].rearrange("a p n -> (a p) n")).then_inc(w_loaded[k], 16)

            with sp.Fori(0, images) as it:
                for k in range(2):
                    rows = T - HT if k else HT
                    nth = sp.snap(it + 1)
                    first = sp.snap(it * T + k * HT)
                    wait_apart(sp, fin_ready[k], nth)
                    sp.dma_start(out[bass.ds(first, rows), :], fin[k][0:rows, :]).then_inc(out_stored[k], 16)
            for k in range(2):
                sp.wait_ge(out_stored[k], 16 * images + 16)

        @block.gpsimd
        def _(pool):
            pool.memset(zeros[:, :], 0).then_inc(zeros_ready, 1)
            pool.wait_ge(table_cleared, 16)
            pool.wait_ge(credits, 1)

            def inverse_root(s, n, it):
                drained(pool, it, (s, f"sum{n}", "x"))
                pool.tensor_tensor(rn[s][:, :], ms[s][:, :], minus_half[:, :], ALU.pow).then_inc(rn_ready[s], 1)

            def send(s, it):
                wait_apart(pool, slot_step[s], it * SLOT_STEPS + SLOT_STEPS)
                for k in range(2):
                    rows = T - HT if k else HT
                    for c in range(2):
                        pool.indirect_dma_start(
                            out=slot_token, out_offset=bass.IndirectOffsetOnAxis(ap=slotu[s][0:rows, 2 * k + c:2 * k + c + 1], axis=0),
                            in_=toku[s][0:rows, k:k + 1], in_offset=None).then_inc(slots_sent[s], 16)
                drained(pool, it, (s, "route", "rows"))
                for k in range(2):
                    rows = T - HT if k else HT
                    pool.dma_start(token_rows[bass.ds((it * SLOTS + s) * T + k * HT, rows), :], hmr[s][0:rows, k, :]
                                   ).then_inc(rows_stored[s], 16)
                pool.dma_start(stream_rows[bass.ds(it * SLOTS + s, 1)].rearrange("a p n -> (a p) n"),
                               srows[s][:, :, :].rearrange("p k n -> p (k n)")).then_inc(rows_stored[s], 16)

            def sent(s, it):
                pool.wait_ge(slots_sent[s], it * 64 + 64)
                pool.wait_ge(rows_stored[s], it * 48 + 48)
                pool.sem_inc(sends_done[s], 1)

            with pool.Fori(0, turns) as it:
                for s, step, a in order:
                    if step.startswith("sum"):
                        inverse_root(s, int(step[3:]), it)
                    if step == "slots":
                        if s:
                            sent(s - 1, it)
                        send(s, it)
                sent(SLOTS - 1, it)
            pool.drain().then_inc(stage1_done, 1)

            with pool.Fori(0, blocks // 2) as it:
                for k in range(2):
                    pool.wait_ge(idx_loaded[k], it * 16 + 16)
                    wait_apart(pool, turned, it * 2 + (k + 1))
                    for c in range(BC):
                        pool.indirect_dma_start(
                            out=exr[k][:, c, :], out_offset=None, in_=token_rows,
                            in_offset=bass.IndirectOffsetOnAxis(ap=eidx[k][:, c:c + 1], axis=0)).then_inc(gathered[k], 16)

            for k in range(2):
                pool.wait_ge(y_stored[k], 16 * (blocks // 2) + 16)
            with pool.Fori(0, images) as it:
                for k in range(2):
                    rows = T - HT if k else HT
                    pool.wait_ge(idx_ready[k], it * 2 + 2)
                    wait_apart(pool, gather_free[k], it + 1)
                    for c in range(2):
                        pool.indirect_dma_start(
                            out=gy[k][0:rows, c, :], out_offset=None, in_=slot_rows,
                            in_offset=bass.IndirectOffsetOnAxis(ap=gidx[k][0:rows, c:c + 1], axis=0)).then_inc(rows_got[k], 16)

        @block.scalar
        def _(act):
            act.sem_inc(exp_done, 2)
            act.sem_inc(heads_copied, 1)
            act.wait_ge(pack_loaded, 16)
            act.wait_ge(credits, 1)

            def square(s, n, it):
                drained(act, it, (s, NORM_SOURCE[n], "x"))
                act.activation(sq[s][:, :], norm_src(s, n)[:, :], ACT.Square).then_inc(sq_ready[s], 1)

            def qk_high(s, l, it):
                ps = filled(act, it, (s, f"qkv{l}", "qk"))
                act.activation(qk_hi[s][:, :, :], two(ps), ACT.Copy).then_inc(hi_ready[s], 1)

            def values(s, l, it):
                ps = filled(act, it, (s, f"qkv{l}", "v"))
                act.activation(va[s][:, :, :, 0:HD].rearrange("p k h d -> p (k h) d"),
                               ps[0:HT, 0:2 * D].rearrange("p (k d) -> p k d", d=HD), ACT.Copy
                               ).then_inc(free_of((s, f"qkv{l}", "v")), 1)

            def stacks(s, step, it):
                use, dst, tile, _ = sel_tiles(step[-1])[1]
                ps = filled(act, it, (s, step, use))
                act.activation(dst[s][:, tile:tile + 2, :], two(ps), ACT.Copy).then_inc(free_of((s, step, use)), 1)

            def exp(s, a, h, it):
                g = 8 * (SLOTS * a + s) + h
                act.wait_ge(scoresT_full, it * HEADS_A_TURN + (g + 1))
                act.activation(pt[s][:, h, :, :], two(scoresT[g % 2], HT), ACT.Exp, scale=SCALE).then_inc(exp_done, 1)

            def heads_copy(s, a, it):
                act.wait_ge(heads_full, it * ATTENTIONS + (SLOTS * a + s + 1))
                act.activation(ot[s][:, :, :], two(heads), ACT.Copy).then_inc(heads_copied, 1)

            def back(s, a, it):
                key = (s, f"back{a}", "x")
                ps = filled(act, it, key)
                act.activation(aT[s][:, :], ps[:, 0:TP], ACT.Copy).then_inc(free_of(key), 1)

            def tanh(s, step, it):
                ps = filled(act, it, (s, step, "x"))
                act.activation(th[s][:, "abc".index(step[4]), :], ps[0:FP, 0:TP], ACT.Tanh, scale=0.5
                               ).then_inc(th_ready[s], 1)

            def stack_copy(s, it):
                key = (s, "stack", "x")
                ps = filled(act, it, key)
                act.activation(qs[s][:, 0, :], ps[:, 0:TP], ACT.Copy)
                act.activation(k3[s][:, :], ps[:, TP:2 * TP], ACT.Copy).then_inc(free_of(key), 1)

            def masks(s, it):
                drained(act, it, (s, "stack", "x"))
                for h in range(4, HEADS):
                    i = act.activation(km[s][:, h, :], k3[s][:, :], ACT.Copy, scale=w("mask")[:, h:h + 1])
                i.then_inc(masks_act[s], 1)

            def rows(s, it):
                key = (s, "route", "rows")
                ps = filled(act, it, key)
                r = ps[0:HT, 0:4 * D].rearrange("p (a k d) -> p a k d", a=2, k=2)
                act.wait_ge(sends_done[s], it + 1)
                act.activation(srows[s][:, :, :], r[:, 0, :, :], ACT.Copy)
                act.activation(hmr[s][:, :, :], r[:, 1, :, :], ACT.Copy).then_inc(free_of(key), 1)

            with act.Fori(0, turns) as it:
                for s, step, a in act_order:
                    n = int("0" + "".join(c for c in step if c.isdigit()))
                    if step.startswith("sum"):
                        square(s, n, it)
                    elif step.startswith("qkv"):
                        if n < 2:
                            qk_high(s, n, it)
                        values(s, n, it)
                    elif step.startswith("sel"):
                        stacks(s, step, it)
                    elif step.startswith("head"):
                        if n >= LAG:
                            exp(s, a, n - LAG, it)
                    elif step.startswith("values"):
                        heads_copy(s, n, it)
                    elif step.startswith("back"):
                        back(s, n, it)
                    elif step.startswith("glu"):
                        tanh(s, step, it)
                    elif step == "stack":
                        stack_copy(s, it)
                    elif step == "masks":
                        masks(s, it)
                    elif step == "route":
                        rows(s, it)
                        act.wait_ge(gd_ready[s], it + 1)
                        act.activation(ge[s][:, :], gd[s][:, :], ACT.Exp).then_inc(ge_ready[s], 1)

            act.drain().then_inc(stage1_done, 1)
            act.sem_inc(act_done, 2)
            act.sem_inc(y_stored[0], 16)
            act.sem_inc(y_stored[1], 16)
            act.wait_ge(map_step, MAP_STEPS)
            with act.Fori(0, blocks // 2) as it:
                for k in range(2):
                    for f in range(EC):
                        n = k * EC + f
                        act.wait_ge(hid_full, it * 2 * EC + (n + 1))
                        act.activation(hid[k][:, f, :], scoresT[n % 2][:, :], ACT.Gelu, bias=eb1[k][:, f:f + 1]
                                       ).then_inc(act_done, 1)
                for k in range(2):
                    act.wait_ge(y_ready, it * 2 + (k + 3))
                    act.dma_start(slot_rows[bass.ds((it * 2 + k) * BLK, BLK), :].rearrange("(p c) n -> p c n", p=128), ey[k]
                                  ).then_inc(y_stored[k], 16)

            with act.Fori(0, images) as it:
                for k in range(2):
                    act.wait_ge(gather_free[k], it + 1)
                    act.dma_start(hr[k], stream_rows[bass.ds(it, 1), :, k * D:(k + 1) * D].rearrange("a p n -> (a p) n")
                                  ).then_inc(hr_loaded[k], 16)
                    act.activation(gidx[k][:, :], moved[:, bass.ds((it * 2 + k) * 2, 2)], ACT.Copy).then_inc(idx_ready[k], 1)
                    act.activation(gg[k][:, :], gates[:, bass.ds(it * 2 + k, 1), :].rearrange("p a c -> p (a c)"), ACT.Copy).then_inc(idx_ready[k], 1)
                for k in range(2):
                    act.wait_ge(var_ready[k], it + 1)
                    rows = T - HT if k else HT
                    act.activation(sd[k][0:rows, :], bn2[k][0:rows, 1:2], ACT.Sqrt).then_inc(sd_ready[k], 1)

        @block.tensor
        def _(pe):
            pe.sem_inc(turned, 2)
            pe.sem_inc(y_full, 2)
            pe.wait_ge(pack_loaded, 16)
            pe.wait_ge(consts_ready, 1)
            ident = w("ident")

            def patch(s, it):
                key = (s, "patch", "x")
                pe.wait_ge(img_loaded[s % 2], it * (SLOTS // 2 * 16) + (s // 2 * 16 + 16))
                ps = take(pe, it, key)
                conv = w("conv").rearrange("p (k o) -> p k o", k=PK)
                for k in range(PK):
                    mm = pe.matmul(ps[:, 0:TP], conv[:, k, :], imgs[s][:, k, :], start=(k == 0), stop=(k == PK - 1))
                mm.then_inc(full_of(key), 1)

            def sums(s, n, it):
                key = (s, f"sum{n}", "x")
                pe.wait_ge(sq_ready[s], it * NORMS + (n + 1))
                ps = take(pe, it, key)
                for k in range(2):
                    mm = pe.matmul(ps[0:HT, k:k + 1], sq[s][:, k * HT:(k + 1) * HT], w("inv"), start=True, stop=True)
                mm.then_inc(full_of(key), 1)

            def scales(s, n, it):
                key = (s, f"scale{n}", "x")
                pe.wait_ge(rn_ready[s], it * NORMS + (n + 1))
                ps = take(pe, it, key)
                for k in range(2):
                    mm = pe.matmul(ps[:, k * HT:(k + 1) * HT], rn[s][:, k:k + 1].to_broadcast([HT, 128]),
                                   ident[0:HT, 0:HT], start=True, stop=True)
                mm.then_inc(full_of(key), 1)

            def center(s, n, it):
                key = (s, f"center{n}", "x")
                drained(pe, it, (s, CENTER_SOURCE[n], "x"), taken=[key])
                ps = take(pe, it, key)
                pe.matmul(ps[:, 0:TP], w("center"), xT[s][:, :], start=True, stop=True).then_inc(full_of(key), 1)

            def qkv(s, l, it):
                drained(pe, it, (s, ["scale0", "scale2", "scale5"][l], "x"), taken=[(s, f"qkv{l}", "qk")])
                ps = take(pe, it, (s, f"qkv{l}", "qk"))
                for k in range(2):
                    if l < 2:
                        mm = pe.matmul(ps[:, k * TP:(k + 1) * TP], w(f"qk_{l}")[:, k * D:(k + 1) * D], hT[s][:, :],
                                       start=True, stop=True)
                    else:
                        mm = pe.matmul(ps[0:HT, k * 2 * HEADS:(k + 1) * 2 * HEADS], hT[s][:, k * HT:(k + 1) * HT],
                                       w("qk_2"), start=True, stop=True)
                mm.then_inc(full_of((s, f"qkv{l}", "qk")), 1)
                ps = take(pe, it, (s, f"qkv{l}", "v"))
                for k in range(2):
                    mm = pe.matmul(ps[0:HT, k * D:(k + 1) * D], hT[s][:, k * HT:(k + 1) * HT], w(f"v_{l}"),
                                   start=True, stop=True)
                mm.then_inc(full_of((s, f"qkv{l}", "v")), 1)

            def select(s, step, it):
                l, which = int(step[3]), 0 if step[-1] == "a" else 1
                drained(pe, it, (s, f"qkv{l}", "qk"), taken=[(s, step, "p0")])
                for use, _, _, at in sel_tiles(step[-1]):
                    ps = take(pe, it, (s, step, use))
                    for j in range(2):
                        for part, src in enumerate((qk_hi, qk_lo)):
                            mm = pe.matmul(ps[:, j * TP:(j + 1) * TP], selr[:, part, (at + j) * D:(at + j + 1) * D],
                                           src[s][:, which, :], start=(part == 0), stop=(part == 1))
                    mm.then_inc(full_of((s, step, use)), 1)

            def head_scores(s, a, h, it):
                g = 8 * (SLOTS * a + s) + h
                if a < 2:
                    if h == 0:
                        drained(pe, it, *[(s, f"sel{a}{x}", p) for x in "ab" for p in ("p0", "p1")])
                    if h == 4:
                        drained(pe, it, *[(s, f"sel{a}c", p) for p in ("p0", "p1")])
                elif h == 0:
                    pe.wait_ge(masks_dve[s], it + 1)
                    pe.wait_ge(masks_act[s], it + 1)
                pe.wait_ge(max_done, it * HEADS_A_TURN + (g + 1))
                q = qs[s][:, h // 2 if a < 2 else 0, :]
                for k in range(2):
                    mm = pe.matmul(scores[g % 2][0:RT, k * TP:(k + 1) * TP], q[:, k * (TP - RT):k * (TP - RT) + RT],
                                   km[s][:, h, :], start=True, stop=True)
                mm.then_inc(scores_full, 1)

            def head_scoresT(s, a, h, it):
                g = 8 * (SLOTS * a + s) + h
                pe.wait_ge(max_done, it * HEADS_A_TURN + (g + 3))
                pe.wait_ge(exp_done, it * HEADS_A_TURN + (g + 1))
                q = qs[s][:, h // 2 if a < 2 else 0, :]
                ps = scoresT[g % 2]
                for k in range(2):
                    for j in range(2):
                        skip = j * (2 * RT - TP)
                        first = k * TP + j * RT
                        pe.matmul(ps[0:HT, first:first + RT - skip], nm[s][:, j, h:h + 1].to_broadcast([RT, HT]),
                                  identr[:, skip:RT], start=(j == 0), stop=False, skip_group_check=True)
                    mm = pe.matmul(ps[0:HT, k * TP:(k + 1) * TP], km[s][:, h, k * HT:(k + 1) * HT], q,
                                   start=False, stop=True, skip_group_check=True)
                mm.then_inc(scoresT_full, 1)

            def head_values(s, a, g, it):
                n = SLOTS * a + s
                if g == 0:
                    drained(pe, it, (s, f"qkv{a}", "v"))
                    pe.wait_ge(heads_copied, it * ATTENTIONS + (n + 1))
                pe.wait_ge(exp_done, it * HEADS_A_TURN + (8 * n + 4 * g + 3 + 3))
                for k in range(2):
                    rows = T - HT if k else HT
                    for j in range(4):
                        mm = pe.matmul(heads[32 * j:32 * j + 32, g * TP:(g + 1) * TP], va[s][0:rows, k, 4 * g + j, :],
                                       pt[s][0:rows, 4 * g + j, k, :], start=(k == 0), stop=(k == 1),
                                       skip_group_check=True)
                if g == 1:
                    mm.then_inc(heads_full, 1)

            def turn(s, a, it):
                key = (s, f"turn{a}", "x")
                pe.wait_ge(heads_copied, it * ATTENTIONS + (SLOTS * a + s + 2))
                ps = take(pe, it, key)
                for k in range(2):
                    for g in range(2):
                        mm = pe.transpose(ps[0:HT, (2 * k + g) * D:(2 * k + g + 1) * D],
                                          ot[s][:, g, k * HT:(k + 1) * HT], ident)
                mm.then_inc(full_of(key), 1)

            def back(s, a, it):
                key = (s, f"back{a}", "x")
                drained(pe, it, (s, f"turn{a}", "x"), taken=[key])
                ps = take(pe, it, key)
                for k in range(2):
                    mm = pe.transpose(ps[:, k * HT:(k + 1) * HT],
                                      ao[s][:, 8 * k:8 * k + 8, :].rearrange("p h d -> p (h d)"), ident[0:HT, 0:HT])
                mm.then_inc(full_of(key), 1)

            def proj(s, a, it):
                key = (s, f"proj{a}", "x")
                drained(pe, it, (s, f"back{a}", "x"), taken=[key])
                ps = take(pe, it, key)
                pe.matmul(ps[:, 0:TP], w(f"wo_{a}"), aT[s][:, :], start=True, stop=True).then_inc(full_of(key), 1)

            def glu(s, step, it):
                l, f = int(step[3]), "abc".index(step[4])
                key = (s, step, "x")
                if f == 0:
                    drained(pe, it, (s, f"scale{2 * l + 1}", "x"), taken=[key])
                ps = take(pe, it, key)
                for k, name in enumerate(("gate", "up")):
                    mm = pe.matmul(ps[0:FP, k * TP:(k + 1) * TP], w(f"{name}_{l}")[:, f * FP:(f + 1) * FP],
                                   hT[s][:, :], start=True, stop=True)
                mm.then_inc(full_of(key), 1)

            def down(s, l, it):
                key = (s, f"down{l}", "x")
                ps = take(pe, it, key)
                wd = w(f"down_{l}").rearrange("p (f o) -> p f o", f=FC)
                for f in range(FC):
                    drained(pe, it, (s, f"glu{l}" + "abc"[f], "x"), taken=[key])
                    mm = pe.matmul(ps[:, 0:TP], wd[0:FP, f, :], gl[s][:, f, :], start=(f == 0), stop=(f == FC - 1))
                mm.then_inc(full_of(key), 1)

            def stack(s, it):
                key = (s, "stack", "x")
                pe.wait_ge(stack_step[s], it * 8 + 8)
                ps = take(pe, it, key)
                for j, src in enumerate((stq, stk)):
                    for k in range(2):
                        mm = pe.transpose(ps[:, j * TP + k * HT:j * TP + (k + 1) * HT],
                                          src[s][:, k, :, :].rearrange("p h d -> p (h d)").bitcast(F32),
                                          ident[0:HT, 0:HT])
                mm.then_inc(full_of(key), 1)

            def route(s, it):
                key = (s, "route", "rows")
                drained(pe, it, (s, "scale6", "x"), taken=[key])
                pe.wait_ge(hm_ready[s], it + 1)
                ps = take(pe, it, key)
                for j, src in enumerate((xT, hT)):
                    for k in range(2):
                        mm = pe.transpose(ps[0:HT, (2 * j + k) * D:(2 * j + k + 1) * D], src[s][:, k * HT:(k + 1) * HT], ident)
                mm.then_inc(full_of(key), 1)
                key = (s, "route", "logits")
                ps = take(pe, it, key)
                for k in range(2):
                    mm = pe.matmul(ps[0:HT, k * EXPERTS:(k + 1) * EXPERTS], hT[s][:, k * HT:(k + 1) * HT], w("wr"),
                                   start=True, stop=True)
                mm.then_inc(full_of(key), 1)

            def ranks(s, it):
                key = (s, "slots", "x")
                pe.wait_ge(chosen_ready[s], it + 1)
                ps = take(pe, it, key)
                last = T - HT
                groups = [[(lowb, HT, 0)], [(lowb, last, 1), (onesb, HT, 0)], [(onesb, HT, 0), (onesb, last, 1)]]
                for j, group in enumerate(groups):
                    terms = [(m, rows, k, c) for m, rows, k in group for c in range(2)]
                    for i, (m, rows, k, c) in enumerate(terms):
                        mm = pe.matmul(ps[0:HT, j * EXPERTS:(j + 1) * EXPERTS], m[0:rows, :], onehb[s][0:rows, 2 * k + c, :],
                                       start=(i == 0), stop=(i == len(terms) - 1))
                mm.then_inc(full_of(key), 1)

            with pe.Fori(0, turns) as it:
                for s, step, a in order:
                    n = int("0" + "".join(c for c in step if c.isdigit()))
                    if step == "patch":
                        patch(s, it)
                    elif step.startswith("sum"):
                        sums(s, n, it)
                    elif step.startswith("scale"):
                        scales(s, n, it)
                    elif step.startswith("center"):
                        center(s, n, it)
                    elif step.startswith("qkv"):
                        qkv(s, n, it)
                    elif step.startswith("sel"):
                        select(s, step, it)
                    elif step.startswith("head"):
                        if n >= LAG:
                            head_scoresT(s, a, n - LAG, it)
                        if n < HEADS:
                            head_scores(s, a, n, it)
                        if n == 7:
                            head_values(s, a, 0, it)
                    elif step.startswith("values"):
                        head_values(s, n, 1, it)
                    elif step.startswith("turn"):
                        turn(s, n, it)
                    elif step.startswith("back"):
                        back(s, n, it)
                    elif step.startswith("proj"):
                        proj(s, n, it)
                    elif step.startswith("glu"):
                        glu(s, step, it)
                    elif step.startswith("down"):
                        down(s, n, it)
                    elif step == "stack":
                        stack(s, it)
                    elif step == "route":
                        route(s, it)
                    elif step == "slots":
                        ranks(s, it)

            pe.drain().then_inc(stage1_done, 1)
            pe.wait_ge(stage1_done, 4)
            turn_bank, hid_bank, y_bank = scores, scoresT, [heads, misc[0]]
            with pe.Fori(0, blocks // 2) as it:
                for k in range(2):
                    pe.wait_ge(gathered[k], it * 16 * BC + 16 * BC)
                    for c in range(BC):
                        mm = pe.transpose(turn_bank[k][:, c * D:(c + 1) * D], exr[k][:, c, :], ident)
                    mm.then_inc(turned, 1)
                for k in range(2):
                    pe.wait_ge(w_loaded[k], it * 16 + 16)
                    pe.wait_ge(tokens_ready, it * 2 + (k + 1))
                    for f in range(EC):
                        n = k * EC + f
                        pe.wait_ge(act_done, it * 2 * EC + (n + 1))
                        pe.matmul(hid_bank[n % 2][:, :], ew1[k][:, f, :], ex[k], start=True, stop=True
                                  ).then_inc(hid_full, 1)
                for k in range(2):
                    pe.wait_ge(y_ready, it * 2 + (k + 1))
                    for c in range(BC):
                        for f in range(EC):
                            if c == 0:
                                pe.wait_ge(act_done, it * 2 * EC + (k * EC + f + 3))
                            pe.matmul(y_bank[k][:, c * D:(c + 1) * D], hid[k][:, f, c * D:(c + 1) * D], ew2[k][:, f, :],
                                      start=(f == 0), stop=False)
                        mm = pe.matmul(y_bank[k][:, c * D:(c + 1) * D], ones1[:, :], eb2[k], start=False, stop=True)
                    mm.then_inc(y_full, 1)

        @block.vector
        def _(dve):
            dve.memset(minus_half[:, :], -0.5)
            dve.memset(ones1[:, :], 1.0)
            dve.memset(onesb[:, :], 1.0)
            for s in range(SLOTS):
                dve.memset(va[s][:, :, :, :], 0.0)
                dve.memset(stq[s][:, :, :, :].bitcast(F32), 0.0)
                dve.memset(stk[s][:, :, :, :].bitcast(F32), 0.0)
            dve.drain()
            for s in range(SLOTS):
                dve.memset(va[s][:, :, :, HD:HD + 1], 1.0)
                dve.memset(stq[s][:, :, :, 4:6].bitcast(F32), 1.0)
            dve.wait_ge(pack_loaded, 16)
            dve.tensor_copy(lowb[:, :], w("lower", HT))
            dve.tensor_copy(nxt[:, :], w("first", HT))
            dve.tensor_copy(identr[:, :], w("ident", RT)[:, 0:RT])
            for s in range(SLOTS):
                dve.tensor_copy(tokf[s][:, :], w("token", HT)[:, 2 * s:2 * s + 2])
            pos = w("pos")
            dve.tensor_scalar(pos[:, 1:TP], pos[:, 1:TP], w("conv_b"), None, ALU.add)
            dve.tensor_tensor(pos[:, 0:1], pos[:, 0:1], w("cls"), ALU.add)
            for l in range(2):
                dve.tensor_scalar(w(f"down_{l}"), w(f"down_{l}"), 0.5, None, ALU.mult)
            dve.wait_ge(sel_loaded, 16)
            dve.tensor_copy(selr[:, :, :].rearrange("p a n -> p (a n)"), ptw[0][:, 0:2 * SEL_COLS])
            dve.drain().then_inc(consts_ready, 1)
            for b in range(MB):
                dve.sem_inc(free[b], 1)
            dve.sem_inc(max_done, 2)
            dve.sem_inc(nxt_ready, 1)
            for s in range(SLOTS):
                dve.sem_inc(tok_ready[s], 1)
                dve.sem_inc(sends_done[s], 1)
            for k in range(2):
                dve.sem_inc(gather_free[k], 1)
                dve.sem_inc(out_stored[k], 16)
            dve.sem_inc(y_ready, 2)
            dve.sem_inc(credits, 1)

            def embed(s, it):
                key = (s, "patch", "x")
                ps = filled(dve, it, key)
                dve.tensor_tensor(xT[s][:, :], ps[:, 0:TP], w("pos"), ALU.add).then_inc(free_of(key), 1)

            def mean_square(s, n, it):
                key = (s, f"sum{n}", "x")
                ps = filled(dve, it, key)
                dve.tensor_scalar(ms[s][:, :], ps[0:HT, 0:2], EPS_LN if n >= 5 else EPS_RMS, None, ALU.add
                                  ).then_inc(free_of(key), 1)

            def normed(s, n, it):
                key = (s, f"scale{n}", "x")
                ps = filled(dve, it, key)
                src, dst = norm_src(s, n)[:, :], norm_dst(s, n)[:, :]
                if n in NORM_WEIGHT:
                    i = dve.scalar_tensor_tensor(out=dst, in0=src, scalar=w(NORM_WEIGHT[n]), in1=ps[:, 0:TP],
                                                 op0=ALU.mult, op1=ALU.mult)
                else:
                    i = dve.tensor_tensor(dst, src, ps[:, 0:TP], ALU.mult)
                i.then_inc(free_of(key), 1)
                if n == 7:
                    drained(dve, it, key)
                    dve.tensor_scalar(dst, dst, w("ln_b"), None, ALU.add).then_inc(hm_ready[s], 1)

            def centered(s, n, it):
                key = (s, f"center{n}", "x")
                ps = filled(dve, it, key)
                dve.tensor_copy((xT if n == 1 else hT)[s][:, :], ps[:, 0:TP]).then_inc(free_of(key), 1)

            def qk_low(s, l, it):
                key = (s, f"qkv{l}", "qk")
                ps = filled(dve, it, key)
                dve.wait_ge(hi_ready[s], it * 2 + (l + 1))
                dve.tensor_tensor(qk_lo[s][:, :, :], two(ps), qk_hi[s][:, :, :], ALU.subtract).then_inc(free_of(key), 1)

            def stacks(s, step, it):
                use, dst, tile, _ = sel_tiles(step[-1])[0]
                ps = filled(dve, it, (s, step, use))
                dve.tensor_copy(dst[s][:, tile:tile + 2, :], two(ps)).then_inc(free_of((s, step, use)), 1)

            def maxima(s, a, h, it):
                g = 8 * (SLOTS * a + s) + h
                dve.wait_ge(scores_full, it * HEADS_A_TURN + (g + 1))
                dve.tensor_reduce(nm[s][:, :, h], two(scores[g % 2], RT)[:, :, 0:T], AX.X, ALU.max, negate=True
                                  ).then_inc(max_done, 1)

            def divide(s, a, it):
                key = (s, f"turn{a}", "x")
                ps = filled(dve, it, key)
                r = ps[0:HT, :].rearrange("p (n c) -> p n c", c=32)
                dve.reciprocal(rc[s][:, :], r[:, :, HD]).then_inc(recip_ready[s], 1)
                dve.wait_ge(recip_ready[s], it * 3 + (a + 1))
                dve.tensor_tensor(ao[s][:, :, :], r[:, :, 0:HD], rc[s][:, :, None].to_broadcast([HT, 2 * HEADS, HD]),
                                  ALU.mult).then_inc(free_of(key), 1)

            def add(s, key, it, twice=False):
                ps = filled(dve, it, key)
                if twice:
                    i = dve.scalar_tensor_tensor(out=xT[s][:, :], in0=xT[s][:, :], scalar=2.0, in1=ps[:, 0:TP],
                                                 op0=ALU.mult, op1=ALU.add)
                else:
                    i = dve.tensor_tensor(xT[s][:, :], xT[s][:, :], ps[:, 0:TP], ALU.add)
                i.then_inc(free_of(key), 1)

            def gated(s, step, it):
                l, f = int(step[3]), "abc".index(step[4])
                key = (s, step, "x")
                n = FC * l + f + 1
                dve.wait_ge(th_ready[s], it * 2 * FC + n)
                ps = misc[where[key][0]]
                dve.scalar_tensor_tensor(out=gl[s][:, f, :], in0=th[s][:, f, :], scalar=1.0, in1=ps[0:FP, 0:TP],
                                         op0=ALU.add, op1=ALU.mult).then_inc(glu_half[s], 1)
                dve.wait_ge(glu_half[s], it * 2 * FC + n)
                dve.tensor_tensor(gl[s][:, f, :], gl[s][:, f, :], ps[0:FP, TP:2 * TP], ALU.mult
                                  ).then_inc(free_of(key), 1)

            def stack(s, it):
                key = (s, "qkv2", "qk")
                ps = filled(dve, it, key)
                qk = ps[0:HT, 0:4 * HEADS].rearrange("p (k n) -> p k n", k=2)
                q, k_ = qk[:, :, 0:HEADS], qk[:, :, HEADS:2 * HEADS]

                def twice(ap):
                    return ap[:, :, :, None].to_broadcast([HT, 2, HEADS, 2])

                q_hi = stq[s][:, :, :, 0]
                dve.tensor_copy(stq[s][:, :, :, 0:2], twice(q)).then_inc(stack_step[s], 1)
                dve.tensor_scalar(kf[s][:, 0, :, :], k_, 2.0, None, ALU.mult).then_inc(stack_step[s], 1)
                dve.wait_ge(stack_step[s], it * 8 + 2)
                for j in range(2):
                    i = dve.tensor_tensor(stq[s][:, :, :, 2 + j], q, q_hi, ALU.subtract)
                i.then_inc(free_of(key), 1)
                dve.tensor_copy(stk[s][:, :, :, 0:3:2], twice(kf[s][:, 0, :, :])).then_inc(stack_step[s], 1)
                dve.scalar_tensor_tensor(out=kf[s][:, 1, :, :], in0=kf[s][:, 0, :, :], scalar=-0.25,
                                         in1=kf[s][:, 0, :, :], op0=ALU.mult, op1=ALU.mult).then_inc(stack_step[s], 1)
                dve.wait_ge(stack_step[s], it * 8 + 4)
                for j in range(2):
                    i = dve.tensor_tensor(stk[s][:, :, :, 1 + 2 * j], kf[s][:, 0, :, :], stk[s][:, :, :, 0], ALU.subtract)
                i.then_inc(stack_step[s], 1)
                dve.tensor_copy(stk[s][:, :, :, 4], kf[s][:, 1, :, :]).then_inc(stack_step[s], 1)
                dve.wait_ge(stack_step[s], it * 8 + 6)
                dve.tensor_tensor(stk[s][:, :, :, 5], kf[s][:, 1, :, :], stk[s][:, :, :, 4], ALU.subtract
                                  ).then_inc(stack_step[s], 1)
                dve.drain().then_inc(stack_step[s], 1)

            def masks(s, it):
                drained(dve, it, (s, "stack", "x"))
                for h in range(4):
                    i = dve.tensor_scalar(km[s][:, h, :], k3[s][:, :], w("mask")[:, h:h + 1], None, ALU.mult)
                i.then_inc(masks_dve[s], 1)

            def choose(s, it):
                key = (s, "route", "logits")
                ps = filled(dve, it, key)
                dve.tensor_tensor(lg[s][:, :, :], ps[0:HT, 0:2 * EXPERTS].rearrange("p (k e) -> p k e", k=2),
                                  w("br", HT)[:, None, :].to_broadcast([HT, 2, EXPERTS]), ALU.add).then_inc(free_of(key), 1)
                b, nth = where[key]
                wait_apart(dve, free[b], it * uses[b] + (nth + 2))
                for k in range(2):
                    dve.max(top[s][:, k, :], lg[s][:, k, :]).then_inc(top_step[s], 1)
                dve.wait_ge(top_step[s], it * 5 + 2)
                dve.tensor_tensor(gd[s][:, :], top[s][:, :, 1], top[s][:, :, 0], ALU.subtract).then_inc(gd_ready[s], 1)
                for k in range(2):
                    dve.max_index(topi[s][:, k, :], top[s][:, k, :], lg[s][:, k, :]).then_inc(top_step[s], 1)
                dve.wait_ge(top_step[s], it * 5 + 4)
                dve.tensor_copy(chosen[s][:, :].rearrange("p (k c) -> p k c", k=2), topi[s][:, :, 0:2]).then_inc(top_step[s], 1)
                dve.wait_ge(top_step[s], it * 5 + 5)
                dve.tensor_tensor(oneh[s][:, :, :], w("iota", HT)[:, None, :].to_broadcast([HT, 4, EXPERTS]),
                                  chosen[s][:, :, None].to_broadcast([HT, 4, EXPERTS]), ALU.is_equal)
                dve.tensor_tensor(onehb[s][:, :, :], w("iota", HT)[:, None, :].to_broadcast([HT, 4, EXPERTS]),
                                  chosen[s][:, :, None].to_broadcast([HT, 4, EXPERTS]), ALU.is_equal).then_inc(chosen_ready[s], 1)
                dve.wait_ge(ge_ready[s], it + 1)
                dve.tensor_scalar(gs[s][:, :], ge[s][:, :], 1.0, None, ALU.add).then_inc(gate_step[s], 1)
                dve.wait_ge(gate_step[s], it * 2 + 1)
                dve.reciprocal(gr[s][:, :], gs[s][:, :]).then_inc(gate_step[s], 1)
                dve.wait_ge(gate_step[s], it * 2 + 2)
                dve.tensor_copy(gates[:, bass.ds((it * SLOTS + s) * 2, 2), 0], gr[s][:, :])
                dve.tensor_tensor(gates[:, bass.ds((it * SLOTS + s) * 2, 2), 1], ge[s][:, :], gr[s][:, :], ALU.mult)

            def place(s, it):
                key = (s, "slots", "x")
                ps = filled(dve, it, key)
                dve.tensor_copy(cnt3[s][:, :, :], ps[0:HT, 0:3 * EXPERTS].rearrange("p (k e) -> p k e", k=3)
                                ).then_inc(free_of(key), 1)
                drained(dve, it, key)
                dve.wait_ge(nxt_ready, it * SLOTS + (s + 1))
                dve.tensor_tensor(rank[s][:, :, :], cnt3[s][:, 0:2, :], nxt[:, None, :].to_broadcast([HT, 2, EXPERTS]), ALU.add
                                  ).then_inc(slot_step[s], 1)
                dve.wait_ge(slot_step[s], it * SLOT_STEPS + 1)
                dve.tensor_tensor(nxt[:, :], nxt[:, :], cnt3[s][:, 2, :], ALU.add).then_inc(nxt_ready, 1)
                for k in range(2):
                    i = dve.tensor_tensor(cand[s][:, 2 * k:2 * k + 2, :], oneh[s][:, 2 * k:2 * k + 2, :],
                                          rank[s][:, k:k + 1, :].to_broadcast([HT, 2, EXPERTS]), ALU.mult)
                i.then_inc(slot_step[s], 1)
                dve.wait_ge(slot_step[s], it * SLOT_STEPS + 2)
                dve.tensor_reduce(slotf[s][:, :], cand[s][:, :, :], AX.X, ALU.add).then_inc(slot_step[s], 1)
                dve.wait_ge(slot_step[s], it * SLOT_STEPS + 3)
                dve.tensor_copy(slots[:, bass.ds((it * SLOTS + s) * 2, 2), :], slotf[s][:, :].rearrange("p (k c) -> p k c", k=2))
                dve.wait_ge(sends_done[s], it + 1)
                dve.tensor_copy(slotu[s][:, :], slotf[s][:, :])
                dve.wait_ge(tok_ready[s], it + 1)
                dve.tensor_copy(toku[s][:, :], tokf[s][:, :]).then_inc(slot_step[s], 1)
                dve.wait_ge(slot_step[s], it * SLOT_STEPS + 4)
                dve.tensor_scalar(tokf[s][:, :], tokf[s][:, :], float(SLOTS * T), None, ALU.add).then_inc(tok_ready[s], 1)

            with dve.Fori(0, turns) as it:
                for s, step, a in dve_order:
                    n = int("0" + "".join(c for c in step if c.isdigit()))
                    if step == "patch":
                        embed(s, it)
                    elif step.startswith("sum"):
                        mean_square(s, n, it)
                    elif step.startswith("scale"):
                        normed(s, n, it)
                    elif step.startswith("center"):
                        centered(s, n, it)
                    elif step.startswith("qkv"):
                        if n < 2:
                            qk_low(s, n, it)
                        else:
                            stack(s, it)
                    elif step.startswith("sel"):
                        stacks(s, step, it)
                    elif step.startswith("head"):
                        if n < HEADS:
                            maxima(s, a, n, it)
                    elif step.startswith("turn"):
                        divide(s, n, it)
                    elif step.startswith("proj"):
                        add(s, (s, step, "x"), it, twice=(n == 2))
                    elif step.startswith("glu"):
                        gated(s, step, it)
                    elif step.startswith("down"):
                        add(s, (s, step, "x"), it)
                    elif step == "masks":
                        masks(s, it)
                    elif step == "route":
                        choose(s, it)
                    elif step == "slots":
                        place(s, it)

            dve.drain().then_inc(stage1_done, 1)
            dve.wait_ge(nxt_ready, images + 1)
            at = [0]

            def step(ins):
                ins.then_inc(map_step, 1)
                at[0] += 1
                dve.wait_ge(map_step, at[0])

            first, fill, number = w("first", HT), w("fill", HT), w("block", 1)
            step(dve.tensor_tensor(held[:, :], nxt[:, :], first, ALU.subtract))
            step(dve.tensor_tensor(fills[:, :, :], held[:, :, None].to_broadcast([HT, EXPERTS, region_blocks]),
                                   fill[:, None, :].to_broadcast([HT, EXPERTS, region_blocks]), ALU.is_gt))
            step(dve.tensor_reduce(nblk[:, :], fills[:, :, :], AX.X, ALU.add))
            step(dve.tensor_scalar(jump[:, :], nblk[:, :], -float(BLK), float(region), ALU.mult, ALU.add))
            step(dve.memset(cum[:, 0:1], 0.0))
            for e in range(EXPERTS):
                step(dve.tensor_tensor(cum[:, e + 1:e + 2], cum[:, e:e + 1], nblk[0:1, e:e + 1], ALU.add))
            step(dve.tensor_tensor(past[:, :, :], number[:, :, None].to_broadcast([1, blocks, EXPERTS]),
                                   cum[:, None, 1:EXPERTS + 1].to_broadcast([1, blocks, EXPERTS]), ALU.is_ge))
            step(dve.tensor_reduce(of_expert[:, :], past[:, :, :], AX.X, ALU.add))
            step(dve.tensor_scalar(work[:, 0, :], of_expert[:, :], float(EXPERTS - 1), None, ALU.min))
            step(dve.tensor_tensor(jumped[:, :, :], past[:, :, :], jump[0:1, None, :].to_broadcast([1, blocks, EXPERTS]), ALU.mult))
            step(dve.tensor_reduce(of_row[:, :], jumped[:, :, :], AX.X, ALU.add))
            step(dve.scalar_tensor_tensor(out=work[:, 1, :], in0=number, scalar=float(BLK), in1=of_row[:, :],
                                          op0=ALU.mult, op1=ALU.add))
            assert at[0] == MAP_STEPS
            rows_of = slots[:, :, :].rearrange("p n c -> p (n c)")
            for e in range(1, EXPERTS):
                step(dve.tensor_scalar(less[:, :], rows_of, float(e * region), jump[:, e - 1:e], ALU.is_ge, ALU.mult))
                step(dve.tensor_tensor(moved[:, :], (rows_of if e == 1 else moved[:, :]), less[:, :], ALU.subtract))

            with dve.Fori(0, blocks // 2) as it:
                for k in range(2):
                    dve.wait_ge(turned, it * 2 + (k + 3))
                    dve.tensor_copy(ex[k], scores[k][:, :]).then_inc(tokens_ready, 1)
                for k in range(2):
                    dve.wait_ge(y_full, it * 2 + (k + 3))
                    dve.wait_ge(y_stored[k], it * 16 + 16)
                    dve.tensor_copy(ey[k], [heads, misc[0]][k][:, :].rearrange("p (c n) -> p c n", c=BC)).then_inc(y_ready, 1)

            with dve.Fori(0, images) as it:
                for k in range(2):
                    rows = T - HT if k else HT
                    r = slice(0, rows)
                    m = mix[k]
                    dve.wait_ge(hr_loaded[k], it * 16 + 16)
                    dve.tensor_scalar(m[:, 0, :], hr[k], 2.0, None, ALU.mult).then_inc(mix_step[k], 1)
                    dve.wait_ge(rows_got[k], it * 32 + 32)
                    dve.wait_ge(mix_step[k], it * 5 + 1)
                    dve.scalar_tensor_tensor(out=m[r, 1, :], in0=gy[k][r, 0, :], scalar=gg[k][r, 0:1], in1=m[r, 0, :],
                                             op0=ALU.mult, op1=ALU.add).then_inc(mix_step[k], 1)
                    dve.wait_ge(mix_step[k], it * 5 + 2)
                    dve.scalar_tensor_tensor(out=m[r, 2, :], in0=gy[k][r, 1, :], scalar=gg[k][r, 1:2], in1=m[r, 1, :],
                                             op0=ALU.mult, op1=ALU.add).then_inc(gather_free[k], 1)
                    dve.wait_ge(gather_free[k], it + 2)
                    dve.bn_stats(bn6[k][r, :], m[r, 2, :]).then_inc(mix_step[k], 1)
                    wait_apart(dve, mix_step[k], it * 5 + 3)
                    dve.bn_aggr(bn2[k][r, :], bn6[k][r, :]).then_inc(mix_step[k], 1)
                    dve.wait_ge(mix_step[k], it * 5 + 4)
                    dve.tensor_scalar(bn2[k][r, 1:2], bn2[k][r, 1:2], EPS_LN, None, ALU.add).then_inc(var_ready[k], 1)
                    dve.wait_ge(sd_ready[k], it + 1)
                    dve.reciprocal(rs[k][r, :], sd[k][r, :]).then_inc(mix_step[k], 1)
                    dve.wait_ge(mix_step[k], it * 5 + 5)
                    dve.wait_ge(out_stored[k], it * 16 + 16)
                    dve.tensor_scalar(fin[k][r, :], m[r, 2, :], bn2[k][r, 0:1], rs[k][r, :], ALU.subtract, ALU.mult
                                      ).then_inc(fin_ready[k], 1)


MAP_STEPS = 4 + EXPERTS + 7
SLOT_STEPS = 4


def layouts(images, x, L0_tok_conv_w, L0_tok_conv_b, L0_tok_cls_token, L0_tok_pos_emb, L0_tok_ln_f,
            L0_attn_Wq, L0_attn_Wk, L0_attn_Wv, L0_attn_Wm, L0_ffn_ln_g, L0_ffn_ln_b, L0_ffn_w_r,
            L0_ffn_b_r, L0_ffn_W1, L0_ffn_b1, L0_ffn_W2, L0_ffn_b2, **rest):
    import numpy as np

    cols, n = pack_layout(images)
    blocks, region_blocks, region, all_slots = sizes(images)
    pack = np.zeros((128, n), np.float32)

    def put(name, a, col=0):
        at = cols[name][0] + col
        pack[0:a.shape[0], at:at + a.shape[1]] = a

    put("conv", np.asarray(L0_tok_conv_w).reshape(D, PK, 128).transpose(2, 1, 0).reshape(128, PK * D))
    pos = np.asarray(L0_tok_pos_emb)[0].T
    put("pos", pos)
    put("pos", pos[:, T - 1:T], T)
    put("cls", np.asarray(L0_tok_cls_token).reshape(D, 1))
    put("conv_b", np.asarray(L0_tok_conv_b).reshape(D, 1))
    for l in range(2):
        r = {k: np.asarray(rest[f"L0_tok_{k}_{l}"]) for k in ("ln1", "qkv", "wo", "ln2", "gate", "up", "down")}
        put(f"ln1_{l}", r["ln1"].reshape(D, 1))
        put(f"ln2_{l}", r["ln2"].reshape(D, 1))
        put(f"qk_{l}", r["qkv"][0:2 * D].T)
        put(f"v_{l}", r["qkv"][2 * D:].T)
        put(f"wo_{l}", r["wo"].T)
        put(f"gate_{l}", r["gate"].T)
        put(f"up_{l}", r["up"].T)
        down = r["down"].T
        for f in range(FC):
            put(f"down_{l}", down[f * FP:(f + 1) * FP], f * D)
    put("ln_f", np.asarray(L0_tok_ln_f).reshape(D, 1))
    for h in range(HEADS):
        at = cols["qk_2"][0]
        pack[h * HD:(h + 1) * HD, at + h] = np.asarray(L0_attn_Wq)[h]
        pack[h * HD:(h + 1) * HD, at + HEADS + h] = np.asarray(L0_attn_Wk)[h]
        at = cols["v_2"][0]
        pack[h * HD:(h + 1) * HD, at + h * HD:at + (h + 1) * HD] = np.asarray(L0_attn_Wv)[h]
        pack[h * HD:(h + 1) * HD, cols["mask"][0] + h] = 1.0
    put("wo_2", np.asarray(L0_attn_Wm))
    put("ln_g", np.asarray(L0_ffn_ln_g).reshape(D, 1))
    put("ln_b", np.asarray(L0_ffn_ln_b).reshape(D, 1))
    put("wr", np.asarray(L0_ffn_w_r).T)
    put("br", np.broadcast_to(np.asarray(L0_ffn_b_r), (128, EXPERTS)))

    put("center", (np.eye(D) - 1.0 / D).astype(np.float32))
    put("ident", np.eye(D, dtype=np.float32))
    put("lower", np.triu(np.ones((HT, HT), np.float32), 1))
    put("iota", np.broadcast_to(np.arange(EXPERTS, dtype=np.float32), (128, EXPERTS)))
    put("first", np.broadcast_to(np.arange(EXPERTS, dtype=np.float32) * region, (128, EXPERTS)))
    t = np.arange(HT, dtype=np.float32)[:, None]
    put("token", np.concatenate([t + s * T + k * HT for s in range(SLOTS) for k in range(2)], 1))
    put("inv", np.full((128, 1), 1.0 / D, np.float32))
    put("fill", np.broadcast_to(np.arange(region_blocks, dtype=np.float32) * BLK, (128, region_blocks)))
    put("block", np.arange(blocks, dtype=np.float32)[None, :])

    sel = np.zeros((128, 2, 4 + HEADS, 128), np.float32)
    for h in range(HEADS):
        for d in range(HD):
            row = 64 * (h % 2) + d
            for group, (q_part, k_part) in enumerate(((0, 0), (0, 1), (1, 0), (1, 1))):
                sel[h * HD + d, q_part, h // 2, row + 16 * group] = 1.0
                sel[h * HD + d, k_part, 4 + h, row + 16 * group] = 1.0

    pixels = np.asarray(x)[0:images].reshape(images, 3, 14, 16, 14, 16).transpose(0, 1, 3, 5, 2, 4)
    pixels = pixels.reshape(images, PK, 128, T - 1).transpose(0, 2, 1, 3)
    img = np.zeros((images, 128, PK, TP), np.float32)
    img[:, :, :, 1:T] = pixels
    img[:, :, :, T] = pixels[:, :, :, T - 2]

    experts = np.zeros((EXPERTS, 128, EXPERT_COLS), np.float32)
    experts[:, :, 0:EH] = np.asarray(L0_ffn_W1)
    experts[:, :, EH:EH + EC * D] = np.asarray(L0_ffn_W2).reshape(EXPERTS, EC, 128, D).transpose(0, 2, 1, 3).reshape(EXPERTS, 128, EC * D)
    experts[:, :, EH + EC * D:EH + EC * D + EC] = np.asarray(L0_ffn_b1).reshape(EXPERTS, EC, 128).transpose(0, 2, 1)
    experts[:, 0, EH + EC * D + EC:] = np.asarray(L0_ffn_b2)
    return {"img": img, "pack": pack, "sel": sel.reshape(128, 2 * SEL_COLS), "experts": experts}


def kernel(**inputs):
    import numpy as _np
    import concourse.bacc as _bacc
    from concourse import mybir as _mybir
    from concourse.bass_utils import run_bass_kernel_spmd as _run

    images = inputs["x"].shape[0]
    arrays = layouts(images, **inputs)
    nc = _bacc.Bacc("TRN2", target_bir_lowering=False, num_devices=1)
    args = [nc.dram_tensor(f"in_{name}", a.shape, _mybir.dt.float32, kind="ExternalInput").ap()
            for name, a in arrays.items()]
    out = nc.dram_tensor("out_rows", (images * T, D), _mybir.dt.float32, kind="ExternalOutput").ap()
    vit_moe_kernel(nc, *args, out)
    r = _run(nc, [{f"in_{name}": a for name, a in arrays.items()}], core_ids=[0])
    return r.results[0]["out_rows"].reshape(images, T, D)
```

```python
from contextlib import ExitStack

import concourse.bass as bass
from concourse import mybir

F32 = mybir.dt.float32
F32R = mybir.dt.float32r
BF16 = mybir.dt.bfloat16
U32 = mybir.dt.uint32
ALU = mybir.AluOpType
ACT = mybir.ActivationFunctionType
AX = mybir.AxisListType

D = 128
HEADS = 8
HD = D // HEADS
T = 197
TP = 198
HT = TP // 2
RT = 100
PK = 6
FF = 345
FC = 3
FP = FF // FC
SLOTS = 4
SHARED_BANKS = 3
SENDS = 4
NORMS = 8
EXPERTS = 8
EH = 512
EC = EH // 128
BLK = 512
BC = BLK // 128
EPS_RMS = 1e-6
EPS_LN = 1e-5


def sizes(images):
    tokens = images * T
    blocks = (2 * tokens + EXPERTS * (BLK - 1)) // BLK
    blocks += blocks % 2
    region_blocks = (tokens + BLK - 1) // BLK
    region = region_blocks * BLK
    return blocks, region_blocks, region, EXPERTS * region + blocks * BLK


def pack_layout(images):
    blocks, region_blocks, _, _ = sizes(images)
    cols = [("conv", PK * D), ("pos", TP), ("cls", 1), ("conv_b", 1)]
    for l in range(2):
        cols += [(f"ln1_{l}", 1), (f"ln2_{l}", 1), (f"qk_{l}", 2 * D), (f"v_{l}", D), (f"wo_{l}", D),
                 (f"gate_{l}", FF), (f"up_{l}", FF), (f"down_{l}", FC * D)]
    cols += [("ln_f", 1), ("qk_2", 2 * HEADS), ("v_2", D), ("wo_2", D), ("ln_g", 1), ("ln_b", 1),
             ("wr", EXPERTS), ("br", EXPERTS), ("center", D), ("ident", D), ("mask", HEADS),
             ("lower", HT), ("iota", EXPERTS), ("first", EXPERTS), ("token", 2 * SLOTS), ("inv", 1),
             ("fill", region_blocks), ("block", blocks)]
    at, out = 0, {}
    for name, n in cols:
        out[name] = (at, n)
        at += n
    return out, at


SEL_COLS = 4 * D + HEADS * D
E1 = EH + EC
E2 = EC * D + D
EXPERT_COLS = E1 + E2

CHAINS = [
    ["patch", "sum0", "scale0", "qkv0", "sel0a", "sel0b", "sel0c"],
    ["values0", "turn0", "back0", "proj0", "sum1", "scale1", "glu0a", "glu0b", "glu0c", "down0", "sum2", "scale2", "qkv1",
     "sel1a", "sel1b", "sel1c"],
    ["values1", "turn1", "back1", "proj1", "sum3", "scale3", "glu1a", "glu1b", "glu1c", "down1", "sum4", "scale4", "center0",
     "sum5", "scale5", "qkv2", "stack", "masks"],
    ["values2", "turn2", "back2", "proj2", "center1", "sum6", "scale6", "center2", "sum7", "scale7", "route",
     "slots"],
]
LAG = 2
HEAD_STEPS = [f"head{i}" for i in range(HEADS + LAG)]


STEP_COST = {
    "patch": (986, 664, 500), "sum": (250, 1380, 288), "scale": (368, 936, 660), "center": (374, 1048, 905),
    "qkv": (1513, 1667, 900), "sel": (571, 50, 653), "stack": (298, 2000, 700), "masks": (0, 4, 0),
    "values": (800, 709, 0), "turn": (356, 1116, 1379), "back": (207, 761, 827), "proj": (222, 701, 897),
    "glu": (680, 0, 1000), "gluc": (782, 1306, 1000), "down": (1000, 1962, 488), "route": (1180, 2697, 696),
    "slots": (200, 156, 376), "head": (600, 49, 0), "head0": (65, 0, 0), "head1": (170, 0, 50),
    "head7": (1500, 0, 50),
}
STACKS, MASKED, SQUARE = 2069, 2650, 277
MAXIMA, EXPONENTIALS, COPY = 204, 1655, 1443


def cost_of(step):
    for kind in (step, step.translate({ord(c): None for c in "0123456789"}), step.rstrip("0123456789abc")):
        if kind in STEP_COST:
            return STEP_COST[kind]


WINDOWS = 3 * SLOTS
FIRST, LOOP, LAST = range(3)
DVE_LATER = {"masks": 600, "qkv": 500, "glu": 350, "turn": 150, "center": 150, "sum": -150}
ACT_LATER = {"masks": 300, "center": 150, "values": -150, "sum": -300, "turn": 0, "glu": 0, "scale": -150, "qkv": -400}
FIRST_CHAIN = 1.0


def due_of_steps():
    start = FIRST_CHAIN
    due = {}

    def spread(s, steps, first, last, a=None):
        n = len(steps)
        due.update({(s, x, a): s + first + (i + 0.5) / n * (last - first) for i, x in enumerate(steps)})

    for s in range(SLOTS):
        spread(s, CHAINS[0], 0, start)
        for a in range(3):
            w = SLOTS * a + start
            spread(s, HEAD_STEPS, w, w + 1, a)
            spread(s, CHAINS[a + 1], w + 1, w + SLOTS - (start if a == 2 else 0))
    return due


def plan_turn():
    due = due_of_steps()
    late = {x for x, t in due.items() if t >= WINDOWS}
    turns = 3
    streams = [sorted((due[x] + WINDOWS * turn, x, turn) for x in due for turn in range(turns)
                      if x[0] == s and x[2] is None) for s in range(SLOTS)]
    streams.append(sorted((due[x] + WINDOWS * turn, x, turn) for x in due for turn in range(turns) if x[2] is not None))
    order, end = [], {}
    now, ready, drained, used = 0, [0] * len(streams), [0] * SHARED_BANKS, 0
    left = [len(due) - len(late) + (len(late) if turn else 0) for turn in range(turns)]

    def earliest(x, turn):
        s, step, a = x
        period = turn + (x in late)
        if period >= turns or period and left[period - 1]:
            return None
        needs = []

        def need(s, step, a, later, turn=turn):
            if turn >= 0:
                needs.append(((s, step, a, turn), later))

        def need_window(w, step, later):
            before = w // WINDOWS
            w %= WINDOWS
            if step == "values":
                need(w % SLOTS, f"values{w // SLOTS}", None, later, turn + before)
            else:
                need(w % SLOTS, step, w // SLOTS, later, turn + before)

        if step == "head0":
            need(s, ["sel0c", "sel1c", "masks"][a], None, MASKED if a == 2 else STACKS)
        if step.startswith("head") and int(step[4:]) >= LAG:
            need(s, f"head{int(step[4:]) - 2}", a, MAXIMA)
        if step == "head7":
            need_window(SLOTS * a + s - 1, "values", COPY)
        if step.startswith("values"):
            need(s, "head9", int(step[6:]), EXPONENTIALS)
        if step in ("sel0a", "sel1a", "stack"):
            need_window(SLOTS * ["sel0a", "sel1a", "stack"].index(step) + s - 2, "head9", 0)
        if any(x not in end for x, _ in needs):
            return None
        return max([end[x] + later for x, later in needs], default=0)

    while left[-1]:
        best = None
        for n, stream in enumerate(streams):
            if stream:
                at = earliest(*stream[0][1:])
                if at is not None:
                    at = max([at, now, ready[n]] +
                             [drained[(used + k) % SHARED_BANKS] for k in range(len(uses_of(stream[0][1][1])))])
                    key = ((at - now) // 60, stream[0][0])
                    if best is None or key < best[0]:
                        best = key, n, at
        _, n, at = best
        _, x, turn = streams[n].pop(0)
        time, then, drain = cost_of(x[1])
        now = at + time
        ready[n] = now + then
        for _ in uses_of(x[1]):
            drained[used % SHARED_BANKS] = now + drain
            used += 1
        end[(*x, turn)] = now
        left[turn + (x in late)] -= 1
        if turn + (x in late) == turns - 1:
            order.append((x, turn))

    on_act, on_dve = [], []
    for (s, step, a), turn in order:
        kind = step.rstrip("0123456789abc")
        t = end[(s, step, a, turn)]
        if kind == "sum":
            on_act.append((end[(s, NORM_SOURCE[int(step[3:])], None, turn)] + SQUARE, (s, step, a)))
        else:
            on_act.append((t + ACT_LATER.get(kind, 0), (s, step, a)))
        on_dve.append((t + DVE_LATER.get(kind, 0), (s, step, a)))

    on_pool = [(end[(*x, turn)] + 350, x) for x, turn in order if x[1].startswith("sum")]
    taken = sorted(t for t, _ in on_pool)
    for x, turn in order:
        if x[1] == "slots":
            t = end[(*x, turn)] + 700
            for piece in range(SENDS):
                for other in taken:
                    if t - 400 < other < t + 1100:
                        t = other + 400
                on_pool.append((t, (x[0], f"send{piece}", None)))
                if x in late:
                    late.add((x[0], f"send{piece}", None))
                t += 1100
    by_time = lambda x: [step for _, step in sorted(x, key=lambda y: y[0])]
    return [x for x, _ in order], by_time(on_act), by_time(on_dve), by_time(on_pool), late


def uses_of(step):
    kind = step.rstrip("0123456789abc")
    return {"qkv": ["qk", "v"], "sel": ["p0", "p1"], "values": [],
            "route": ["rows", "logits"], "head": [], "masks": []}.get(kind, ["x"])


class Ranks:

    def __init__(self):
        self.keys = []

    def add(self, key, is_late):
        self.keys.append((key, is_late))

    def of(self, key):
        i = [k for k, _ in self.keys].index(key)
        is_late = self.keys[i][1]
        late_before = sum(x for _, x in self.keys[:i])
        return i - late_before, i, late_before, is_late, sum(x for _, x in self.keys[i:])

    def totals(self):
        return sum(not x for _, x in self.keys), len(self.keys)


class At:

    def __init__(self, part, is_late, turn, loop, turns):
        self.part, self.is_late, self.turn, self.loop, self.turns = part, is_late, turn, loop, turns

    def before(self, ranks, key, more=0, scale=1):
        first, body, last, key_late, late_behind = ranks.of(key)
        in_first, per_turn = ranks.totals()
        turns_ago = self.is_late - key_late
        if self.part == FIRST:
            assert turns_ago == 0
            return first * scale + more
        assert turns_ago == 0 or turns_ago == 1 and late_behind == 0
        if self.part == LOOP:
            return self.loop * (per_turn * scale) + ((in_first + body - turns_ago * per_turn) * scale + more)
        n = in_first + (self.turns - 1 - turns_ago) * per_turn + (body if turns_ago else last)
        return n * scale + more


def plan_banks(order, late):
    where, ranks, n = {}, [Ranks() for _ in range(SHARED_BANKS)], 0
    attentions = Ranks()
    for x in order:
        s, step, a = x
        for use in uses_of(step):
            where[(s, step, use)] = n % SHARED_BANKS
            ranks[n % SHARED_BANKS].add((s, step, use), x in late)
            n += 1
        if step == "head0":
            attentions.add((s, a), x in late)
    return where, ranks, attentions


NORM_SOURCE = ["patch", "proj0", "down0", "proj1", "down1", "center0", "center1", "center2"]
NORM_WEIGHT = {0: "ln1_0", 1: "ln2_0", 2: "ln1_1", 3: "ln2_1", 4: "ln_f", 7: "ln_g"}
CENTER_SOURCE = ["scale4", "proj2", "scale6"]
PARTS = ((0, 0), (0, 1), (1, 0))
SCALE = float(HD) ** -0.5


def vit_moe_kernel(nc, img, pack, sel, experts, out):
    images = img.shape[0]
    turns = images // SLOTS
    blocks, region_blocks, region, all_slots = sizes(images)
    tiles = 2 * images
    cols, pack_cols = pack_layout(images)
    order, act_order, dve_order, pool_order, late = plan_turn()
    where, ranks, attentions = plan_banks(order, late)

    def steps(which, part, loop=None, later=None):
        for s, step, a in which:
            is_late = (s, step, a) in late
            if (part == FIRST and is_late) or (part == LAST and not is_late):
                continue
            turn = {FIRST: 0, LOOP: loop if is_late else later, LAST: turns - 1}[part]
            n = int("0" + "".join(c for c in step if c.isdigit()))
            yield s, step, a, n, At(part, is_late, turn, loop, turns)

    stream_rows = nc.dram_tensor("stream_rows", [HT, 2 * images, D], F32, kind="Internal").ap()
    token_rows = nc.dram_tensor("token_rows", [images * T, D], F32, kind="Internal").ap()
    slot_token = nc.dram_tensor("slot_token", [all_slots, 1], U32, kind="Internal").ap()
    slot_rows = nc.dram_tensor("slot_rows", [blocks * BLK, D], F32, kind="Internal").ap()

    with ExitStack() as ctx:
        def sb(name, shape, dt=F32):
            return ctx.enter_context(nc.sbuf_tensor(name, shape, dt))

        def pair(name, shape, dt=F32):
            return [sb(f"{name}{s}", shape, dt) for s in range(2)]

        def each(name, shape, dt=F32):
            return [sb(f"{name}{s}", shape, dt) for s in range(SLOTS)]

        def shared(name, shape, dt=F32):
            return pair(name, shape, dt) * (SLOTS // 2)

        def bank(name):
            return ctx.enter_context(nc.psum_tensor(name, [128, 512], F32))

        def sem(name):
            return ctx.enter_context(nc.semaphore(name))

        def sems(name, n=2):
            return [sem(f"{name}{s}") for s in range(n)]

        wp = sb("wp", [128, pack_cols])

        def w(name, rows=128):
            at, n = cols[name]
            return wp[0:rows, at:at + n]

        selr = sb("selr", [128, 2, SEL_COLS], F32R)
        identr = sb("identr", [RT, RT], F32R)
        lowb = sb("lowb", [HT, HT], BF16)
        onesb = sb("onesb", [HT, HT], BF16)
        minus_half = sb("minus_half", [HT, 2])

        imgs = shared("imgs", [128, PK, TP])
        xT = each("xT", [128, TP])
        hT = each("hT", [128, TP])
        sq = each("sq", [128, TP])
        ms = each("ms", [HT, 2])
        rn = each("rn", [HT, 2])
        qk_hi = each("qk_hi", [128, 2, TP], F32R)
        qk_lo = each("qk_lo", [128, 2, TP], F32R)
        qs = shared("qs", [128, 4, TP], F32R)
        km = shared("km", [128, HEADS, TP], F32R)
        va = each("va", [HT, 2, HEADS, 32])
        nm = each("nm", [RT, 2, HEADS], F32R)
        ptw = shared("ptw", [128, HEADS * 2 * TP])
        pt = [x[0:HT, :].rearrange("p (h k t) -> p h k t", h=HEADS, k=2) for x in ptw]
        ot = each("ot", [128, 2, TP])
        rc = each("rc", [HT, 2 * HEADS])
        ao = each("ao", [HT, 2 * HEADS, HD])
        aT = each("aT", [128, TP])
        th = each("th", [FP, FC, TP])
        gl = each("gl", [FP, FC, TP])
        stq = each("stq", [HT, 2, HEADS, HD], F32R)
        stk = each("stk", [HT, 2, HEADS, HD], F32R)
        kf = each("kf", [HT, 2, 2, HEADS])
        k3 = each("k3", [128, TP])
        srows = each("srows", [HT, 2, D])
        hmr = each("hmr", [HT, 2, D])
        lg = each("lg", [HT, 2, EXPERTS])
        top = each("top", [HT, 2, 8])
        topi = each("topi", [HT, 2, 8], U32)
        chosen = each("chosen", [HT, 4])
        gd = each("gd", [HT, 2])
        ge = each("ge", [HT, 2])
        gs = each("gs", [HT, 2])
        gr = each("gr", [HT, 2])
        oneh = each("oneh", [HT, 4, EXPERTS])
        onehb = each("onehb", [HT, 4, EXPERTS], BF16)
        cnt3 = each("cnt3", [HT, 3, EXPERTS])
        rank = each("rank", [HT, 2, EXPERTS])
        cand = each("cand", [HT, 4, EXPERTS])
        slotf = each("slotf", [HT, 4])
        slotu = each("slotu", [HT, 4], U32)
        tokf = each("tokf", [HT, 2])
        toku = each("toku", [HT, 2], U32)

        gates = sb("gates", [HT, tiles, 2])
        slots = sb("slots", [HT, tiles, 2])
        nxt = sb("nxt", [HT, EXPERTS])
        zeros = sb("zeros", [128, all_slots // 128], U32)

        hid = [x[:, 0:EC * BLK].rearrange("p (f n) -> p f n", f=EC) for x in ptw[0:2]]
        ex_parts = [[x[:, :, :].rearrange("p a b -> p (a b)")[:, 0:BLK] for x in y[0:2]] for y in (qs, km)]
        ey = [x[:, (EC + 1) * BLK:(EC + 2) * BLK].rearrange("p (c n) -> p c n", c=BC) for x in ptw[0:2]]
        exr = [x[:, :, :].rearrange("p a b -> p (a b)")[:, 0:BC * D].rearrange("p (c n) -> p c n", c=BC)
               for x in imgs[0:2]]
        ew = [wp[:, k * EXPERT_COLS:(k + 1) * EXPERT_COLS] for k in range(2)]
        assert 2 * EXPERT_COLS <= cols["ln_f"][0]
        ew1 = [x[:, 0:EH] for x in ew]
        ew1_parts = [[x[:, :] for x in pair(name, [128, EH], F32R)] for name in ("ew1_hi", "ew1_lo")]
        eb1 = [x[:, EH:E1] for x in ew]
        ew2 = [x[:, E1:E1 + EC * D].rearrange("p (f n) -> p f n", f=EC) for x in ew]
        eb2 = [x[:, E1 + EC * D:EXPERT_COLS] for x in ew]
        eidx = pair("eidx", [128, BC], U32)
        enow = pair("enow", [128, BC], U32)
        held = sb("held", [HT, EXPERTS])
        fills = sb("fills", [HT, EXPERTS, region_blocks])
        nblk = sb("nblk", [HT, EXPERTS])
        cum = sb("cum", [1, EXPERTS + 1])
        jump = sb("jump", [HT, EXPERTS])
        less = sb("less", [HT, 2 * tiles])
        moved = sb("moved", [HT, 2 * tiles])
        past = sb("past", [1, blocks, EXPERTS])
        jumped = sb("jumped", [1, blocks, EXPERTS])
        of_expert = sb("of_expert", [1, blocks])
        of_row = sb("of_row", [1, blocks])
        work = sb("work", [1, 2, blocks + 3], U32)
        halves = 2 * images
        assert halves <= 128
        where_rows = sb("where_rows", [halves, HT + 1, 2], U32)
        turned_gates = sb("turned_gates", [halves, HT + 1, 2])
        by_choice = sb("by_choice", [HT, 4, halves])
        gidx = pair("gidx", [halves, 2, 2], U32)
        gg = pair("gg", [halves, 2, 2])
        th_rows = [ptw[0][:, k * 3 * D:(k + 1) * 3 * D] for k in range(4)]
        gl_rows = [ptw[1][:, k * 3 * D:(k + 1) * 3 * D] for k in range(4)]
        gy = [x[:, 0:2 * D].rearrange("p (a n) -> p a n", a=2) for x in th_rows]
        fin = [x[:, 2 * D:3 * D] for x in th_rows]
        mix = [x[:, 0:2 * D].rearrange("p (a n) -> p a n", a=2) for x in gl_rows]
        hr = [x[:, 2 * D:3 * D] for x in gl_rows]
        bn6 = each("bn6", [halves, 6])
        bn2 = each("bn2", [halves, 2])
        sd = each("sd", [halves, 1])
        rs = each("rs", [halves, 1])
        eps = sb("eps", [128, 1])

        scores = [bank(f"scores{k}") for k in range(2)]
        scoresT = [bank(f"scoresT{k}") for k in range(2)]
        heads = bank("heads")
        misc = [bank(f"misc{k}") for k in range(SHARED_BANKS)]

        def two(ps, rows=128, n=TP):
            return ps[0:rows, 0:2 * n].rearrange("p (a n) -> p a n", a=2)

        pack_loaded = sem("pack_loaded")
        sel_loaded = sem("sel_loaded")
        consts_ready = sem("consts_ready")
        credits = sem("credits")
        zeros_ready = sem("zeros_ready")
        table_cleared = sem("table_cleared")
        img_loaded = sems("img_loaded")
        full = sems("bank_full", SHARED_BANKS)
        free = sems("bank_drained", SHARED_BANKS)
        scores_full = sem("scores_full")
        max_done = sem("max_done")
        scoresT_full = sem("scoresT_full")
        exp_done = sem("exp_done")
        heads_full = sem("heads_full")
        heads_copied = sem("heads_copied")
        sq_ready = sems("sq_ready", SLOTS)
        rn_ready = sems("rn_ready", SLOTS)
        hi_ready = sems("hi_ready", SLOTS)
        th_ready = sems("th_ready", SLOTS)
        glu_half = sems("glu_half", SLOTS)
        recip_ready = sems("recip_ready", SLOTS)
        stack_step = sems("stack_step", SLOTS)
        masks_dve = sems("masks_dve", SLOTS)
        masks_act = sems("masks_act", SLOTS)
        hm_ready = sems("hm_ready", SLOTS)
        top_step = sems("top_step", SLOTS)
        gd_ready = sems("gd_ready", SLOTS)
        ge_ready = sems("ge_ready", SLOTS)
        chosen_ready = sems("chosen_ready", SLOTS)
        slot_step = sems("slot_step", SLOTS)
        nxt_ready = sem("nxt_ready")
        tok_ready = sems("tok_ready", SLOTS)
        rows_stored = sems("rows_stored", SLOTS)
        slots_sent = sems("slots_sent", SLOTS)
        sends_done = sems("sends_done", SLOTS)
        stage1_done = sem("stage1_done")
        map_step = sem("map_step")
        idx_loaded = sems("idx_loaded")
        now_ready = sem("now_ready")
        gathered = sems("gathered")
        w1_loaded = sems("w1_loaded")
        w2_loaded = sems("w2_loaded")
        turned = sem("turned")
        tokens_high = sem("tokens_high")
        tokens_ready = sem("tokens_ready")
        w1_high = sem("w1_high")
        w1_ready = sem("w1_ready")
        hid_full = sem("hid_full")
        act_done = sem("act_done")
        y_full = sem("y_full")
        y_ready = sem("y_ready")
        y_stored = sems("y_stored")
        idx_ready = sems("idx_ready")
        gates_ready = sems("gates_ready")
        choices_ready = sem("choices_ready")
        choices_turned = sem("choices_turned")
        hr_loaded = sems("hr_loaded")
        rows_got = sems("rows_got")
        mix_step = sems("mix_step")
        var_ready = sems("var_ready")
        sd_ready = sems("sd_ready")
        fin_ready = sems("fin_ready")
        out_stored = sems("out_stored")
        gather_free = sems("gather_free")

        passed = {eng.engine: sem(f"passed_{name}")
                  for name, eng in (("sp", nc.sync), ("pool", nc.gpsimd), ("dve", nc.vector))}

        def take(pe, at, key):
            b = where[key]
            pe.wait_ge(free[b], at.before(ranks[b], key, 1))
            return misc[b]

        def filled(eng, at, key):
            b = where[key]
            eng.wait_ge(full[b], at.before(ranks[b], key, 1))
            return misc[b]

        def drained(eng, at, *keys, taken=()):
            last = {}
            for key in keys:
                b = where[key]
                if b not in last or ranks[b].of(key)[1] > ranks[b].of(last[b])[1]:
                    last[b] = key
            for b, key in last.items():
                if b not in [where[key] for key in taken]:
                    eng.wait_ge(free[b], at.before(ranks[b], key, 2))

        def wait_apart(eng, semaphore, value):
            eng.wait_ge(semaphore, value)
            eng.sem_inc(passed[eng.engine], 1)

        def nth(pair, k, per_block, more=0):
            return (pair * (2 * per_block) if pair is not None else 0) + (k * per_block + more)

        def wait_block(eng, semaphore, pair, k, per_block, more=0):
            if pair is not None or nth(None, k, per_block, more) > 0:
                eng.wait_ge(semaphore, nth(pair, k, per_block, more))

        def same(pair, k, per_block, more=0):
            return (pair * per_block if pair is not None else 0) + ((k // 2 + 1) * per_block + more)

        def full_of(key):
            return full[where[key]]

        def free_of(key):
            return free[where[key]]

        def norm_src(s, n):
            return hT[s] if n in (5, 7) else xT[s]

        def norm_dst(s, n):
            return xT[s] if n in (4, 6) else hT[s]

        def sel_tiles(part):
            if part == "a":
                return [("p0", qs, 0, 0), ("p1", qs, 2, 2)]
            first = 0 if part == "b" else 4
            return [("p0", km, first, 4 + first), ("p1", km, first + 2, 6 + first)]

        turns3 = HT // 4
        full_group = [[(2 * g + k, halves) for k in range(2)] for g in range(2)]
        last_group = [[(0, halves), (1, halves)], [(2, images)]]
        assert HT == 4 * turns3 + 3

        turn_bank, hid_bank, y_bank = scores, scoresT + misc[1:3], [heads, misc[0]]

        block = ctx.enter_context(nc.Block())

        @block.sync
        def _(sp):
            sp.dma_start(wp[:, :], pack).then_inc(pack_loaded, 16)
            sp.dma_start(ptw[0][:, 0:2 * SEL_COLS], sel).then_inc(sel_loaded, 16)
            for s in range(2):
                sp.dma_start(imgs[s][:, :, :], img[s]).then_inc(img_loaded[s], 16)
            sp.wait_ge(zeros_ready, 1)
            sp.dma_start(slot_token.rearrange("(p n) o -> p (n o)", p=128), zeros[:, :]).then_inc(table_cleared, 16)

            def next_image(s, at):
                key = (s, "patch", "x")
                done = at.before(ranks[where[key]], key, 1)
                number = at.turn * SLOTS + (s + 2)
                if isinstance(number, int):
                    sp.wait_ge(full[where[key]], done)
                    src = img[number]
                else:
                    number = sp.snap(number)
                    wait_apart(sp, full[where[key]], sp.snap(done))
                    src = img[bass.ds(number, 1)].rearrange("a p k t -> (a p) k t")
                sp.dma_start(imgs[s][:, :, :], src).then_inc(img_loaded[s % 2], 16)

            def rows_out(s, at):
                key = (s, "route", "rows")
                done = at.before(ranks[where[key]], key, 2)
                number = at.turn * SLOTS + s
                if isinstance(number, int):
                    sp.wait_ge(free[where[key]], done)
                else:
                    number = sp.snap(number)
                    wait_apart(sp, free[where[key]], sp.snap(done))
                for k in range(2):
                    rows = T - HT if k else HT
                    sp.dma_start(token_rows[bass.ds(number * T + k * HT, rows), :], hmr[s][0:rows, k, :]
                                 ).then_inc(rows_stored[s], 16)
                sp.dma_start(stream_rows.rearrange("n (k i) d -> n k i d", k=2)[:, :, bass.ds(number, 1), :].rearrange("n k a d -> n k (a d)"),
                             srows[s][:, :, :]).then_inc(rows_stored[s], 16)

            def run(part, loop=None, later=None, loads=SLOTS):
                for s, step, a, n, at in steps(order, part, loop, later):
                    if step == "patch" and s < loads:
                        next_image(s, at)
                    if step == "route":
                        rows_out(s, at)

            run(FIRST)
            with sp.Fori(0, turns - 2) as loop:
                run(LOOP, loop, sp.snap(loop + 1))
            run(LOOP, turns - 2, turns - 1, loads=SLOTS - 2)
            run(LAST)

            sp.wait_ge(map_step, MAP_STEPS)
            sp.wait_ge(stage1_done, 4)

            def load_numbers(block, k):
                row = sp.value_load(work[0:1, 1, block], min_val=0, max_val=all_slots - BLK)
                sp.dma_start(eidx[k][:, :], slot_token[bass.ds(row, BLK), :].rearrange("(p c) o -> p (c o)", p=128)
                             ).then_inc(idx_loaded[k], 16)

            def load(k, e, first, cols, loaded):
                sp.dma_start(ew[k][:, first:first + cols],
                             experts[bass.ds(e, 1), :, first:first + cols].rearrange("a p n -> (a p) n")).then_inc(loaded, 16)

            def expert_of(block):
                return sp.value_load(work[0:1, 0, block], min_val=0, max_val=EXPERTS - 1)

            def store(k, pair):
                sp.dma_start(slot_rows[bass.ds((pair * 2 + k) * BLK, BLK), :].rearrange("(p c) n -> p c n", p=128), ey[k]
                             ).then_inc(y_stored[k], 16)

            for k in range(2):
                load_numbers(slice(k, k + 1), k)
            for k in range(2):
                e = expert_of(slice(k, k + 1))
                load(k, e, 0, E1, w1_loaded[k])
                load(k, e, E1, E2, w2_loaded[k])
            for k in range(2):
                sp.wait_ge(now_ready, k + 1)
                load_numbers(slice(k + 2, k + 3), k)
            sp.wait_ge(now_ready, 3)
            load_numbers(slice(4, 5), 0)
            sp.wait_ge(act_done, EC)
            load(0, expert_of(slice(2, 3)), 0, E1, w1_loaded[0])
            with sp.Fori(0, blocks // 2 - 1) as it:
                for k in range(2):
                    numbers_used = sp.snap(it * 2 + (k + 4))
                    row = sp.value_load(work[0:1, 1, bass.ds(it * 2 + (k + 5), 1)], min_val=0, max_val=all_slots - BLK)
                    wait_apart(sp, now_ready, numbers_used)
                    sp.dma_start(eidx[1 - k][:, :], slot_token[bass.ds(row, BLK), :].rearrange("(p c) o -> p (c o)", p=128)
                                 ).then_inc(idx_loaded[1 - k], 16)
                    e = expert_of(bass.ds(it * 2 + (k + 2), 1))
                    e_next = expert_of(bass.ds(it * 2 + (k + 3), 1))
                    chunks = sp.snap(it * (2 * EC) + (k + 2) * EC)
                    done = sp.snap(it * 2 + (k + 3))
                    wait_apart(sp, act_done, chunks)
                    load(1 - k, e_next, 0, E1, w1_loaded[1 - k])
                    wait_apart(sp, y_ready, done)
                    load(k, e, E1, E2, w2_loaded[k])
                    store(k, it)
            for k in range(2):
                sp.wait_ge(y_ready, blocks - 2 + k + 3)
                store(k, blocks // 2 - 1)

            out_tokens = out.rearrange("(i t) n -> i t n", t=T)

            def store_tiles(it, groups):
                for g in range(2):
                    for k, parts in groups[g]:
                        if isinstance(it, int):
                            token = it * 4 + k
                            sp.wait_ge(fin_ready[g], it * 2 + (k % 2 + 1))
                        else:
                            done = sp.snap(it * 2 + (k % 2 + 1))
                            token = sp.snap(it * 4 + k)
                            wait_apart(sp, fin_ready[g], done)
                        for half in range(parts // images):
                            sp.dma_start(out_tokens[:, bass.ds(token + half * HT, 1), :].rearrange("i a n -> i (a n)"),
                                         fin[k][half * images:(half + 1) * images, :]).then_inc(out_stored[g], 16)

            with sp.Fori(0, turns3) as it:
                store_tiles(it, full_group)
            store_tiles(turns3, last_group)
            sp.wait_ge(out_stored[0], 64 * turns3 + 64 + 64)
            sp.wait_ge(out_stored[1], 64 * turns3 + 64 + 16)

        @block.gpsimd
        def _(pool):
            pool.memset(zeros[:, :], 0).then_inc(zeros_ready, 1)
            pool.wait_ge(table_cleared, 16)
            pool.wait_ge(credits, 1)

            def inverse_root(s, n, at):
                drained(pool, at, (s, f"sum{n}", "x"))
                pool.tensor_tensor(rn[s][:, :], ms[s][:, :], minus_half[:, :], ALU.pow).then_inc(rn_ready[s], 1)

            def send(s, piece, at):
                if piece == 0:
                    if at.part == LOOP:
                        wait_apart(pool, slot_step[s], at.turn * SLOT_STEPS + SLOT_STEPS)
                    else:
                        pool.wait_ge(slot_step[s], at.turn * SLOT_STEPS + SLOT_STEPS)
                k = piece // 2
                rows = T - HT if k else HT
                pool.indirect_dma_start(
                    out=slot_token, out_offset=bass.IndirectOffsetOnAxis(ap=slotu[s][0:rows, piece:piece + 1], axis=0),
                    in_=toku[s][0:rows, k:k + 1], in_offset=None).then_inc(slots_sent[s], 16)

            def run(part, loop=None, later=None):
                for s, step, a, n, at in steps(pool_order, part, loop, later):
                    if step.startswith("sum"):
                        inverse_root(s, n, at)
                    else:
                        send(s, n, at)
                    if step == "sum1" and part == LOOP:
                        pool.wait_ge(slots_sent[s], loop * 64 + 64)
                        pool.sem_inc(sends_done[s], 1)

            run(FIRST)
            with pool.Fori(0, turns - 1) as loop:
                run(LOOP, loop, pool.snap(loop + 1))
            run(LAST)
            for s in range(SLOTS):
                pool.wait_ge(slots_sent[s], turns * 64)
                pool.wait_ge(rows_stored[s], turns * 48 + 48)
            pool.drain().then_inc(stage1_done, 1)

            with pool.Fori(0, blocks // 2) as it:
                for k in range(2):
                    wait_apart(pool, now_ready, nth(it, k, 1, 1))
                    for c in range(BC):
                        pool.indirect_dma_start(
                            out=exr[k][:, c, :], out_offset=None, in_=token_rows,
                            in_offset=bass.IndirectOffsetOnAxis(ap=enow[k][:, c:c + 1], axis=0)).then_inc(gathered[k], 16)

            for k in range(2):
                pool.wait_ge(y_stored[k], 16 * (blocks // 2))

            def gather_rows(it, groups):
                for g in range(2):
                    pool.wait_ge(idx_ready[g], it + 1)
                    if isinstance(it, int):
                        pool.wait_ge(gather_free[g], it * 2 + 2)
                    else:
                        wait_apart(pool, gather_free[g], it * 2 + 2)
                    for k, parts in groups[g]:
                        for c in range(2):
                            pool.indirect_dma_start(
                                out=gy[k][0:parts, c, :], out_offset=None, in_=slot_rows,
                                in_offset=bass.IndirectOffsetOnAxis(ap=gidx[g][0:parts, k % 2, c:c + 1], axis=0)
                            ).then_inc(rows_got[g], 16)

            with pool.Fori(0, turns3) as it:
                gather_rows(it, full_group)
            gather_rows(turns3, last_group)

        @block.scalar
        def _(act):
            act.sem_inc(exp_done, 2)
            act.sem_inc(heads_copied, 1)
            act.wait_ge(pack_loaded, 16)
            act.wait_ge(credits, 1)

            def square(s, n, at):
                drained(act, at, (s, NORM_SOURCE[n], "x"))
                act.activation(sq[s][:, :], norm_src(s, n)[:, :], ACT.Square).then_inc(sq_ready[s], 1)

            def centered(s, n, at):
                key = (s, f"center{n}", "x")
                ps = filled(act, at, key)
                act.activation((xT if n == 1 else hT)[s][:, :], ps[:, 0:TP], ACT.Copy).then_inc(free_of(key), 1)

            def qk_high(s, l, at):
                ps = filled(act, at, (s, f"qkv{l}", "qk"))
                act.activation(qk_hi[s][:, :, :], two(ps), ACT.Copy).then_inc(hi_ready[s], 1)

            def values(s, l, at):
                ps = filled(act, at, (s, f"qkv{l}", "v"))
                act.activation(va[s][:, :, :, 0:HD].rearrange("p k h d -> p (k h) d"),
                               ps[0:HT, 0:2 * D].rearrange("p (k d) -> p k d", d=HD), ACT.Copy
                               ).then_inc(free_of((s, f"qkv{l}", "v")), 1)

            def stacks(s, step, at):
                use, dst, tile, _ = sel_tiles(step[-1])[1]
                ps = filled(act, at, (s, step, use))
                act.activation(dst[s][:, tile:tile + 2, :], two(ps), ACT.Copy).then_inc(free_of((s, step, use)), 1)

            def exp(s, a, h, at):
                act.wait_ge(scoresT_full, at.before(attentions, (s, a), h + 1, HEADS))
                act.activation(pt[s][:, h, :, :], two(scoresT[h % 2], HT), ACT.Exp, scale=SCALE).then_inc(exp_done, 1)

            def heads_copy(s, a, at):
                act.wait_ge(heads_full, at.before(attentions, (s, a), 1))
                act.activation(ot[s][:, :, :], two(heads), ACT.Copy).then_inc(heads_copied, 1)

            def back(s, a, at):
                key = (s, f"back{a}", "x")
                ps = filled(act, at, key)
                act.activation(aT[s][:, :], ps[:, 0:TP], ACT.Copy).then_inc(free_of(key), 1)

            def tanh(s, step, at):
                ps = filled(act, at, (s, step, "x"))
                act.activation(th[s][:, "abc".index(step[4]), :], ps[0:FP, 0:TP], ACT.Tanh, scale=0.5
                               ).then_inc(th_ready[s], 1)

            def stack_copy(s, at):
                key = (s, "stack", "x")
                ps = filled(act, at, key)
                act.activation(qs[s][:, 0, :], ps[:, 0:TP], ACT.Copy)
                act.activation(k3[s][:, :], ps[:, TP:2 * TP], ACT.Copy).then_inc(free_of(key), 1)

            def masks(s, at):
                drained(act, at, (s, "stack", "x"))
                for h in range(4, HEADS):
                    i = act.activation(km[s][:, h, :], k3[s][:, :], ACT.Copy, scale=w("mask")[:, h:h + 1])
                i.then_inc(masks_act[s], 1)

            def rows(s, at):
                key = (s, "route", "rows")
                ps = filled(act, at, key)
                r = ps[0:HT, 0:4 * D].rearrange("p (a k d) -> p a k d", a=2, k=2)
                act.wait_ge(rows_stored[s], at.turn * 48 + 48)
                act.activation(srows[s][:, :, :], r[:, 0, :, :], ACT.Copy, scale=2.0)
                act.activation(hmr[s][:, :, :], r[:, 1, :, :], ACT.Copy).then_inc(free_of(key), 1)

            def run(part, loop=None, later=None):
                for s, step, a, n, at in steps(act_order, part, loop, later):
                    if step.startswith("sum"):
                        square(s, n, at)
                    elif step.startswith("center"):
                        centered(s, n, at)
                    elif step.startswith("qkv"):
                        if n < 2:
                            qk_high(s, n, at)
                        values(s, n, at)
                    elif step.startswith("sel"):
                        stacks(s, step, at)
                    elif step.startswith("head"):
                        if n >= LAG:
                            exp(s, a, n - LAG, at)
                    elif step.startswith("values"):
                        heads_copy(s, n, at)
                    elif step.startswith("back"):
                        back(s, n, at)
                    elif step.startswith("glu"):
                        tanh(s, step, at)
                    elif step == "stack":
                        stack_copy(s, at)
                    elif step == "masks":
                        masks(s, at)
                    elif step == "route":
                        rows(s, at)
                        act.wait_ge(gd_ready[s], at.turn + 1)
                        act.activation(ge[s][:, :], gd[s][:, :], ACT.Exp).then_inc(ge_ready[s], 1)

            run(FIRST)
            with act.Fori(0, turns - 1) as loop:
                run(LOOP, loop, act.snap(loop + 1))
            run(LAST)
            act.drain().then_inc(stage1_done, 1)
            act.wait_ge(stage1_done, 4)

            def high_tokens(pair, k):
                act.wait_ge(turned, nth(pair, k, 1, 1))
                act.activation(ex_parts[0][k % 2], turn_bank[k % 2][:, :], ACT.Copy).then_inc(tokens_high, 1)

            def gelu(pair, k):
                for f in range(EC):
                    act.wait_ge(hid_full, nth(pair, k, EC, f + 1))
                    act.activation(hid[k % 2][:, f, :], hid_bank[f][:, :], ACT.Gelu, bias=eb1[k % 2][:, f:f + 1]
                                   ).then_inc(act_done, 1)

            high_tokens(None, 0)
            high_tokens(None, 1)
            gelu(None, 0)
            with act.Fori(0, blocks // 2 - 1) as it:
                for k in range(1, 3):
                    high_tokens(it, k + 1)
                    gelu(it, k)
            gelu(None, blocks - 1)

            def load_stream(it, groups, g):
                act.wait_ge(gather_free[g], it * 2 + 2)
                for k, parts in groups[g]:
                    act.dma_start(hr[k][0:parts, :], stream_rows[bass.ds(it * 4 + k, 1), 0:parts, :].rearrange("a p n -> (a p) n")
                                  ).then_inc(hr_loaded[g], 16)

            def deviations(it, groups, g):
                act.wait_ge(var_ready[g], it * 2 + len(groups[g]))
                for k, parts in groups[g]:
                    act.activation(sd[k][0:parts, :], bn2[k][0:parts, 1:2], ACT.Sqrt, bias=eps[0:parts, :]).then_inc(sd_ready[g], 1)

            act.wait_ge(y_full, blocks)
            for g in range(2):
                load_stream(0, full_group, g)
            with act.Fori(0, turns3 - 1) as it:
                for g in range(2):
                    load_stream(it + 1, full_group, g)
                    deviations(it, full_group, g)
            for g in range(2):
                load_stream(turns3, last_group, g)
                deviations(turns3 - 1, full_group, g)
            for g in range(2):
                deviations(turns3, last_group, g)

        @block.tensor
        def _(pe):
            pe.wait_ge(pack_loaded, 16)
            pe.wait_ge(consts_ready, 1)
            ident = w("ident")

            def patch(s, at):
                key = (s, "patch", "x")
                pe.wait_ge(img_loaded[s % 2], at.turn * (SLOTS // 2 * 16) + (s // 2 * 16 + 16))
                ps = take(pe, at, key)
                conv = w("conv").rearrange("p (k o) -> p k o", k=PK)
                for k in range(PK):
                    mm = pe.matmul(ps[:, 0:TP], conv[:, k, :], imgs[s][:, k, :], start=(k == 0), stop=(k == PK - 1))
                mm.then_inc(full_of(key), 1)

            def sums(s, n, at):
                key = (s, f"sum{n}", "x")
                pe.wait_ge(sq_ready[s], at.turn * NORMS + (n + 1))
                ps = take(pe, at, key)
                for k in range(2):
                    mm = pe.matmul(ps[0:HT, k:k + 1], sq[s][:, k * HT:(k + 1) * HT], w("inv"), start=True, stop=True)
                mm.then_inc(full_of(key), 1)

            def scales(s, n, at):
                key = (s, f"scale{n}", "x")
                pe.wait_ge(rn_ready[s], at.turn * NORMS + (n + 1))
                ps = take(pe, at, key)
                for k in range(2):
                    mm = pe.matmul(ps[:, k * HT:(k + 1) * HT], rn[s][:, k:k + 1].to_broadcast([HT, 128]),
                                   ident[0:HT, 0:HT], start=True, stop=True)
                mm.then_inc(full_of(key), 1)

            def center(s, n, at):
                key = (s, f"center{n}", "x")
                drained(pe, at, (s, CENTER_SOURCE[n], "x"), taken=[key])
                ps = take(pe, at, key)
                pe.matmul(ps[:, 0:TP], w("center"), xT[s][:, :], start=True, stop=True).then_inc(full_of(key), 1)

            def qkv(s, l, at):
                drained(pe, at, (s, ["scale0", "scale2", "scale5"][l], "x"), taken=[(s, f"qkv{l}", "qk")])
                ps = take(pe, at, (s, f"qkv{l}", "qk"))
                for k in range(2):
                    if l < 2:
                        mm = pe.matmul(ps[:, k * TP:(k + 1) * TP], w(f"qk_{l}")[:, k * D:(k + 1) * D], hT[s][:, :],
                                       start=True, stop=True)
                    else:
                        mm = pe.matmul(ps[0:HT, k * 2 * HEADS:(k + 1) * 2 * HEADS], hT[s][:, k * HT:(k + 1) * HT],
                                       w("qk_2"), start=True, stop=True)
                mm.then_inc(full_of((s, f"qkv{l}", "qk")), 1)
                ps = take(pe, at, (s, f"qkv{l}", "v"))
                for k in range(2):
                    mm = pe.matmul(ps[0:HT, k * D:(k + 1) * D], hT[s][:, k * HT:(k + 1) * HT], w(f"v_{l}"),
                                   start=True, stop=True)
                mm.then_inc(full_of((s, f"qkv{l}", "v")), 1)

            def select(s, step, at):
                l, which = int(step[3]), 0 if step[-1] == "a" else 1
                drained(pe, at, (s, f"qkv{l}", "qk"), taken=[(s, step, "p0")])
                for use, _, _, col in sel_tiles(step[-1]):
                    ps = take(pe, at, (s, step, use))
                    for j in range(2):
                        for part, src in enumerate((qk_hi, qk_lo)):
                            mm = pe.matmul(ps[:, j * TP:(j + 1) * TP], selr[:, part, (col + j) * D:(col + j + 1) * D],
                                           src[s][:, which, :], start=(part == 0), stop=(part == 1))
                    mm.then_inc(full_of((s, step, use)), 1)

            def head_scores(s, a, h, at):
                if a < 2:
                    if h == 0:
                        drained(pe, at, *[(s, f"sel{a}{x}", p) for x in "ab" for p in ("p0", "p1")])
                    if h == 4:
                        drained(pe, at, *[(s, f"sel{a}c", p) for p in ("p0", "p1")])
                elif h < 4:
                    pe.wait_ge(masks_dve[s], at.turn * 4 + (h + 1))
                elif h == 4:
                    pe.wait_ge(masks_act[s], at.turn + 1)
                q = qs[s][:, h // 2 if a < 2 else 0, :]
                for k in range(2):
                    mm = pe.matmul(scores[h % 2][0:RT, k * TP:(k + 1) * TP], q[:, k * (TP - RT):k * (TP - RT) + RT],
                                   km[s][:, h, :], start=True, stop=True)
                mm.then_inc(scores_full, 1)

            def head_scoresT(s, a, h, at):
                pe.wait_ge(max_done, at.before(attentions, (s, a), h + 3, HEADS))
                pe.wait_ge(exp_done, at.before(attentions, (s, a), h + 1, HEADS))
                q = qs[s][:, h // 2 if a < 2 else 0, :]
                ps = scoresT[h % 2]
                both = two(ps, HT)
                for j in range(2):
                    skip = j * (2 * RT - TP)
                    pe.matmul(both[:, :, j * RT:(j + 1) * RT - skip], nm[s][:, j, h:h + 1].to_broadcast([RT, HT]),
                              identr[:, skip:RT][:, None, :].to_broadcast([RT, 2, RT - skip]), start=(j == 0), stop=False,
                              skip_group_check=True)
                for k in range(2):
                    mm = pe.matmul(ps[0:HT, k * TP:(k + 1) * TP], km[s][:, h, k * HT:(k + 1) * HT], q,
                                   start=False, stop=True, skip_group_check=True)
                mm.then_inc(scoresT_full, 1)

            def head_values(s, a, g, at):
                if g == 0:
                    drained(pe, at, (s, f"qkv{a}", "v"))
                    pe.wait_ge(heads_copied, at.before(attentions, (s, a), 1))
                pe.wait_ge(exp_done, at.before(attentions, (s, a), 4 * g + 3 + 3, HEADS))
                for k in range(2):
                    rows = T - HT if k else HT
                    for j in range(4):
                        mm = pe.matmul(heads[32 * j:32 * j + 32, g * TP:(g + 1) * TP], va[s][0:rows, k, 4 * g + j, :],
                                       pt[s][0:rows, 4 * g + j, k, :], start=(k == 0), stop=(k == 1),
                                       skip_group_check=True)
                if g == 1:
                    mm.then_inc(heads_full, 1)

            def turn(s, a, at):
                key = (s, f"turn{a}", "x")
                pe.wait_ge(heads_copied, at.before(attentions, (s, a), 2))
                ps = take(pe, at, key)
                for k in range(2):
                    for g in range(2):
                        mm = pe.transpose(ps[0:HT, (2 * k + g) * D:(2 * k + g + 1) * D],
                                          ot[s][:, g, k * HT:(k + 1) * HT], ident)
                mm.then_inc(full_of(key), 1)

            def back(s, a, at):
                key = (s, f"back{a}", "x")
                drained(pe, at, (s, f"turn{a}", "x"), taken=[key])
                ps = take(pe, at, key)
                for k in range(2):
                    mm = pe.transpose(ps[:, k * HT:(k + 1) * HT],
                                      ao[s][:, 8 * k:8 * k + 8, :].rearrange("p h d -> p (h d)"), ident[0:HT, 0:HT])
                mm.then_inc(full_of(key), 1)

            def proj(s, a, at):
                key = (s, f"proj{a}", "x")
                drained(pe, at, (s, f"back{a}", "x"), taken=[key])
                ps = take(pe, at, key)
                pe.matmul(ps[:, 0:TP], w(f"wo_{a}"), aT[s][:, :], start=True, stop=True).then_inc(full_of(key), 1)

            def glu(s, step, at):
                l, f = int(step[3]), "abc".index(step[4])
                key = (s, step, "x")
                if f == 0:
                    drained(pe, at, (s, f"scale{2 * l + 1}", "x"), taken=[key])
                ps = take(pe, at, key)
                for k, name in enumerate(("gate", "up")):
                    mm = pe.matmul(ps[0:FP, k * TP:(k + 1) * TP], w(f"{name}_{l}")[:, f * FP:(f + 1) * FP],
                                   hT[s][:, :], start=True, stop=True)
                mm.then_inc(full_of(key), 1)

            def down(s, l, at):
                key = (s, f"down{l}", "x")
                ps = take(pe, at, key)
                wd = w(f"down_{l}").rearrange("p (f o) -> p f o", f=FC)
                for f in range(FC):
                    drained(pe, at, (s, f"glu{l}" + "abc"[f], "x"), taken=[key])
                    mm = pe.matmul(ps[:, 0:TP], wd[0:FP, f, :], gl[s][:, f, :], start=(f == 0), stop=(f == FC - 1))
                mm.then_inc(full_of(key), 1)

            def stack(s, at):
                key = (s, "stack", "x")
                pe.wait_ge(stack_step[s], at.turn * 8 + 8)
                ps = take(pe, at, key)
                for j, src in enumerate((stq, stk)):
                    for k in range(2):
                        mm = pe.transpose(ps[:, j * TP + k * HT:j * TP + (k + 1) * HT],
                                          src[s][:, k, :, :].rearrange("p h d -> p (h d)").bitcast(F32),
                                          ident[0:HT, 0:HT])
                mm.then_inc(full_of(key), 1)

            def route(s, at):
                key = (s, "route", "rows")
                drained(pe, at, (s, "scale6", "x"), taken=[key])
                pe.wait_ge(hm_ready[s], at.turn + 1)
                ps = take(pe, at, key)
                for j, src in enumerate((xT, hT)):
                    for k in range(2):
                        mm = pe.transpose(ps[0:HT, (2 * j + k) * D:(2 * j + k + 1) * D], src[s][:, k * HT:(k + 1) * HT], ident)
                mm.then_inc(full_of(key), 1)
                key = (s, "route", "logits")
                ps = take(pe, at, key)
                for k in range(2):
                    mm = pe.matmul(ps[0:HT, k * EXPERTS:(k + 1) * EXPERTS], hT[s][:, k * HT:(k + 1) * HT], w("wr"),
                                   start=True, stop=True)
                mm.then_inc(full_of(key), 1)

            def ranks(s, at):
                key = (s, "slots", "x")
                pe.wait_ge(chosen_ready[s], at.turn + 1)
                ps = take(pe, at, key)
                last = T - HT
                groups = [[(lowb, HT, 0)], [(lowb, last, 1), (onesb, HT, 0)], [(onesb, HT, 0), (onesb, last, 1)]]
                for j, group in enumerate(groups):
                    terms = [(m, rows, k, c) for m, rows, k in group for c in range(2)]
                    for i, (m, rows, k, c) in enumerate(terms):
                        mm = pe.matmul(ps[0:HT, j * EXPERTS:(j + 1) * EXPERTS], m[0:rows, :], onehb[s][0:rows, 2 * k + c, :],
                                       start=(i == 0), stop=(i == len(terms) - 1))
                mm.then_inc(full_of(key), 1)

            def run(part, loop=None, later=None):
                for s, step, a, n, at in steps(order, part, loop, later):
                    if step == "patch":
                        patch(s, at)
                    elif step.startswith("sum"):
                        sums(s, n, at)
                    elif step.startswith("scale"):
                        scales(s, n, at)
                    elif step.startswith("center"):
                        center(s, n, at)
                    elif step.startswith("qkv"):
                        qkv(s, n, at)
                    elif step.startswith("sel"):
                        select(s, step, at)
                    elif step.startswith("head"):
                        if n >= LAG:
                            head_scoresT(s, a, n - LAG, at)
                        if n < HEADS:
                            head_scores(s, a, n, at)
                        if n == 7:
                            head_values(s, a, 0, at)
                    elif step.startswith("values"):
                        head_values(s, n, 1, at)
                    elif step.startswith("turn"):
                        turn(s, n, at)
                    elif step.startswith("back"):
                        back(s, n, at)
                    elif step.startswith("proj"):
                        proj(s, n, at)
                    elif step.startswith("glu"):
                        glu(s, step, at)
                    elif step.startswith("down"):
                        down(s, n, at)
                    elif step == "stack":
                        stack(s, at)
                    elif step == "route":
                        route(s, at)
                    elif step == "slots":
                        ranks(s, at)

            run(FIRST)
            with pe.Fori(0, turns - 1) as loop:
                run(LOOP, loop, pe.snap(loop + 1))
            run(LAST)
            pe.drain().then_inc(stage1_done, 1)
            pe.wait_ge(stage1_done, 4)

            def product(ps, lhs, rhs):
                for i, (a, b) in enumerate(PARTS):
                    mm = pe.matmul(ps, lhs[a], rhs[b], start=(i == 0), stop=(i == len(PARTS) - 1))
                return mm

            def turn_tokens(pair, k):
                pe.wait_ge(gathered[k % 2], same(pair, k, 16 * BC))
                wait_block(pe, tokens_ready, pair, k, 1, -1)
                for c in range(BC):
                    mm = pe.transpose(turn_bank[k % 2][:, c * D:(c + 1) * D], exr[k % 2][:, c, :], ident)
                mm.then_inc(turned, 1)

            def hidden(pair, k):
                pe.wait_ge(w1_ready, nth(pair, k, 1, 1))
                pe.wait_ge(tokens_ready, nth(pair, k, 1, 1))
                for f in range(EC):
                    wait_block(pe, act_done, pair, k, EC, f + 1 - EC)
                    product(hid_bank[f][:, :], [x[k % 2][:, f * D:(f + 1) * D] for x in ew1_parts], [x[k % 2] for x in ex_parts]
                            ).then_inc(hid_full, 1)

            def results(pair, k):
                pe.wait_ge(w2_loaded[k % 2], same(pair, k, 16))
                pe.wait_ge(y_ready, nth(pair, k, 1, 1))
                for c in range(BC):
                    ps = y_bank[k % 2][:, c * D:(c + 1) * D]
                    for f in range(EC):
                        if c == 0:
                            pe.wait_ge(act_done, nth(pair, k, EC, f + 1))
                        mm = pe.matmul(ps, hid[k % 2][:, f, c * D:(c + 1) * D], ew2[k % 2][:, f, :], start=(f == 0),
                                       stop=(f == EC - 1))
                mm.then_inc(y_full, 1)

            pe.wait_ge(choices_ready, 1)
            for n in range(2):
                for c in range(2):
                    pe.transpose(y_bank[0][0:halves, (2 * n + c) * HT:(2 * n + c + 1) * HT], by_choice[:, 2 * n + c, :], ident[0:HT, 0:HT])
            pe.drain().then_inc(choices_turned, 1)

            turn_tokens(None, 0)
            turn_tokens(None, 1)
            hidden(None, 0)
            with pe.Fori(0, blocks // 2 - 1) as it:
                for k in range(1, 3):
                    turn_tokens(it, k + 1)
                    hidden(it, k)
                    results(it, k - 1)
            hidden(None, blocks - 1)
            results(None, blocks - 2)
            results(None, blocks - 1)

        @block.vector
        def _(dve):
            dve.memset(minus_half[:, :], -0.5)
            dve.memset(eps[:, :], EPS_LN)
            dve.memset(where_rows[:, HT:HT + 1, :], 0)
            dve.memset(turned_gates[:, HT:HT + 1, :], 0.0)
            dve.memset(work[:, :, blocks:blocks + 3], 0)
            dve.memset(onesb[:, :], 1.0)
            for s in range(SLOTS):
                dve.memset(va[s][:, :, :, :], 0.0)
                dve.memset(stq[s][:, :, :, :].bitcast(F32), 0.0)
                dve.memset(stk[s][:, :, :, :].bitcast(F32), 0.0)
            dve.drain()
            for s in range(SLOTS):
                dve.memset(va[s][:, :, :, HD:HD + 1], 1.0)
                dve.memset(stq[s][:, :, :, 4:6].bitcast(F32), 1.0)
            dve.wait_ge(pack_loaded, 16)
            dve.tensor_copy(lowb[:, :], w("lower", HT))
            dve.tensor_copy(nxt[:, :], w("first", HT))
            dve.tensor_copy(identr[:, :], w("ident", RT)[:, 0:RT])
            for s in range(SLOTS):
                dve.tensor_copy(tokf[s][:, :], w("token", HT)[:, 2 * s:2 * s + 2])
            pos = w("pos")
            dve.tensor_scalar(pos[:, 1:TP], pos[:, 1:TP], w("conv_b"), None, ALU.add)
            dve.tensor_tensor(pos[:, 0:1], pos[:, 0:1], w("cls"), ALU.add)
            for l in range(2):
                dve.tensor_scalar(w(f"down_{l}"), w(f"down_{l}"), 0.5, None, ALU.mult)
            dve.wait_ge(sel_loaded, 16)
            dve.tensor_copy(selr[:, :, :].rearrange("p a n -> p (a n)"), ptw[0][:, 0:2 * SEL_COLS])
            dve.drain().then_inc(consts_ready, 1)
            for b in range(SHARED_BANKS):
                dve.sem_inc(free[b], 1)
            dve.sem_inc(max_done, 2)
            dve.sem_inc(nxt_ready, 1)
            for s in range(SLOTS):
                dve.sem_inc(tok_ready[s], 1)
                dve.sem_inc(sends_done[s], 1)
                dve.sem_inc(rows_stored[s], 48)
            dve.sem_inc(y_ready, 2)
            for g in range(2):
                dve.sem_inc(gather_free[g], 2)
                dve.sem_inc(out_stored[g], 64)
            dve.sem_inc(credits, 1)

            def embed(s, at):
                key = (s, "patch", "x")
                ps = filled(dve, at, key)
                dve.tensor_tensor(xT[s][:, :], ps[:, 0:TP], w("pos"), ALU.add).then_inc(free_of(key), 1)

            def mean_square(s, n, at):
                key = (s, f"sum{n}", "x")
                ps = filled(dve, at, key)
                dve.tensor_scalar(ms[s][:, :], ps[0:HT, 0:2], EPS_LN if n >= 5 else EPS_RMS, None, ALU.add
                                  ).then_inc(free_of(key), 1)

            def normed(s, n, at):
                key = (s, f"scale{n}", "x")
                ps = filled(dve, at, key)
                src, dst = norm_src(s, n)[:, :], norm_dst(s, n)[:, :]
                if n in NORM_WEIGHT:
                    i = dve.scalar_tensor_tensor(out=dst, in0=src, scalar=w(NORM_WEIGHT[n]), in1=ps[:, 0:TP],
                                                 op0=ALU.mult, op1=ALU.mult)
                else:
                    i = dve.tensor_tensor(dst, src, ps[:, 0:TP], ALU.mult)
                i.then_inc(free_of(key), 1)
                if n == 7:
                    drained(dve, at, key)
                    dve.tensor_scalar(dst, dst, w("ln_b"), None, ALU.add).then_inc(hm_ready[s], 1)

            def qk_low(s, l, at):
                key = (s, f"qkv{l}", "qk")
                ps = filled(dve, at, key)
                dve.wait_ge(hi_ready[s], at.turn * 2 + (l + 1))
                dve.tensor_tensor(qk_lo[s][:, :, :], two(ps), qk_hi[s][:, :, :], ALU.subtract).then_inc(free_of(key), 1)

            def stacks(s, step, at):
                use, dst, tile, _ = sel_tiles(step[-1])[0]
                ps = filled(dve, at, (s, step, use))
                dve.tensor_copy(dst[s][:, tile:tile + 2, :], two(ps)).then_inc(free_of((s, step, use)), 1)

            def maxima(s, a, h, at):
                dve.wait_ge(scores_full, at.before(attentions, (s, a), h + 1, HEADS))
                dve.tensor_reduce(nm[s][:, :, h], two(scores[h % 2], RT)[:, :, 0:T], AX.X, ALU.max, negate=True
                                  ).then_inc(max_done, 1)

            def divide(s, a, at):
                key = (s, f"turn{a}", "x")
                ps = filled(dve, at, key)
                r = ps[0:HT, :].rearrange("p (n c) -> p n c", c=32)
                dve.reciprocal(rc[s][:, :], r[:, :, HD]).then_inc(recip_ready[s], 1)
                dve.wait_ge(recip_ready[s], at.turn * 3 + (a + 1))
                dve.tensor_tensor(ao[s][:, :, :], r[:, :, 0:HD], rc[s][:, :, None].to_broadcast([HT, 2 * HEADS, HD]),
                                  ALU.mult).then_inc(free_of(key), 1)

            def add(s, key, at, twice=False):
                ps = filled(dve, at, key)
                if twice:
                    i = dve.scalar_tensor_tensor(out=xT[s][:, :], in0=xT[s][:, :], scalar=2.0, in1=ps[:, 0:TP],
                                                 op0=ALU.mult, op1=ALU.add)
                else:
                    i = dve.tensor_tensor(xT[s][:, :], xT[s][:, :], ps[:, 0:TP], ALU.add)
                i.then_inc(free_of(key), 1)

            def gated(s, step, at):
                l, f = int(step[3]), "abc".index(step[4])
                key = (s, step, "x")
                n = FC * l + f + 1
                dve.wait_ge(th_ready[s], at.turn * 2 * FC + n)
                ps = misc[where[key]]
                dve.scalar_tensor_tensor(out=gl[s][:, f, :], in0=th[s][:, f, :], scalar=1.0, in1=ps[0:FP, 0:TP],
                                         op0=ALU.add, op1=ALU.mult).then_inc(glu_half[s], 1)
                dve.wait_ge(glu_half[s], at.turn * 2 * FC + n)
                dve.tensor_tensor(gl[s][:, f, :], gl[s][:, f, :], ps[0:FP, TP:2 * TP], ALU.mult
                                  ).then_inc(free_of(key), 1)

            def stack(s, at):
                key = (s, "qkv2", "qk")
                ps = filled(dve, at, key)
                qk = ps[0:HT, 0:4 * HEADS].rearrange("p (k n) -> p k n", k=2)
                q, k_ = qk[:, :, 0:HEADS], qk[:, :, HEADS:2 * HEADS]

                def twice(ap):
                    return ap[:, :, :, None].to_broadcast([HT, 2, HEADS, 2])

                q_hi = stq[s][:, :, :, 0]
                dve.tensor_copy(stq[s][:, :, :, 0:2], twice(q)).then_inc(stack_step[s], 1)
                dve.tensor_scalar(kf[s][:, 0, :, :], k_, 2.0, None, ALU.mult).then_inc(stack_step[s], 1)
                dve.wait_ge(stack_step[s], at.turn * 8 + 2)
                for j in range(2):
                    i = dve.tensor_tensor(stq[s][:, :, :, 2 + j], q, q_hi, ALU.subtract)
                i.then_inc(free_of(key), 1)
                dve.tensor_copy(stk[s][:, :, :, 0:3:2], twice(kf[s][:, 0, :, :])).then_inc(stack_step[s], 1)
                dve.scalar_tensor_tensor(out=kf[s][:, 1, :, :], in0=kf[s][:, 0, :, :], scalar=-0.25,
                                         in1=kf[s][:, 0, :, :], op0=ALU.mult, op1=ALU.mult).then_inc(stack_step[s], 1)
                dve.wait_ge(stack_step[s], at.turn * 8 + 4)
                for j in range(2):
                    i = dve.tensor_tensor(stk[s][:, :, :, 1 + 2 * j], kf[s][:, 0, :, :], stk[s][:, :, :, 0], ALU.subtract)
                i.then_inc(stack_step[s], 1)
                dve.tensor_copy(stk[s][:, :, :, 4], kf[s][:, 1, :, :]).then_inc(stack_step[s], 1)
                dve.wait_ge(stack_step[s], at.turn * 8 + 6)
                dve.tensor_tensor(stk[s][:, :, :, 5], kf[s][:, 1, :, :], stk[s][:, :, :, 4], ALU.subtract
                                  ).then_inc(stack_step[s], 1)
                dve.drain().then_inc(stack_step[s], 1)

            def masks(s, at):
                drained(dve, at, (s, "stack", "x"))
                for h in range(4):
                    dve.tensor_scalar(km[s][:, h, :], k3[s][:, :], w("mask")[:, h:h + 1], None, ALU.mult).then_inc(masks_dve[s], 1)

            def choose(s, at):
                key = (s, "route", "logits")
                ps = filled(dve, at, key)
                dve.tensor_tensor(lg[s][:, :, :], ps[0:HT, 0:2 * EXPERTS].rearrange("p (k e) -> p k e", k=2),
                                  w("br", HT)[:, None, :].to_broadcast([HT, 2, EXPERTS]), ALU.add).then_inc(free_of(key), 1)
                b = where[key]
                if at.part == LOOP:
                    wait_apart(dve, free[b], at.before(ranks[b], key, 2))
                else:
                    dve.wait_ge(free[b], at.before(ranks[b], key, 2))
                for k in range(2):
                    dve.max(top[s][:, k, :], lg[s][:, k, :]).then_inc(top_step[s], 1)
                dve.wait_ge(top_step[s], at.turn * 7 + 2)
                dve.tensor_tensor(gd[s][:, :], top[s][:, :, 1], top[s][:, :, 0], ALU.subtract).then_inc(gd_ready[s], 1)
                for k in range(2):
                    dve.max_index(topi[s][:, k, :], top[s][:, k, :], lg[s][:, k, :]).then_inc(top_step[s], 1)
                dve.wait_ge(top_step[s], at.turn * 7 + 4)
                dve.tensor_copy(chosen[s][:, :].rearrange("p (k c) -> p k c", k=2), topi[s][:, :, 0:2]).then_inc(top_step[s], 1)
                dve.wait_ge(top_step[s], at.turn * 7 + 5)
                dve.tensor_tensor(oneh[s][:, :, :], w("iota", HT)[:, None, :].to_broadcast([HT, 4, EXPERTS]),
                                  chosen[s][:, :, None].to_broadcast([HT, 4, EXPERTS]), ALU.is_equal)
                dve.tensor_tensor(onehb[s][:, :, :], w("iota", HT)[:, None, :].to_broadcast([HT, 4, EXPERTS]),
                                  chosen[s][:, :, None].to_broadcast([HT, 4, EXPERTS]), ALU.is_equal).then_inc(chosen_ready[s], 1)

            def weigh(s, at):
                dve.wait_ge(ge_ready[s], at.turn + 1)
                dve.tensor_scalar(gs[s][:, :], ge[s][:, :], 1.0, None, ALU.add).then_inc(top_step[s], 1)
                dve.wait_ge(top_step[s], at.turn * 7 + 6)
                dve.reciprocal(gr[s][:, :], gs[s][:, :]).then_inc(top_step[s], 1)
                dve.wait_ge(top_step[s], at.turn * 7 + 7)
                dve.tensor_copy(gates[:, bass.ds((at.turn * SLOTS + s) * 2, 2), 0], gr[s][:, :])
                dve.tensor_tensor(gates[:, bass.ds((at.turn * SLOTS + s) * 2, 2), 1], ge[s][:, :], gr[s][:, :], ALU.mult)

            def place(s, at):
                key = (s, "slots", "x")
                ps = filled(dve, at, key)
                dve.tensor_copy(cnt3[s][:, :, :], ps[0:HT, 0:3 * EXPERTS].rearrange("p (k e) -> p k e", k=3)
                                ).then_inc(free_of(key), 1)
                drained(dve, at, key)
                dve.wait_ge(nxt_ready, at.turn * SLOTS + (s + 1))
                dve.tensor_tensor(rank[s][:, :, :], cnt3[s][:, 0:2, :], nxt[:, None, :].to_broadcast([HT, 2, EXPERTS]), ALU.add
                                  ).then_inc(slot_step[s], 1)
                dve.wait_ge(slot_step[s], at.turn * SLOT_STEPS + 1)
                dve.tensor_tensor(nxt[:, :], nxt[:, :], cnt3[s][:, 2, :], ALU.add).then_inc(nxt_ready, 1)
                for k in range(2):
                    i = dve.tensor_tensor(cand[s][:, 2 * k:2 * k + 2, :], oneh[s][:, 2 * k:2 * k + 2, :],
                                          rank[s][:, k:k + 1, :].to_broadcast([HT, 2, EXPERTS]), ALU.mult)
                i.then_inc(slot_step[s], 1)
                dve.wait_ge(slot_step[s], at.turn * SLOT_STEPS + 2)
                dve.tensor_reduce(slotf[s][:, :], cand[s][:, :, :], AX.X, ALU.add).then_inc(slot_step[s], 1)
                dve.wait_ge(slot_step[s], at.turn * SLOT_STEPS + 3)
                dve.tensor_copy(slots[:, bass.ds((at.turn * SLOTS + s) * 2, 2), :], slotf[s][:, :].rearrange("p (k c) -> p k c", k=2))
                dve.wait_ge(sends_done[s], at.turn + 1)
                dve.tensor_copy(slotu[s][:, :], slotf[s][:, :])
                dve.wait_ge(tok_ready[s], at.turn + 1)
                dve.tensor_copy(toku[s][:, :], tokf[s][:, :]).then_inc(slot_step[s], 1)
                dve.wait_ge(slot_step[s], at.turn * SLOT_STEPS + 4)
                dve.tensor_scalar(tokf[s][:, :], tokf[s][:, :], float(SLOTS * T), None, ALU.add).then_inc(tok_ready[s], 1)

            def run(part, loop=None, later=None):
                for s, step, a, n, at in steps(dve_order, part, loop, later):
                    if step == "patch":
                        embed(s, at)
                    elif step.startswith("sum"):
                        mean_square(s, n, at)
                    elif step.startswith("scale"):
                        normed(s, n, at)
                    elif step.startswith("qkv"):
                        if n < 2:
                            qk_low(s, n, at)
                        else:
                            stack(s, at)
                    elif step.startswith("sel"):
                        stacks(s, step, at)
                    elif step.startswith("head"):
                        if n < HEADS:
                            maxima(s, a, n, at)
                    elif step.startswith("turn"):
                        divide(s, n, at)
                    elif step.startswith("proj"):
                        add(s, (s, step, "x"), at, twice=(n == 2))
                    elif step.startswith("glu"):
                        gated(s, step, at)
                    elif step.startswith("down"):
                        add(s, (s, step, "x"), at)
                    elif step == "masks":
                        masks(s, at)
                    elif step == "route":
                        choose(s, at)
                    elif step == "slots":
                        place(s, at)
                        weigh(s, at)

            run(FIRST)
            with dve.Fori(0, turns - 1) as loop:
                run(LOOP, loop, dve.snap(loop + 1))
            run(LAST)
            dve.drain().then_inc(stage1_done, 1)
            dve.wait_ge(nxt_ready, images + 1)
            at = [0]

            def step(ins):
                ins.then_inc(map_step, 1)
                at[0] += 1
                dve.wait_ge(map_step, at[0])

            first, fill, number = w("first", HT), w("fill", HT), w("block", 1)
            step(dve.tensor_tensor(held[:, :], nxt[:, :], first, ALU.subtract))
            step(dve.tensor_tensor(fills[:, :, :], held[:, :, None].to_broadcast([HT, EXPERTS, region_blocks]),
                                   fill[:, None, :].to_broadcast([HT, EXPERTS, region_blocks]), ALU.is_gt))
            step(dve.tensor_reduce(nblk[:, :], fills[:, :, :], AX.X, ALU.add))
            step(dve.tensor_scalar(jump[:, :], nblk[:, :], -float(BLK), float(region), ALU.mult, ALU.add))
            step(dve.memset(cum[:, 0:1], 0.0))
            for e in range(EXPERTS):
                step(dve.tensor_tensor(cum[:, e + 1:e + 2], cum[:, e:e + 1], nblk[0:1, e:e + 1], ALU.add))
            step(dve.tensor_tensor(past[:, :, :], number[:, :, None].to_broadcast([1, blocks, EXPERTS]),
                                   cum[:, None, 1:EXPERTS + 1].to_broadcast([1, blocks, EXPERTS]), ALU.is_ge))
            step(dve.tensor_reduce(of_expert[:, :], past[:, :, :], AX.X, ALU.add))
            step(dve.tensor_scalar(work[:, 0, 0:blocks], of_expert[:, :], float(EXPERTS - 1), None, ALU.min))
            step(dve.tensor_tensor(jumped[:, :, :], past[:, :, :], jump[0:1, None, :].to_broadcast([1, blocks, EXPERTS]), ALU.mult))
            step(dve.tensor_reduce(of_row[:, :], jumped[:, :, :], AX.X, ALU.add))
            step(dve.scalar_tensor_tensor(out=work[:, 1, 0:blocks], in0=number, scalar=float(BLK), in1=of_row[:, :],
                                          op0=ALU.mult, op1=ALU.add))
            assert at[0] == MAP_STEPS
            rows_of = slots[:, :, :].rearrange("p n c -> p (n c)")
            for e in range(1, EXPERTS):
                step(dve.tensor_scalar(less[:, :], rows_of, float(e * region), jump[:, e - 1:e], ALU.is_ge, ALU.mult))
                step(dve.tensor_tensor(moved[:, :], (rows_of if e == 1 else moved[:, :]), less[:, :], ALU.subtract))

            for n, src in enumerate((moved[:, :], gates[:, :, :].rearrange("p n c -> p (n c)"))):
                for k in range(2):
                    dve.tensor_copy(by_choice[:, 2 * n:2 * n + 2, k * images:(k + 1) * images],
                                    src.rearrange("p (i k c) -> p c k i", k=2, c=2)[:, :, k, :])
            dve.drain().then_inc(choices_ready, 1)

            dve.wait_ge(choices_turned, 1)
            choices = y_bank[0][0:halves, 0:4 * HT].rearrange("p (n c t) -> p n t c", n=2, c=2)
            dve.tensor_copy(where_rows[:, 0:HT, :], choices[:, 0, :, :])
            dve.tensor_copy(turned_gates[:, 0:HT, :], choices[:, 1, :, :])
            dve.drain()

            def token_numbers(pair, k):
                dve.wait_ge(idx_loaded[k % 2], same(pair, k, 16))
                dve.tensor_copy(enow[k % 2][:, :], eidx[k % 2][:, :]).then_inc(now_ready, 1)

            def low_tokens(pair, k):
                dve.wait_ge(tokens_high, nth(pair, k, 1, 1))
                dve.tensor_tensor(ex_parts[1][k % 2], turn_bank[k % 2][:, :], ex_parts[0][k % 2], ALU.subtract).then_inc(tokens_ready, 1)
                token_numbers(pair, k + 2)

            def split_w1(pair, k):
                dve.wait_ge(w1_loaded[k % 2], same(pair, k, 16))
                dve.tensor_copy(ew1_parts[0][k % 2], ew1[k % 2]).then_inc(w1_high, 1)
                dve.wait_ge(w1_high, nth(pair, k, 1, 1))
                dve.tensor_tensor(ew1_parts[1][k % 2], ew1[k % 2], ew1_parts[0][k % 2], ALU.subtract).then_inc(w1_ready, 1)

            def copy_results(pair, k):
                dve.wait_ge(y_full, nth(pair, k, 1, 1))
                if pair is not None or k >= 2:
                    dve.wait_ge(y_stored[k % 2], same(pair, k, 16, -16))
                dve.tensor_tensor(ey[k % 2], y_bank[k % 2][:, :].rearrange("p (c n) -> p c n", c=BC),
                                  eb2[k % 2][:, None, :].to_broadcast([128, BC, D]), ALU.add).then_inc(y_ready, 1)

            token_numbers(None, 0)
            token_numbers(None, 1)
            split_w1(None, 0)
            low_tokens(None, 0)
            split_w1(None, 1)
            low_tokens(None, 1)
            for k in (1, 2):
                low_tokens(None, k + 1)
                split_w1(None, k + 1)
                copy_results(None, k - 1)
            with dve.Fori(0, blocks // 2 - 2) as it:
                for k in (3, 4):
                    low_tokens(it, k + 1)
                    split_w1(it, k + 1)
                    copy_results(it, k - 1)
            copy_results(None, blocks - 2)
            copy_results(None, blocks - 1)

            def numbers(it, g):
                dve.tensor_copy(gidx[g][:, :, :], where_rows[:, bass.ds(it * 4 + 2 * g, 2), :]).then_inc(idx_ready[g], 1)

            def normalise(it, groups, last=False):
                for g in range(2):
                    here = groups[g]
                    dve.tensor_copy(gg[g][:, :, :], turned_gates[:, bass.ds(it * 4 + 2 * g, 2), :]).then_inc(gates_ready[g], 1)
                    dve.wait_ge(rows_got[g], it * 64 + 32 * len(here))
                    if not last:
                        numbers(it + 1, g)
                    dve.wait_ge(gates_ready[g], it + 1)
                    dve.wait_ge(hr_loaded[g], it * 32 + 16 * len(here))
                    for k, parts in here:
                        dve.scalar_tensor_tensor(out=mix[k][0:parts, 0, :], in0=gy[k][0:parts, 0, :],
                                                 scalar=gg[g][0:parts, k % 2, 0:1], in1=hr[k][0:parts, :],
                                                 op0=ALU.mult, op1=ALU.add).then_inc(mix_step[g], 1)
                    n = len(here)
                    for k, parts in here:
                        dve.wait_ge(mix_step[g], it * 6 + (1 + k % 2))
                        dve.scalar_tensor_tensor(out=mix[k][0:parts, 1, :], in0=gy[k][0:parts, 1, :],
                                                 scalar=gg[g][0:parts, k % 2, 1:2], in1=mix[k][0:parts, 0, :],
                                                 op0=ALU.mult, op1=ALU.add).then_inc(gather_free[g], 1)
                    for k, parts in here:
                        dve.wait_ge(gather_free[g], it * 2 + (3 + k % 2))
                        dve.bn_stats(bn6[k][0:parts, :], mix[k][0:parts, 1, :]).then_inc(mix_step[g], 1)
                    for k, parts in here:
                        if last:
                            dve.wait_ge(mix_step[g], it * 6 + (n + 1 + k % 2))
                        else:
                            wait_apart(dve, mix_step[g], it * 6 + (n + 1 + k % 2))
                        dve.bn_aggr(bn2[k][0:parts, :], bn6[k][0:parts, :]).then_inc(var_ready[g], 1)
                for g in range(2):
                    for k, parts in groups[g]:
                        dve.wait_ge(sd_ready[g], it * 2 + (1 + k % 2))
                        dve.reciprocal(rs[k][0:parts, :], sd[k][0:parts, :]).then_inc(mix_step[g], 1)
                for g in range(2):
                    for k, parts in groups[g]:
                        dve.wait_ge(mix_step[g], it * 6 + (2 * len(groups[g]) + 1 + k % 2))
                        dve.wait_ge(out_stored[g], it * 64 + 64)
                        dve.tensor_scalar(fin[k][0:parts, :], mix[k][0:parts, 1, :], bn2[k][0:parts, 0:1], rs[k][0:parts, :],
                                          ALU.subtract, ALU.mult).then_inc(fin_ready[g], 1)

            for g in range(2):
                numbers(0, g)
            with dve.Fori(0, turns3) as it:
                normalise(it, full_group)
            normalise(turns3, last_group, last=True)


MAP_STEPS = 4 + EXPERTS + 7
SLOT_STEPS = 4


def layouts(images, x, L0_tok_conv_w, L0_tok_conv_b, L0_tok_cls_token, L0_tok_pos_emb, L0_tok_ln_f,
            L0_attn_Wq, L0_attn_Wk, L0_attn_Wv, L0_attn_Wm, L0_ffn_ln_g, L0_ffn_ln_b, L0_ffn_w_r,
            L0_ffn_b_r, L0_ffn_W1, L0_ffn_b1, L0_ffn_W2, L0_ffn_b2, **rest):
    import numpy as np

    cols, n = pack_layout(images)
    blocks, region_blocks, region, all_slots = sizes(images)
    pack = np.zeros((128, n), np.float32)

    def put(name, a, col=0):
        at = cols[name][0] + col
        pack[0:a.shape[0], at:at + a.shape[1]] = a

    put("conv", np.asarray(L0_tok_conv_w).reshape(D, PK, 128).transpose(2, 1, 0).reshape(128, PK * D))
    pos = np.asarray(L0_tok_pos_emb)[0].T
    put("pos", pos)
    put("pos", pos[:, T - 1:T], T)
    put("cls", np.asarray(L0_tok_cls_token).reshape(D, 1))
    put("conv_b", np.asarray(L0_tok_conv_b).reshape(D, 1))
    for l in range(2):
        r = {k: np.asarray(rest[f"L0_tok_{k}_{l}"]) for k in ("ln1", "qkv", "wo", "ln2", "gate", "up", "down")}
        put(f"ln1_{l}", r["ln1"].reshape(D, 1))
        put(f"ln2_{l}", r["ln2"].reshape(D, 1))
        put(f"qk_{l}", r["qkv"][0:2 * D].T)
        put(f"v_{l}", r["qkv"][2 * D:].T)
        put(f"wo_{l}", r["wo"].T)
        put(f"gate_{l}", r["gate"].T)
        put(f"up_{l}", r["up"].T)
        down = r["down"].T
        for f in range(FC):
            put(f"down_{l}", down[f * FP:(f + 1) * FP], f * D)
    put("ln_f", np.asarray(L0_tok_ln_f).reshape(D, 1))
    for h in range(HEADS):
        at = cols["qk_2"][0]
        pack[h * HD:(h + 1) * HD, at + h] = np.asarray(L0_attn_Wq)[h]
        pack[h * HD:(h + 1) * HD, at + HEADS + h] = np.asarray(L0_attn_Wk)[h]
        at = cols["v_2"][0]
        pack[h * HD:(h + 1) * HD, at + h * HD:at + (h + 1) * HD] = np.asarray(L0_attn_Wv)[h]
        pack[h * HD:(h + 1) * HD, cols["mask"][0] + h] = 1.0
    put("wo_2", np.asarray(L0_attn_Wm))
    put("ln_g", np.asarray(L0_ffn_ln_g).reshape(D, 1))
    put("ln_b", np.asarray(L0_ffn_ln_b).reshape(D, 1))
    put("wr", np.asarray(L0_ffn_w_r).T)
    put("br", np.broadcast_to(np.asarray(L0_ffn_b_r), (128, EXPERTS)))

    put("center", (np.eye(D) - 1.0 / D).astype(np.float32))
    put("ident", np.eye(D, dtype=np.float32))
    put("lower", np.triu(np.ones((HT, HT), np.float32), 1))
    put("iota", np.broadcast_to(np.arange(EXPERTS, dtype=np.float32), (128, EXPERTS)))
    put("first", np.broadcast_to(np.arange(EXPERTS, dtype=np.float32) * region, (128, EXPERTS)))
    t = np.arange(HT, dtype=np.float32)[:, None]
    put("token", np.concatenate([t + s * T + k * HT for s in range(SLOTS) for k in range(2)], 1))
    put("inv", np.full((128, 1), 1.0 / D, np.float32))
    put("fill", np.broadcast_to(np.arange(region_blocks, dtype=np.float32) * BLK, (128, region_blocks)))
    put("block", np.arange(blocks, dtype=np.float32)[None, :])

    sel = np.zeros((128, 2, 4 + HEADS, 128), np.float32)
    for h in range(HEADS):
        for d in range(HD):
            row = 64 * (h % 2) + d
            for group, (q_part, k_part) in enumerate(((0, 0), (0, 1), (1, 0), (1, 1))):
                sel[h * HD + d, q_part, h // 2, row + 16 * group] = 1.0
                sel[h * HD + d, k_part, 4 + h, row + 16 * group] = 1.0

    pixels = np.asarray(x)[0:images].reshape(images, 3, 14, 16, 14, 16).transpose(0, 1, 3, 5, 2, 4)
    pixels = pixels.reshape(images, PK, 128, T - 1).transpose(0, 2, 1, 3)
    img = np.zeros((images, 128, PK, TP), np.float32)
    img[:, :, :, 1:T] = pixels
    img[:, :, :, T] = pixels[:, :, :, T - 2]

    experts = np.zeros((EXPERTS, 128, EXPERT_COLS), np.float32)
    experts[:, :, 0:EH] = np.asarray(L0_ffn_W1)
    experts[:, :, EH:E1] = np.asarray(L0_ffn_b1).reshape(EXPERTS, EC, 128).transpose(0, 2, 1)
    w2 = np.asarray(L0_ffn_W2).reshape(EXPERTS, EC, 128, D).transpose(0, 2, 1, 3)
    experts[:, :, E1:E1 + EC * D] = w2.reshape(EXPERTS, 128, EC * D)
    experts[:, :, E1 + EC * D:] = np.asarray(L0_ffn_b2)[:, None, :]
    return {"img": img, "pack": pack, "sel": sel.reshape(128, 2 * SEL_COLS), "experts": experts}


def kernel(**inputs):
    import numpy as _np
    import concourse.bacc as _bacc
    from concourse import mybir as _mybir
    from concourse.bass_utils import run_bass_kernel_spmd as _run

    images = inputs["x"].shape[0]
    arrays = layouts(images, **inputs)
    nc = _bacc.Bacc("TRN2", target_bir_lowering=False, num_devices=1)
    args = [nc.dram_tensor(f"in_{name}", a.shape, _mybir.dt.float32, kind="ExternalInput").ap()
            for name, a in arrays.items()]
    out = nc.dram_tensor("out_rows", (images * T, D), _mybir.dt.float32, kind="ExternalOutput").ap()
    vit_moe_kernel(nc, *args, out)
    r = _run(nc, [{f"in_{name}": a for name, a in arrays.items()}], core_ids=[0])
    return r.results[0]["out_rows"].reshape(images, T, D)
```
